# Optimizing a Trainium2 kernel written in Bass

```python
import numpy as np
import jax
import jax.numpy as jnp

def _softmax(x, axis=-1):
    return jax.nn.softmax(x, axis=axis)

def _gelu(x):
    return jax.nn.gelu(x, approximate=True)

def _silu(x):
    return jax.nn.silu(x)

def _sigmoid(x):
    return jax.nn.sigmoid(x)

def _layernorm(x, axis=-1, eps=1e-05):
    m = jnp.mean(x, axis=axis, keepdims=True)
    v = jnp.var(x, axis=axis, keepdims=True)
    return (x - m) / jnp.sqrt(v + eps)

def _scatter_add(tgt, idx, src, axis=0):
    return tgt.at[idx].add(src)

def _segment_sum(src, seg, n):
    return jax.ops.segment_sum(src, seg, n)
kernel_name = 'mk_flamingo_gated_d2_seqx_r8_1dc51c'

def setup_inputs(seed: int=0):
    np.random.seed(seed)
    _w = jnp.asarray

    def _rec_inputs():
        import jax
        import jax.numpy as jnp
        _rk = jax.random.key(seed)
        x = -9.806e-05 + 1 * jax.random.normal(jax.random.fold_in(_rk, 1), (4, 256, 128), jnp.float32)
        _lenS = 256 - jax.random.randint(jax.random.fold_in(_rk, 7), (4,), 0, max(1, 256 // 4) + 1, jnp.int32)
        _lenS2 = 256 - jax.random.randint(jax.random.fold_in(_rk, 8), (4,), 0, max(1, 256 // 4) + 1, jnp.int32)
        _ctx_1024P = jax.random.normal(jax.random.fold_in(_rk, 11), (4, 16, 128), jnp.float32)
        _ctx_1024c = jax.random.dirichlet(jax.random.fold_in(_rk, 511), 0.3 * jnp.ones((16,), jnp.float32), (4, 256))
        _ctx_1024t = jnp.einsum('bsk,bkd->bsd', _ctx_1024c, _ctx_1024P)
        _ctx_1024t = _ctx_1024t * jax.lax.rsqrt(jnp.mean(jnp.square(_ctx_1024t)) + 1e-12) * 0.953939
        ctx_1024 = -1.52775e-05 + 0.999936 * (_ctx_1024t + 0.3 * jax.random.normal(jax.random.fold_in(_rk, 611), (4, 256, 128), jnp.float32))
        _g = jax.random.normal(jax.random.fold_in(_rk, 9001), (2, 2), jnp.float32)
        _g = jnp.sign(_g) * jnp.maximum(jnp.abs(_g), 1.0) + (_g == 0) * 1.0
        g_xattn = _g[0]
        g_ffn = _g[1]
        return (x, ctx_1024, g_xattn, g_ffn)
    x, ctx_1024, g_xattn, g_ffn = _rec_inputs()

    def _L0_xattn_setup():
        import jax, jax.numpy as jnp
        import numpy as np
        D = 128
        NUM_ITERS = 3
        EPS = 1e-06
        SCALE = D ** (-0.5)

        def rmsnorm(x, w, eps=EPS):
            return x * jax.lax.rsqrt(jnp.mean(x * x, axis=-1, keepdims=True) + eps) * w

        def gru_cell(x, h, wih, whh, bih, bhh):
            gx = x @ wih.T + bih
            gh = h @ whh.T + bhh
            xr, xz, xn = jnp.split(gx, 3, axis=-1)
            hr, hz, hn = jnp.split(gh, 3, axis=-1)
            r = jax.nn.sigmoid(xr + hr)
            z = jax.nn.sigmoid(xz + hz)
            n = jnp.tanh(xn + r * hn)
            return (1.0 - z) * n + z * h
        key = jax.random.key(seed)
        ks = jax.random.split(key, 8)
        B, K, M, d = (8, 64, 512, D)
        w_std = d ** (-0.5)
        return {'slots': jax.random.normal(ks[0], (B, K, d), jnp.float32), 'P': jax.random.normal(ks[1], (B, M, d), jnp.float32), 'Wq': jax.random.normal(ks[2], (d, d), jnp.float32) * w_std, 'Wk': jax.random.normal(ks[3], (d, d), jnp.float32) * w_std, 'Wv': jax.random.normal(ks[4], (d, d), jnp.float32) * w_std, 'gru_wih': jax.random.normal(ks[5], (3 * d, d), jnp.float32) * w_std, 'gru_whh': jax.random.normal(ks[6], (3 * d, d), jnp.float32) * w_std, 'gru_bih': jnp.zeros((3 * d,), jnp.float32), 'gru_bhh': jnp.zeros((3 * d,), jnp.float32), 'slot_norm_w': jnp.ones((d,), jnp.float32), 'input_norm_w': jnp.ones((d,), jnp.float32)}
    _L0_xattn_all = _L0_xattn_setup()
    _L0_xattn_in = {k: v for k, v in _L0_xattn_all.items() if k in ('Wq', 'Wk', 'Wv', 'gru_wih', 'gru_whh', 'gru_bih', 'gru_bhh', 'slot_norm_w', 'input_norm_w')}
    del _L0_xattn_all

    def _L0_ffn_setup():
        import jax, jax.numpy as jnp
        import numpy as np
        key = jax.random.key(seed)
        k1, k2, k3 = jax.random.split(key, 3)
        B, T, D, E = (4, 256, 128, 8)
        x = jax.random.normal(k1, (B, T, D), dtype=jnp.float32)
        gate_w = jax.random.normal(k2, (E, D), dtype=jnp.float32) * (1.0 / np.sqrt(D))
        bound = float(np.sqrt(6.0 / (D + D)))
        We = jax.random.uniform(k3, (E, D, D), dtype=jnp.float32, minval=-bound, maxval=bound)
        return {'x': x, 'gate_w': gate_w, 'We': We}
    _L0_ffn_all = _L0_ffn_setup()
    _L0_ffn_in = {k: v for k, v in _L0_ffn_all.items() if k in ('gate_w', 'We')}
    del _L0_ffn_all

    def _L1_xattn_setup():
        import jax, jax.numpy as jnp
        import numpy as np
        NUM_HEADS = 16
        B, S, D_MODEL = (8, 256, 128)
        HEAD_DIM = 64
        key = jax.random.key(seed)
        ks = jax.random.split(key, 8)
        s_in = 1.0 / np.sqrt(D_MODEL)
        s_out = 1.0 / np.sqrt(NUM_HEADS * HEAD_DIM)
        return {'query': jax.random.normal(ks[0], (B, S, D_MODEL), jnp.float32), 'key': jax.random.normal(ks[1], (B, S, D_MODEL), jnp.float32), 'value': jax.random.normal(ks[2], (B, S, D_MODEL), jnp.float32), 'Wq': jax.random.normal(ks[3], (D_MODEL, HEAD_DIM), jnp.float32) * s_in, 'bq': jnp.zeros((HEAD_DIM,), jnp.float32), 'Wk': jax.random.normal(ks[4], (D_MODEL, HEAD_DIM), jnp.float32) * s_in, 'bk': jnp.zeros((HEAD_DIM,), jnp.float32), 'Wv': jax.random.normal(ks[5], (D_MODEL, HEAD_DIM), jnp.float32) * s_in, 'bv': jnp.zeros((HEAD_DIM,), jnp.float32), 'Wo': jax.random.normal(ks[6], (NUM_HEADS * HEAD_DIM, D_MODEL), jnp.float32) * s_out, 'bo': jnp.zeros((D_MODEL,), jnp.float32)}
    _L1_xattn_all = _L1_xattn_setup()
    _L1_xattn_in = {k: v for k, v in _L1_xattn_all.items() if k in ('Wq', 'bq', 'Wk', 'bk', 'Wv', 'bv', 'Wo', 'bo')}
    del _L1_xattn_all

    def _L1_ffn_setup():
        import jax, jax.numpy as jnp
        import numpy as np
        from jax import lax
        D = 128
        H = 512
        E = 8
        TOPK = 2
        key = jax.random.key(seed)
        ks = jax.random.split(key, 7)
        s = 0.02
        return {'x': jax.random.normal(ks[0], (2, 256, D), dtype=jnp.float32), 'W1': jax.random.normal(ks[1], (E, D, H), dtype=jnp.float32) * s, 'b1': jnp.zeros((E, H), dtype=jnp.float32), 'W2': jax.random.normal(ks[2], (E, H, D), dtype=jnp.float32) * s, 'b2': jnp.zeros((E, D), dtype=jnp.float32), 'Wr': jax.random.normal(ks[3], (D, E), dtype=jnp.float32) * s, 'br': jnp.zeros((E,), dtype=jnp.float32)}
    _L1_ffn_all = _L1_ffn_setup()
    _L1_ffn_in = {k: v for k, v in _L1_ffn_all.items() if k in ('W1', 'b1', 'W2', 'b2', 'Wr', 'br')}
    del _L1_ffn_all
    return {'x': x, 'ctx_1024': ctx_1024, 'g_xattn': g_xattn, 'g_ffn': g_ffn, 'L0_xattn_Wq': _L0_xattn_in['Wq'], 'L0_xattn_Wk': _L0_xattn_in['Wk'], 'L0_xattn_Wv': _L0_xattn_in['Wv'], 'L0_xattn_gru_wih': _L0_xattn_in['gru_wih'], 'L0_xattn_gru_whh': _L0_xattn_in['gru_whh'], 'L0_xattn_gru_bih': _L0_xattn_in['gru_bih'], 'L0_xattn_gru_bhh': _L0_xattn_in['gru_bhh'], 'L0_xattn_slot_norm_w': _L0_xattn_in['slot_norm_w'], 'L0_xattn_input_norm_w': _L0_xattn_in['input_norm_w'], 'L0_ffn_gate_w': _L0_ffn_in['gate_w'], 'L0_ffn_We': _L0_ffn_in['We'], 'L1_xattn_Wq': _L1_xattn_in['Wq'], 'L1_xattn_bq': _L1_xattn_in['bq'], 'L1_xattn_Wk': _L1_xattn_in['Wk'], 'L1_xattn_bk': _L1_xattn_in['bk'], 'L1_xattn_Wv': _L1_xattn_in['Wv'], 'L1_xattn_bv': _L1_xattn_in['bv'], 'L1_xattn_Wo': _L1_xattn_in['Wo'], 'L1_xattn_bo': _L1_xattn_in['bo'], 'L1_ffn_W1': _L1_ffn_in['W1'], 'L1_ffn_b1': _L1_ffn_in['b1'], 'L1_ffn_W2': _L1_ffn_in['W2'], 'L1_ffn_b2': _L1_ffn_in['b2'], 'L1_ffn_Wr': _L1_ffn_in['Wr'], 'L1_ffn_br': _L1_ffn_in['br']}

def reference(x, ctx_1024, g_xattn, g_ffn, L0_xattn_Wq, L0_xattn_Wk, L0_xattn_Wv, L0_xattn_gru_wih, L0_xattn_gru_whh, L0_xattn_gru_bih, L0_xattn_gru_bhh, L0_xattn_slot_norm_w, L0_xattn_input_norm_w, L0_ffn_gate_w, L0_ffn_We, L1_xattn_Wq, L1_xattn_bq, L1_xattn_Wk, L1_xattn_bk, L1_xattn_Wv, L1_xattn_bv, L1_xattn_Wo, L1_xattn_bo, L1_ffn_W1, L1_ffn_b1, L1_ffn_W2, L1_ffn_b2, L1_ffn_Wr, L1_ffn_br):
    import jax
    import jax.numpy as jnp

    def _L0_xattn_ref(slots, P, Wq, Wk, Wv, gru_wih, gru_whh, gru_bih, gru_bhh, slot_norm_w, input_norm_w):
        import jax, jax.numpy as jnp
        import numpy as np
        D = 128
        NUM_ITERS = 3
        EPS = 1e-06
        SCALE = D ** (-0.5)

        def rmsnorm(x, w, eps=EPS):
            return x * jax.lax.rsqrt(jnp.mean(x * x, axis=-1, keepdims=True) + eps) * w

        def gru_cell(x, h, wih, whh, bih, bhh):
            gx = x @ wih.T + bih
            gh = h @ whh.T + bhh
            xr, xz, xn = jnp.split(gx, 3, axis=-1)
            hr, hz, hn = jnp.split(gh, 3, axis=-1)
            r = jax.nn.sigmoid(xr + hr)
            z = jax.nn.sigmoid(xz + hz)
            n = jnp.tanh(xn + r * hn)
            return (1.0 - z) * n + z * h
        Pn = rmsnorm(P, input_norm_w)
        k_proj = Pn @ Wk.T
        v_proj = Pn @ Wv.T
        for _ in range(NUM_ITERS):
            sn = rmsnorm(slots, slot_norm_w)
            q_proj = sn @ Wq.T
            scores = jnp.einsum('bkd,bmd->bkm', q_proj, k_proj) * SCALE
            attn = jax.nn.softmax(scores, axis=-2)
            attn = attn / (jnp.sum(attn, axis=-1, keepdims=True) + EPS)
            updates = jnp.einsum('bkm,bmd->bkd', attn, v_proj)
            slots = gru_cell(updates, slots, gru_wih, gru_whh, gru_bih, gru_bhh)
        return slots

    def _L0_ffn_ref(x, gate_w, We):
        import jax, jax.numpy as jnp
        import numpy as np
        top_k = 2
        logits = jnp.einsum('btd,ed->bte', x, gate_w)
        top_val, top_idx = jax.lax.top_k(logits, top_k)
        top_w = jax.nn.softmax(top_val, axis=-1)
        y_all = jnp.einsum('btd,edm->btem', x, We)
        x_experts = jnp.take_along_axis(y_all, top_idx[..., None], axis=2)
        out = jnp.sum(x_experts * top_w[..., None], axis=2)
        return out

    def _L1_xattn_ref(query, key, value, Wq, bq, Wk, bk, Wv, bv, Wo, bo):
        import jax, jax.numpy as jnp
        import numpy as np
        NUM_HEADS = 16
        B, S, D_MODEL = (8, 256, 128)
        HEAD_DIM = 64
        q = query @ Wq + bq
        k = key @ Wk + bk
        v = value @ Wv + bv
        scale = jnp.sqrt(jnp.asarray(q.shape[-1], q.dtype))
        scores = jnp.einsum('bqd,bkd->bqk', q, k) / scale
        attn = jax.nn.softmax(scores, axis=-1)
        ctx = jnp.einsum('bqk,bkd->bqd', attn, v)
        cat = jnp.tile(ctx, (1, 1, NUM_HEADS))
        return cat @ Wo + bo

    def _L1_ffn_ref(x, W1, b1, W2, b2, Wr, br):
        import jax, jax.numpy as jnp
        import numpy as np
        from jax import lax
        D = 128
        H = 512
        E = 8
        TOPK = 2
        B, S, _ = x.shape
        xf = x.reshape(-1, D)
        logits = xf @ Wr + br
        topv, _ = lax.top_k(logits, TOPK)
        thresh = topv[:, TOPK - 1:TOPK]
        masked = jnp.where(logits >= thresh, logits, -jnp.inf)
        weights = jax.nn.softmax(masked, axis=-1)
        h = jax.nn.gelu(jnp.einsum('td,edh->eth', xf, W1) + b1[:, None, :], approximate=False)
        expert_out = jnp.einsum('eth,ehd->etd', h, W2) + b2[:, None, :]
        out = jnp.einsum('etd,te->td', expert_out, weights)
        return out.reshape(B, S, D)
    x = x + jnp.tanh(g_xattn[0]) * _L0_xattn_ref(_layernorm(x, axis=-1), ctx_1024, L0_xattn_Wq, L0_xattn_Wk, L0_xattn_Wv, L0_xattn_gru_wih, L0_xattn_gru_whh, L0_xattn_gru_bih, L0_xattn_gru_bhh, L0_xattn_slot_norm_w, L0_xattn_input_norm_w)
    x = x + jnp.tanh(g_ffn[0]) * _L0_ffn_ref(_layernorm(x, axis=-1), L0_ffn_gate_w, L0_ffn_We)
    x = x + jnp.tanh(g_xattn[1]) * _L1_xattn_ref(_layernorm(x, axis=-1), ctx_1024, ctx_1024, L1_xattn_Wq, L1_xattn_bq, L1_xattn_Wk, L1_xattn_bk, L1_xattn_Wv, L1_xattn_bv, L1_xattn_Wo, L1_xattn_bo)
    x = x + jnp.tanh(g_ffn[1]) * _L1_ffn_ref(_layernorm(x, axis=-1), L1_ffn_W1, L1_ffn_b1, L1_ffn_W2, L1_ffn_b2, L1_ffn_Wr, L1_ffn_br)
    return x

_drawn_inputs = setup_inputs


def setup_inputs(seed=0):
    import zlib

    import numpy as np

    out = dict(_drawn_inputs(seed))
    spreads = {'g_ffn': (-1.0, 0.6),
     'L0_xattn_gru_bih': (0.0, 0.1),
     'L0_xattn_gru_bhh': (0.0, 0.1),
     'L0_xattn_slot_norm_w': (1.0, 0.2),
     'L0_xattn_input_norm_w': (1.0, 0.2),
     'L1_xattn_bq': (0.0, 0.619),
     'L1_xattn_bk': (0.0, 0.8),
     'L1_xattn_bv': (0.0, 0.1),
     'L1_xattn_bo': (0.0, 0.1),
     'L1_ffn_b1': (0.0, 0.783),
     'L1_ffn_b2': (0.0, 0.1),
     'L1_ffn_br': (0.0, 0.279)}
    factors = {}
    for name, (base, spread) in spreads.items():
        noise = np.random.default_rng([zlib.crc32(name.encode()), seed]).standard_normal(out[name].shape)
        drawn = base * np.exp(spread * noise) if base else spread * noise
        out[name] = jnp.asarray(drawn.astype(out[name].dtype))
    for name, factor in factors.items():
        out[name] = (out[name] * factor).astype(out[name].dtype)
    return out
```

```python
import concourse.bass as bass
from concourse import mybir
from contextlib import ExitStack


def flamingo_gated_two_layer_kernel(
    nc: bass.Bass,
    x_in: bass.AP, ctx_in: bass.AP, g_xattn: bass.AP, g_ffn: bass.AP,
    a0_Wq: bass.AP, a0_Wk: bass.AP, a0_Wv: bass.AP,
    gru_wih: bass.AP, gru_whh: bass.AP, gru_bih: bass.AP, gru_bhh: bass.AP,
    slot_norm_w: bass.AP, input_norm_w: bass.AP,
    f0_gate_w: bass.AP, f0_We: bass.AP,
    a1_Wq: bass.AP, a1_bq: bass.AP, a1_Wk: bass.AP, a1_bk: bass.AP,
    a1_Wv: bass.AP, a1_bv: bass.AP, a1_Wo: bass.AP, a1_bo: bass.AP,
    f1_W1: bass.AP, f1_b1: bass.AP, f1_W2: bass.AP, f1_b2: bass.AP,
    f1_Wr: bass.AP, f1_br: bass.AP,
    out: bass.AP,
):
    f32 = mybir.dt.float32
    f32r = mybir.dt.float32r
    u32 = mybir.dt.uint32
    ALU = mybir.AluOpType
    ACT = mybir.ActivationFunctionType
    AX_X = mybir.AxisListType.X

    B, S, D = x_in.shape
    T = B * S
    P = 128
    NT = T // P
    HT = NT // 2
    HW = HT * P
    BH = B // 2
    MT = S // P
    G3 = 3
    NE = f0_We.shape[0]
    DH = a1_Wq.shape[1]
    NHEAD = a1_Wo.shape[0] // DH
    HID = f1_W1.shape[2]
    NC = HID // P
    ITERS = 3
    SCALE = float(D) ** -0.5
    QSCALE = float(DH) ** -0.5
    RMS_EPS, LN_EPS = 1e-6, 1e-5

    R_BIH, R_BHH, R_SW, R_IW, R_BO, R_BQ, R_BK, R_BV = 0, 3, 6, 7, 8, 9, 10, 11
    R_B1 = 12
    R_B2 = R_B1 + NE * NC
    R_GW = R_B2 + NE
    NROW = R_GW + NE

    x_v = x_in.rearrange("b (t p) d -> p (b t) d", p=P)
    ctx_v = ctx_in.rearrange("b (t p) d -> p (b t) d", p=P)
    out_v = out.rearrange("b (t p) d -> p (b t) d", p=P)
    W1_v = f1_W1.rearrange("e d h -> d e h")
    W2_v = f1_W2.rearrange("e (c p) d -> p e c d", p=P)

    ctx = ExitStack()
    with ctx:
        def sb(name, shape, dt=f32):
            return ctx.enter_context(nc.sbuf_tensor(name, shape, dt))

        def sem(name):
            return ctx.enter_context(nc.semaphore(name))

        ident = sb("ident", [P, P])
        neg_half = sb("neg_half", [P, NT])
        ones = sb("ones", [P, 1])
        iota8 = sb("iota8", [P, NE])
        rows = sb("rows", [NROW, P])
        vec = sb("vec", [P, NROW])
        g_raw = sb("g_raw", [P, 4])
        tg = sb("tg", [P, 4])
        br_bc = sb("br_bc", [P, NE])
        b_gate = sb("b_gate", [P, 2])
        b_sum = sb("b_sum", [P, 2])
        bq_s = sb("bq_s", [DH, 1])
        out_bias = sb("out_bias", [P, 1])

        x_tok = sb("x_tok", [P, NT, D])
        c_tok = sb("c_tok", [P, NT, D])
        pn_tok = sb("pn_tok", [P, NT, D])
        x_res = sb("x_res", [P, T])
        ctxT = sb("ctxT", [P, T])
        pnT = sb("pnT", [P, T])
        kqT = sb("kqT", [P, T])
        wq0 = sb("wq0", [P, D])
        wk0 = sb("wk0", [P, D])
        wv0 = sb("wv0", [P, D])
        wih = sb("wih", [P, G3, D])
        whh = sb("whh", [P, G3, D])
        mq = sb("mq", [P, D])
        wihT = sb("wihT", [P, G3 * D])
        whhT = sb("whhT", [P, G3 * D])
        gxw = sb("gxw", [P, G3 * D])
        wq1 = sb("wq1", [P, DH])
        wk1 = sb("wk1", [P, DH])
        wv1 = sb("wv1", [P, DH])
        wv1T = sb("wv1T", [DH, D])
        wo1 = sb("wo1", [DH, NHEAD, D])
        wvo = sb("wvo", [P, D])
        kT1 = sb("kT1", [DH, T])
        vo1 = sb("vo1", [P, NT, D])
        we0 = sb("we0", [P, NE, D])
        wr1 = sb("wr1", [P, NE])

        st = sb("st", [P, 4, NT, 6])
        mv = sb("mv", [P, 4, NT, 2])
        ve = sb("ve", [P, 4, NT])
        rs = sb("rs", [P, 4, NT])
        css = sb("css", [P, NT])
        cse = sb("cse", [P, NT])
        crs = sb("crs", [P, NT])

        slots = sb("slots", [P, T])
        sq = sb("sq", [P, T])
        sn = sb("sn", [P, T])
        mse = sb("mse", [P, NT])
        rst = sb("rst", [P, NT])
        neg_max = sb("neg_max", [P, NT])
        row_sum = sb("row_sum", [P, NT])
        row_inv = sb("row_inv", [P, NT])
        E = sb("E", [P, NT, S])
        pv = sb("pv", [P, NT, D + 1])
        su = sb("su", [P, NT])
        siv = sb("siv", [P, NT])
        upd_tok = sb("upd_tok", [P, NT, D])
        updT = sb("updT", [P, T])
        tr = sb("tr", [P, T])
        tz = sb("tz", [P, T])
        rg = sb("rg", [P, T])
        t1 = sb("t1", [P, T])
        t2 = sb("t2", [P, T])
        nn = sb("nn", [P, T])
        dd = sb("dd", [P, T])

        xn_tok = sb("xn_tok", [P, NT, D])
        xnT = sb("xnT", [P, T])
        lg = sb("lg", [P, NT, NE])
        m8 = sb("m8", [P, NT, 8])
        ix = sb("ix", [P, NT, 8], u32)
        ixf = sb("ixf", [P, NT, 8])
        dl = sb("dl", [P, NT])
        ed = sb("ed", [P, NT])
        den = sb("den", [P, NT])
        wa = sb("wa", [P, NT])
        wag = sb("wag", [P, NT])
        wbg = sb("wbg", [P, NT])
        q1 = sb("q1", [P, NT, NE])
        q2 = sb("q2", [P, NT, NE])
        gw0 = sb("gw0", [P, NT, NE])
        gw1 = sb("gw1", [P, NT, NE])
        xe = sb("xe", [P, 2, 2, HW])
        qT1 = sb("qT1", [DH, T])
        pT1 = sb("pT1", [P, 2, MT, HW])

        xh = sb("xh", [P, T], f32r)
        xl = sb("xl", [P, T], f32r)
        w1r = [sb(f"w1r{s}", [P, HID]) for s in range(2)]
        w2r = [sb(f"w2r{s}", [P, NC, D]) for s in range(2)]
        w1h = [sb(f"w1h{s}", [P, HID], f32r) for s in range(2)]
        w1l = [sb(f"w1l{s}", [P, HID], f32r) for s in range(2)]
        w2h = [sb(f"w2h{s}", [P, NC, D], f32r) for s in range(2)]
        w2l = [sb(f"w2l{s}", [P, NC, D], f32r) for s in range(2)]
        b1s = [sb(f"b1s{s}", [P, NC]) for s in range(2)]
        b2s = [sb(f"b2s{s}", [P, 1]) for s in range(2)]
        gws = [sb(f"gws{s}", [P, NT, 1]) for s in range(2)]
        wbc = [tr, tz]
        hh = [sb(f"hh{s}", [P, T], f32r) for s in range(2)]
        hl = [sb(f"hl{s}", [P, T], f32r) for s in range(2)]
        ygated = t2
        o_tok = upd_tok

        SC = ctx.enter_context(nc.psum_tensor("SC", [P, 2, 2, 512], f32))
        GB = ctx.enter_context(nc.psum_tensor("GB", [P, 4, 512], f32))
        R_, Z_, XN_, HN_ = range(4)

        ld_x, ld_c, ld_rows, ld_gate = sem("ld_x"), sem("ld_c"), sem("ld_rows"), sem("ld_gate")
        ld_qkv0, ld_gru, ld_a1, ld_f0 = sem("ld_qkv0"), sem("ld_gru"), sem("ld_a1"), sem("ld_f0")
        ld_ffn = [sem("ld_ffn0"), sem("ld_ffn1")]
        rows_clear, id_clear, id_ready, consts = sem("rows_clear"), sem("id_clear"), sem("id_ready"), sem("consts")
        stored = sem("stored")
        vecT, vec_ready, tg_ready, bias_ready = sem("vecT"), sem("vec_ready"), sem("tg_ready"), sem("bias_ready")
        xT_ps, xres_ready = sem("xT_ps"), sem("xres_ready")
        mq_ps, mq_ready, wT_ps, wT_ready, gxw_ps, gxw_ready = (sem(n) for n in (
            "mq_ps", "mq_ready", "wT_ps", "wT_ready", "gxw_ps", "gxw_ready"))
        css_ready, cse_ready, crs_ready, pn_ready = sem("css_ready"), sem("cse_ready"), sem("crs_ready"), sem("pn_ready")
        pnT_ps, pnT_ready, kq_ps, kq_ready = sem("pnT_ps"), sem("pnT_ready"), sem("kq_ps"), sem("kq_ready")
        wos_step, gws_ready = sem("wos_step"), sem("gws_ready")
        wv1T_ps, wv1T_ready, wvo_ps, wvo_ready = sem("wv1T_ps"), sem("wv1T_ready"), sem("wvo_ps"), sem("wvo_ready")
        ctxT_ps, ctxT_ready, kT1_ps, kT1_ready = sem("ctxT_ps"), sem("ctxT_ready"), sem("kT1_ps"), sem("kT1_ready")
        vo1_ps, vo1_ready, ob_ps, ob_ready = sem("vo1_ps"), sem("vo1_ready"), sem("ob_ps"), sem("ob_ready")
        ln_tok = [sem(f"ln_tok{k}") for k in range(4)]
        ln_var = [sem(f"ln_var{k}") for k in range(4)]
        ln_rstd = [sem(f"ln_rstd{k}") for k in range(4)]
        ln_norm = [sem(f"ln_norm{k}") for k in range(4)]
        ln_back = [sem(f"ln_back{k}") for k in range(4)]
        ln_out = [sem(f"ln_out{k}") for k in range(4)]
        slots_ready, sq_ready, ms_ps, mse_ready, rst_ready, rb_ps, sn_ready = (sem(n) for n in (
            "slots_ready", "sq_ready", "ms_ps", "mse_ready", "rst_ready", "rb_ps", "sn_ready"))
        score_ps, max_ready, exp_ready, pv_ready, upd_ps, upd_tok_ready, updT_ps, updT_ready = (sem(n) for n in (
            "score_ps", "max_ready", "exp_ready", "pv_ready", "upd_ps", "upd_tok_ready", "updT_ps", "updT_ready"))
        gr_ps, gn_ps, gz_ps, tr_ready, tz_ready, cand_in, cand_ready = (sem(n) for n in (
            "gr_ps", "gn_ps", "gz_ps", "tr_ready", "tz_ready", "cand_in", "cand_ready"))
        dve_step, dve_loop, res_ready = sem("dve_step"), sem("dve_loop"), sem("res_ready")
        lg0_ps, dl_ready, ed_ready, gw0_ready, wb0_ps, xe_ready, y0_step, y0_ps = (sem(n) for n in (
            "lg0_ps", "dl_ready", "ed_ready", "gw0_ready", "wb0_ps", "xe_ready", "y0_step", "y0_ps"))
        q1_ps, q1_ready, s1_ps, max1_ready, exp1_ready, p1_ready, pT1_ps, pT1_ready, o1_ps = (sem(n) for n in (
            "q1_ps", "q1_ready", "s1_ps", "max1_ready", "exp1_ready", "p1_ready", "pT1_ps", "pT1_ready", "o1_ps"))
        xhl_ready, lg1_ps, sh_ready, ex_ready, gw1_ready = (sem(n) for n in (
            "xhl_ready", "lg1_ps", "sh_ready", "ex_ready", "gw1_ready"))
        w_high, w_ready, w1_ps, hh_ready, gelu_ready, hl_ready, h_used, wb1_ps, wb1_ready, y1_gated, y1_added = (sem(n) for n in (
            "w_high", "w_ready", "w1_ps", "hh_ready", "gelu_ready", "hl_ready", "h_used", "wb1_ps", "wb1_ready", "y1_gated", "y1_added"))
        oT_ps, o_ready = sem("oT_ps"), sem("o_ready")

        block = ctx.enter_context(nc.Block())

        def cols(h):
            return slice(h * HW, (h + 1) * HW)

        def tiles(h):
            return slice(h * HT, (h + 1) * HT)

        def qb(h, n):
            return SC[:, h, n, :] if n < 2 else GB[:, 2 * h + n - 2, :]

        def tiled(ap, n=HT):
            return ap.rearrange("p (t d) -> p t d", t=n)

        row_loads = [
            (R_BIH, G3, gru_bih.rearrange("(g d) -> g d", d=P), P),
            (R_BHH, G3, gru_bhh.rearrange("(g d) -> g d", d=P), P),
            (R_SW, 1, slot_norm_w.rearrange("(a d) -> a d", a=1), P),
            (R_IW, 1, input_norm_w.rearrange("(a d) -> a d", a=1), P),
            (R_BO, 1, a1_bo.rearrange("(a d) -> a d", a=1), P),
            (R_BQ, 1, a1_bq.rearrange("(a d) -> a d", a=1), DH),
            (R_BK, 1, a1_bk.rearrange("(a d) -> a d", a=1), DH),
            (R_BV, 1, a1_bv.rearrange("(a d) -> a d", a=1), DH),
            (R_B1, NE * NC, f1_b1.rearrange("e (c d) -> (e c) d", d=P), P),
            (R_B2, NE, f1_b2, P),
            (R_GW, NE, f0_gate_w, P),
        ]

        @block.sync
        def _(sp):
            for h in range(2):
                sp.dma_start(x_tok[:, tiles(h), :], x_v[:, tiles(h), :]).then_inc(ld_x, 16)
            sp.wait_ge(rows_clear, 1)
            for r, n, src, w in row_loads:
                sp.dma_start(rows[r:r + n, 0:w], src).then_inc(ld_rows, 16)
            sp.dma_start(wo1[:, :, :], a1_Wo.rearrange("(n p) d -> p n d", p=DH)).then_inc(ld_a1, 16)
            sp.dma_start(we0[:, :, :], f0_We.rearrange("e d m -> d e m")).then_inc(ld_f0, 16)
            sp.dma_start(wr1[:, :], f1_Wr).then_inc(ld_f0, 16)
            for s in range(2):
                sp.dma_start(w1r[s][:, :], W1_v[:, s, :]).then_inc(ld_ffn[s], 16)
                sp.dma_start(w2r[s][:, :, :], W2_v[:, s, :, :]).then_inc(ld_ffn[s], 16)
            with sp.Fori(1, NE // 2) as i:
                for s in range(2):
                    sp.wait_ge(w_ready, 4 * i + 2 * s - 2)
                    sp.dma_start(w1r[s][:, :], W1_v[:, bass.ds(2 * i + s, 1), :]).then_inc(ld_ffn[s], 16)
                    sp.dma_start(w2r[s][:, :, :], W2_v[:, bass.ds(2 * i + s, 1), :, :]).then_inc(ld_ffn[s], 16)
            for h in range(2):
                sp.wait_ge(o_ready, h + 1)
                sp.dma_start(out_v[:, tiles(h), :], o_tok[:, tiles(h), :]).then_inc(stored, 16)
            sp.wait_ge(stored, 32)

        @block.gpsimd
        def _(pool):
            pool.memset(rows[:, :], 0.0).then_inc(rows_clear, 1)
            pool.memset(ident[:, :], 0.0).then_inc(id_clear, 1)
            pool.memset(ones[:, :], 1.0)
            pool.memset(neg_half[:, :], -0.5).then_inc(consts, 1)
            pool.wait_ge(id_clear, 1)
            pool.affine_select(out=ident[:, :], in_=ident[:, :], compare_op=ALU.not_equal, fill=1.0,
                               base=0, pattern=[[-1, P]], channel_multiplier=1).then_inc(id_ready, 1)
            pool.iota(iota8[:, :], pattern=[[1, NE]], base=0, channel_multiplier=0,
                      allow_small_or_imprecise_dtypes=True).then_inc(consts, 1)
            pool.wait_ge(consts, 2)
            for h in range(2):
                pool.wait_ge(ln_var[0], h + 1)
                pool.tensor_tensor(rs[:, 0, tiles(h)], ve[:, 0, tiles(h)], neg_half[:, 0:HT],
                                   ALU.pow).then_inc(ln_rstd[0], 1)
            pool.wait_ge(cse_ready, 1)
            pool.tensor_tensor(crs[:, :], cse[:, :], neg_half[:, :], ALU.pow).then_inc(crs_ready, 1)

            def slot_rstd(n, h):
                pool.wait_ge(mse_ready, n)
                pool.tensor_tensor(rst[:, tiles(h)], mse[:, tiles(h)], neg_half[:, 0:HT],
                                   ALU.pow).then_inc(rst_ready, 1)

            slot_rstd(1, 0)
            pool.wait_ge(ld_a1, 64)
            n, k = NHEAD, 0
            while n > 1:
                n //= 2
                k += 1
                pool.tensor_tensor(wo1[:, 0:n, :], wo1[:, 0:n, :], wo1[:, n:2 * n, :], ALU.add).then_inc(wos_step, 1)
                pool.wait_ge(wos_step, k)
            def slot_trip(it):
                slot_rstd(2 * it + 2, 1)
                slot_rstd(2 * it + 3, 0)

            slot_trip(0)
            with pool.Fori(1, ITERS) as it:
                slot_trip(it)

            def split_weights(i, s, first):
                pool.wait_ge(ld_ffn[s], 32 * i + 32)
                if not first:
                    pool.wait_ge(h_used, NC * (2 * i + s - 1))
                    pool.wait_ge(y1_gated, 2 * i + s - 1)
                pool.tensor_tensor(w1h[s][:, :], w1r[s][:, :], ones[:, :].to_broadcast([P, HID]), ALU.mult).then_inc(w_high, 1)
                pool.tensor_copy(w2h[s][:, :, :], w2r[s][:, :, :]).then_inc(w_high, 1)
                pool.tensor_copy(b1s[s][:, :], vec[:, bass.ds(R_B1 + NC * (2 * i + s), NC)]).then_inc(w_high, 1)
                pool.tensor_copy(b2s[s][:, :], vec[:, bass.ds(R_B2 + 2 * i + s, 1)]).then_inc(w_high, 1)
                pool.wait_ge(w_high, 4 * (2 * i + s) + 4)
                pool.tensor_tensor(w1l[s][:, :], w1r[s][:, :], w1h[s][:, :].bitcast(f32), ALU.subtract).then_inc(w_ready, 1)
                pool.tensor_tensor(w2l[s][:, :, :], w2r[s][:, :, :], w2h[s][:, :, :].bitcast(f32), ALU.subtract).then_inc(w_ready, 1)

            def stage_gates(i, s):
                pool.tensor_copy(gws[s][:, :, :], gw1[:, :, bass.ds(2 * i + s, 1)]).then_inc(gws_ready, 1)

            split_weights(0, 0, True)
            split_weights(0, 1, True)
            for k in range(1, 4):
                for h in range(2):
                    pool.wait_ge(ln_var[k], h + 1)
                    pool.tensor_tensor(rs[:, k, tiles(h)], ve[:, k, tiles(h)], neg_half[:, 0:HT],
                                       ALU.pow).then_inc(ln_rstd[k], 1)
            pool.wait_ge(gw1_ready, 2)
            stage_gates(0, 0)
            stage_gates(0, 1)
            with pool.Fori(1, NE // 2) as i:
                for s in range(2):
                    split_weights(i, s, False)
                    stage_gates(i, s)

        @block.scalar
        def _(act):
            for h in range(2):
                act.dma_start(c_tok[:, tiles(h), :], ctx_v[:, tiles(h), :]).then_inc(ld_c, 16)
            for dst, src in ((wk0, a0_Wk), (wq0, a0_Wq), (wv0, a0_Wv)):
                act.dma_start(dst[:, :], src).then_inc(ld_qkv0, 16)
            for dst, src in ((wih, gru_wih), (whh, gru_whh)):
                act.dma_start(dst[:, :, :], src.rearrange("(g p) d -> p g d", p=P)).then_inc(ld_gru, 16)
            act.dma_start(g_raw[:, 0:2], g_xattn.partition_broadcast(P)).then_inc(ld_gate, 16)
            act.dma_start(g_raw[:, 2:4], g_ffn.partition_broadcast(P)).then_inc(ld_gate, 16)
            act.dma_start(br_bc[:, :], f1_br.partition_broadcast(P)).then_inc(ld_gate, 16)
            for dst, src in ((wq1, a1_Wq), (wk1, a1_Wk), (wv1, a1_Wv)):
                act.dma_start(dst[:, :], src).then_inc(ld_a1, 16)

            act.wait_ge(ld_c, 32)
            for t in range(NT):
                last = act.activation(updT[:, t * P:(t + 1) * P], c_tok[:, t, :], ACT.Square,
                                      accum_out=css[:, t:t + 1])
            last.then_inc(css_ready, 1)
            for h in range(2):
                act.wait_ge(xT_ps, h + 1)
                act.activation(x_res[:, cols(h)], SC[:, h, 1, :], ACT.Copy).then_inc(xres_ready, 1)
            for n, (bank, dst) in enumerate(((Z_ + 1, wihT), (Z_ + 2, whhT))):
                act.wait_ge(wT_ps, n + 1)
                act.activation(dst[:, :], GB[:, bank, 0:G3 * D], ACT.Copy).then_inc(wT_ready, 1)
            act.wait_ge(crs_ready, 1)
            for t in range(NT):
                last = act.activation(pn_tok[:, t, :], c_tok[:, t, :], ACT.Copy, scale=crs[:, t:t + 1])
            last.then_inc(pn_ready, 1)
            for h in range(2):
                act.wait_ge(ln_back[0], h + 1)
                act.activation(slots[:, cols(h)], SC[:, h, 0, :], ACT.Copy).then_inc(slots_ready, 1)
            act.wait_ge(slots_ready, 1)
            act.activation(sq[:, cols(0)], slots[:, cols(0)], ACT.Square).then_inc(sq_ready, 1)
            for h in range(2):
                act.wait_ge(pnT_ps, h + 1)
                act.activation(pnT[:, cols(h)], SC[:, h, 1, :], ACT.Copy).then_inc(pnT_ready, 1)
            act.wait_ge(vec_ready, 1)
            for h in range(2):
                act.wait_ge(kq_ps, h + 1)
                act.activation(kqT[:, cols(h)], GB[:, 1 + h, :], ACT.Copy,
                               scale=vec[:, R_SW:R_SW + 1]).then_inc(kq_ready, 1)
            act.wait_ge(ld_gate, 48)
            act.activation(tg[:, :], g_raw[:, :], ACT.Tanh).then_inc(tg_ready, 1)
            for h in range(2):
                act.wait_ge(ctxT_ps, h + 1)
                act.activation(ctxT[:, cols(h)], GB[:, 3 * h, :], ACT.Copy).then_inc(ctxT_ready, 1)
            act.wait_ge(wv1T_ps, 1)
            act.activation(wv1T[:, :], GB[0:DH, 1, 0:D], ACT.Copy).then_inc(wv1T_ready, 1)
            act.wait_ge(wvo_ps, 1)
            act.activation(wvo[:, :], GB[:, 2, 0:D], ACT.Copy).then_inc(wvo_ready, 1)
            for h in range(2):
                act.wait_ge(kT1_ps, h + 1)
                act.activation(kT1[:, cols(h)], GB[0:DH, 1 + h, :], ACT.Identity,
                               bias=vec[0:DH, R_BK:R_BK + 1]).then_inc(kT1_ready, 1)
            act.wait_ge(tg_ready, 1)
            for h in range(2):
                act.wait_ge(vo1_ps, h + 1)
                act.activation(vo1[:, tiles(h), :], tiled(GB[:, 3 * h, :]), ACT.Copy,
                               scale=tg[:, 1:2]).then_inc(vo1_ready, 1)

            def square_slots(n, h):
                act.wait_ge(slots_ready, n)
                act.activation(sq[:, cols(h)], slots[:, cols(h)], ACT.Square).then_inc(sq_ready, 1)

            def slot_exp(n, h):
                act.wait_ge(max_ready, n)
                for j in range(HT):
                    t = h * HT + j
                    last = act.activation(E[:, t, :], SC[:, h, j // MT, (j % MT) * S:(j % MT + 1) * S],
                                          ACT.Exp, bias=neg_max[:, t:t + 1], accum_out=row_sum[:, t:t + 1])
                last.then_inc(exp_ready, 1)

            def copy_updates(n, h):
                act.wait_ge(updT_ps, n)
                act.activation(updT[:, cols(h)], GB[:, XN_, :], ACT.Copy).then_inc(updT_ready, 1)

            def gates(n, h):
                act.wait_ge(gr_ps, n)
                act.activation(tr[:, cols(h)], GB[:, R_, :], ACT.Tanh, scale=0.5,
                               bias=b_gate[:, 0:1]).then_inc(tr_ready, 1)
                act.wait_ge(gz_ps, n)
                act.activation(tz[:, cols(h)], GB[:, Z_, :], ACT.Tanh, scale=0.5,
                               bias=b_gate[:, 1:2]).then_inc(tz_ready, 1)
                act.wait_ge(cand_in, n)
                act.activation(nn[:, cols(h)], t2[:, cols(h)], ACT.Tanh,
                               bias=vec[:, R_BIH + 2:R_BIH + 3]).then_inc(cand_ready, 1)

            act.wait_ge(bias_ready, 1)
            def slot_trip(it):
                slot_exp(2 * it + 1, 0)
                square_slots(2 * it + 2, 1)
                copy_updates(2 * it + 1, 0)
                slot_exp(2 * it + 2, 1)
                gates(2 * it + 1, 0)
                copy_updates(2 * it + 2, 1)
                square_slots(2 * it + 3, 0)
                gates(2 * it + 2, 1)

            slot_trip(0)
            with act.Fori(1, ITERS) as it:
                slot_trip(it)

            def norm_back(k):
                for h in range(2):
                    act.wait_ge(ln_back[k], h + 1)
                    act.activation(xnT[:, cols(h)], qb(h, 1), ACT.Copy).then_inc(ln_out[k], 1)

            norm_back(1)
            for h in range(2):
                act.wait_ge(dl_ready, h + 1)
                act.activation(ed[:, tiles(h)], dl[:, tiles(h)], ACT.Exp).then_inc(ed_ready, 1)
            norm_back(2)
            for h in range(2):
                act.wait_ge(q1_ps, h + 1)
                act.activation(qT1[:, cols(h)], GB[0:DH, 2 * h, :], ACT.Identity, scale=QSCALE,
                               bias=bq_s[:, 0:1]).then_inc(q1_ready, 1)
            for h in range(2):
                act.wait_ge(max1_ready, h + 1)
                for j in range(HT):
                    t = h * HT + j
                    last = act.activation(E[:, t, :], SC[:, h, j // MT, (j % MT) * S:(j % MT + 1) * S],
                                          ACT.Exp, bias=neg_max[:, t:t + 1], accum_out=row_sum[:, t:t + 1])
                last.then_inc(exp1_ready, 1)
            for h in range(2):
                for m in range(MT):
                    act.wait_ge(pT1_ps, MT * h + m + 1)
                    act.activation(pT1[:, h, m, :], SC[:, h, m, :], ACT.Copy).then_inc(pT1_ready, 1)
            norm_back(3)
            for h in range(2):
                act.wait_ge(sh_ready, h + 1)
                act.activation(q1[:, tiles(h), :], q2[:, tiles(h), :], ACT.Exp).then_inc(ex_ready, 1)
            def expert_pair(i, first):
                for u in range(2 * NC):
                    s, c = u // NC, u % NC
                    n = 2 * NC * i + u + 1
                    act.wait_ge(w1_ps, n)
                    if not (first and u < 2):
                        act.wait_ge(h_used, n - 2)
                    act.activation(hh[u % 2][:, :], SC[:, u % 2, :, :].rearrange("p a b -> p (a b)"),
                                   ACT.Gelu, bias=b1s[s][:, c:c + 1]).then_inc(hh_ready, 1)
                    act.activation(SC[:, u % 2, :, :], SC[:, u % 2, :, :], ACT.Gelu,
                                   bias=b1s[s][:, c:c + 1]).then_inc(gelu_ready, 1)

            expert_pair(0, True)
            with act.Fori(1, NE // 2) as i:
                expert_pair(i, False)
            for h in range(2):
                act.wait_ge(oT_ps, h + 1)
                act.activation(o_tok[:, tiles(h), :], tiled(qb(h, 0)), ACT.Copy).then_inc(o_ready, 1)

        @block.vector
        def _(dve):
            steps = [0]

            def link(ins):
                steps[0] += 1
                ins.then_inc(dve_step, 1)
                dve.wait_ge(dve_step, steps[0])

            def ln_stats(k, h, src):
                if k:
                    dve.wait_ge(ln_tok[k], h + 1)
                for j in range(HT):
                    last = dve.bn_stats(st[:, k, h * HT + j, :], src(j))
                link(last)
                for j in range(HT):
                    last = dve.bn_aggr(mv[:, k, h * HT + j, :], st[:, k, h * HT + j, :])
                link(last)
                dve.tensor_scalar_add(ve[:, k, tiles(h)], mv[:, k, tiles(h), 1], LN_EPS).then_inc(ln_var[k], 1)

            def ln_normalise(k, h, src):
                dve.wait_ge(ln_rstd[k], h + 1)
                for j in range(HT):
                    t = h * HT + j
                    last = dve.tensor_scalar(xn_tok[:, t, :], src(j), mv[:, k, t, 0:1], rs[:, k, t:t + 1],
                                             ALU.subtract, ALU.mult)
                last.then_inc(ln_norm[k], 1)

            dve.wait_ge(ld_x, 32)
            for h in range(2):
                ln_stats(0, h, lambda j: x_tok[:, h * HT + j, :])
            dve.wait_ge(vecT, 1)
            dve.tensor_copy(vec[:, :], GB[:, 0, 0:NROW]).then_inc(vec_ready, 1)
            for h in range(2):
                ln_normalise(0, h, lambda j: x_tok[:, h * HT + j, :])
            dve.wait_ge(css_ready, 1)
            dve.tensor_scalar(cse[:, :], css[:, :], 1.0 / D, RMS_EPS, ALU.mult, ALU.add).then_inc(cse_ready, 1)
            dve.wait_ge(vec_ready, 1)
            dve.wait_ge(mq_ps, 1)
            dve.tensor_scalar(mq[:, :], GB[:, 1, 0:D], vec[:, R_IW:R_IW + 1], SCALE,
                              ALU.mult, ALU.mult).then_inc(mq_ready, 1)
            link(dve.tensor_tensor(b_sum[:, :], vec[:, R_BIH:R_BIH + 2], vec[:, R_BHH:R_BHH + 2], ALU.add))
            dve.tensor_scalar_mul(bq_s[:, :], vec[0:DH, R_BQ:R_BQ + 1], QSCALE)
            dve.tensor_scalar_mul(b_gate[:, :], b_sum[:, :], 0.5).then_inc(bias_ready, 1)
            dve.wait_ge(gxw_ps, 1)
            dve.tensor_scalar(gxw[:, :], GB[:, 0, 0:G3 * D], vec[:, R_IW:R_IW + 1], None,
                              ALU.mult).then_inc(gxw_ready, 1)

            def slot_ms(n, h):
                dve.wait_ge(ms_ps, n)
                dve.tensor_scalar(mse[:, tiles(h)], SC[:, h, 0, 0:HT], 1.0 / D, RMS_EPS,
                                  ALU.mult, ALU.add).then_inc(mse_ready, 1)

            def slot_norm(n, h):
                dve.wait_ge(rb_ps, n)
                dve.tensor_tensor(sn[:, cols(h)], SC[:, h, 1, :], slots[:, cols(h)], ALU.mult).then_inc(sn_ready, 1)

            slot_ms(1, 0)
            slot_norm(1, 0)
            dve.wait_ge(ob_ps, 1)
            dve.wait_ge(tg_ready, 1)
            dve.tensor_scalar(out_bias[:, :], GB[:, 3, 0:1], vec[:, R_BO:R_BO + 1], tg[:, 1:2],
                              ALU.add, ALU.mult).then_inc(ob_ready, 1)

            LOOP_STEPS = 2 * 7
            def slot_trip(it):
                k = [0]

                def loop_link(ins):
                    k[0] += 1
                    ins.then_inc(dve_loop, 1)
                    dve.wait_ge(dve_loop, LOOP_STEPS * it + k[0])

                def slot_max(n, h):
                    dve.wait_ge(score_ps, n)
                    dve.tensor_reduce(neg_max[:, tiles(h)], SC[:, h, :, :].rearrange("p b (m k) -> p (b m) k", m=MT),
                                      AX_X, ALU.max, negate=True).then_inc(max_ready, 1)

                def slot_values(n, h):
                    dve.wait_ge(exp_ready, n)
                    loop_link(dve.reciprocal(row_inv[:, tiles(h)], row_sum[:, tiles(h)]))
                    inv = row_inv[:, tiles(h)].rearrange("p (t a) -> p t a", a=1)
                    dve.tensor_copy(pv[:, tiles(h), D:D + 1], inv)
                    dve.tensor_tensor(pv[:, tiles(h), 0:D], pn_tok[:, tiles(h), :],
                                      inv.to_broadcast([P, HT, D]), ALU.mult).then_inc(pv_ready, 1)

                def scale_updates(n, h):
                    dve.wait_ge(upd_ps, n)
                    u = SC[:, h, :, 0:MT * (D + 1)].rearrange("p b (t c) -> p b t c", c=D + 1)
                    s_u = su[:, tiles(h)].rearrange("p (b t a) -> p b t a", b=BH, a=1)
                    loop_link(dve.tensor_scalar_add(s_u, u[:, :, :, D:D + 1], RMS_EPS))
                    loop_link(dve.reciprocal(siv[:, tiles(h)], su[:, tiles(h)]))
                    dve.tensor_tensor(upd_tok[:, tiles(h), :].rearrange("p (b t) d -> p b t d", b=BH),
                                      u[:, :, :, 0:D],
                                      siv[:, tiles(h)].rearrange("p (b t a) -> p b t a", b=BH, a=1)
                                      .to_broadcast([P, BH, MT, D]), ALU.mult).then_inc(upd_tok_ready, 1)

                def candidate(n, h):
                    c = cols(h)
                    dve.wait_ge(tr_ready, n)
                    loop_link(dve.tensor_scalar(rg[:, c], tr[:, c], 0.5, 0.5, ALU.mult, ALU.add))
                    dve.wait_ge(gn_ps, n)
                    loop_link(dve.scalar_tensor_tensor(t1[:, c], GB[:, HN_, :], vec[:, R_BHH + 2:R_BHH + 3],
                                                       rg[:, c], ALU.add, ALU.mult))
                    dve.tensor_tensor(t2[:, c], GB[:, XN_, :], t1[:, c], ALU.add).then_inc(cand_in, 1)

                def new_slots(n, h):
                    c = cols(h)
                    dve.wait_ge(cand_ready, n)
                    loop_link(dve.tensor_tensor(dd[:, c], slots[:, c], nn[:, c], ALU.subtract))
                    loop_link(dve.scalar_tensor_tensor(t1[:, c], tz[:, c], 1.0, dd[:, c], ALU.add, ALU.mult))
                    dve.scalar_tensor_tensor(slots[:, c], t1[:, c], 0.5, nn[:, c],
                                             ALU.mult, ALU.add).then_inc(slots_ready, 1)

                slot_max(2 * it + 1, 0)
                slot_values(2 * it + 1, 0)
                slot_ms(2 * it + 2, 1)
                scale_updates(2 * it + 1, 0)
                slot_norm(2 * it + 2, 1)
                slot_max(2 * it + 2, 1)
                candidate(2 * it + 1, 0)
                slot_values(2 * it + 2, 1)
                new_slots(2 * it + 1, 0)
                scale_updates(2 * it + 2, 1)
                slot_ms(2 * it + 3, 0)
                candidate(2 * it + 2, 1)
                slot_norm(2 * it + 3, 0)
                new_slots(2 * it + 2, 1)
                assert k[0] == LOOP_STEPS

            slot_trip(0)
            with dve.Fori(1, ITERS) as it:
                slot_trip(it)

            dve.wait_ge(slots_ready, 2 * ITERS + 2)
            for h in range(2):
                dve.scalar_tensor_tensor(x_res[:, cols(h)], slots[:, cols(h)], tg[:, 0:1], x_res[:, cols(h)],
                                         ALU.mult, ALU.add).then_inc(res_ready, 1)

            def layer_norm(k):
                for h in range(2):
                    ln_stats(k, h, lambda j: tiled(qb(h, 0))[:, j, :])
                for h in range(2):
                    ln_normalise(k, h, lambda j: tiled(qb(h, 0))[:, j, :])

            def per_tile(ap, h):
                return ap[:, tiles(h)].rearrange("p (t a) -> p t a", a=1).to_broadcast([P, HT, NE])

            layer_norm(1)
            iota_t = iota8[:, :].rearrange("p (a e) -> p a e", a=1).to_broadcast([P, HT, NE])
            for h in range(2):
                t = tiles(h)
                dve.wait_ge(lg0_ps, h + 1)
                link(dve.tensor_copy(lg[:, t, :], qb(h, 0)[:, 0:HT * NE].rearrange("p (t e) -> p t e", t=HT)))
                for j in range(HT):
                    last = dve.max(m8[:, h * HT + j, :], lg[:, h * HT + j, :])
                link(last)
                dve.tensor_tensor(dl[:, t], m8[:, t, 1], m8[:, t, 0], ALU.subtract).then_inc(dl_ready, 1)
                for j in range(HT):
                    last = dve.max_index(ix[:, h * HT + j, :], m8[:, h * HT + j, :], lg[:, h * HT + j, :])
                link(last)
                link(dve.tensor_copy(ixf[:, t, :], ix[:, t, :]))
                dve.tensor_tensor(q1[:, t, :], iota_t, ixf[:, t, 0:1].to_broadcast([P, HT, NE]), ALU.is_equal)
                dve.tensor_tensor(q2[:, t, :], iota_t, ixf[:, t, 1:2].to_broadcast([P, HT, NE]), ALU.is_equal)
                dve.wait_ge(ed_ready, h + 1)
                link(dve.tensor_scalar_add(den[:, t], ed[:, t], 1.0))
                link(dve.reciprocal(wa[:, t], den[:, t]))
                link(dve.tensor_scalar(wag[:, t], wa[:, t], tg[:, 2:3], None, ALU.mult))
                link(dve.tensor_tensor(wbg[:, t], ed[:, t], wag[:, t], ALU.mult))
                dve.tensor_tensor(q1[:, t, :], q1[:, t, :], per_tile(wag, h), ALU.mult)
                link(dve.tensor_tensor(q2[:, t, :], q2[:, t, :], per_tile(wbg, h), ALU.mult))
                dve.tensor_tensor(gw0[:, t, :], q1[:, t, :], q2[:, t, :], ALU.add).then_inc(gw0_ready, 1)
            n = 0
            for e in range(NE):
                for h in range(2):
                    n += 1
                    dve.wait_ge(wb0_ps, n)
                    if e >= 2:
                        dve.wait_ge(y0_step, n - 4)
                    dve.tensor_tensor(xe[:, h, e % 2, :], qb(h, 2 + e % 2), xnT[:, cols(h)],
                                      ALU.mult).then_inc(xe_ready, 1)
            for h in range(2):
                dve.wait_ge(y0_step, 2 * NE - 1 + h)
                dve.tensor_tensor(x_res[:, cols(h)], qb(h, 1), x_res[:, cols(h)], ALU.add).then_inc(res_ready, 1)

            layer_norm(2)
            for h in range(2):
                dve.wait_ge(s1_ps, h + 1)
                dve.tensor_reduce(neg_max[:, tiles(h)], SC[:, h, :, :].rearrange("p b (m k) -> p (b m) k", m=MT),
                                  AX_X, ALU.max, negate=True).then_inc(max1_ready, 1)
            for h in range(2):
                dve.wait_ge(exp1_ready, h + 1)
                link(dve.reciprocal(row_inv[:, tiles(h)], row_sum[:, tiles(h)]))
                for j in range(HT):
                    t = h * HT + j
                    last = dve.tensor_scalar(E[:, t, :], E[:, t, :], row_inv[:, t:t + 1], None, ALU.mult)
                last.then_inc(p1_ready, 1)
            for h in range(2):
                dve.wait_ge(o1_ps, h + 1)
                dve.scalar_tensor_tensor(x_res[:, cols(h)], GB[:, 2 * h, :], out_bias[:, 0:1], x_res[:, cols(h)],
                                         ALU.add, ALU.add).then_inc(res_ready, 1)

            layer_norm(3)
            for h in range(2):
                dve.wait_ge(ln_out[3], h + 1)
                link(dve.tensor_copy(xh[:, cols(h)], xnT[:, cols(h)]))
                dve.tensor_tensor(xl[:, cols(h)], xnT[:, cols(h)], xh[:, cols(h)].bitcast(f32),
                                  ALU.subtract).then_inc(xhl_ready, 1)
            for h in range(2):
                t = tiles(h)
                dve.wait_ge(lg1_ps, h + 1)
                link(dve.tensor_tensor(lg[:, t, :], qb(h, 0)[:, 0:HT * NE].rearrange("p (t e) -> p t e", t=HT),
                                       br_bc[:, :].rearrange("p (a e) -> p a e", a=1).to_broadcast([P, HT, NE]), ALU.add))
                for j in range(HT):
                    last = dve.max(m8[:, h * HT + j, :], lg[:, h * HT + j, :])
                link(last)
                dve.tensor_tensor(q2[:, t, :], lg[:, t, :], m8[:, t, 0:1].to_broadcast([P, HT, NE]),
                                  ALU.subtract).then_inc(sh_ready, 1)
                link(dve.tensor_tensor(gw1[:, t, :], lg[:, t, :], m8[:, t, 1:2].to_broadcast([P, HT, NE]), ALU.is_ge))
                dve.wait_ge(ex_ready, h + 1)
                link(dve.tensor_tensor(q1[:, t, :], q1[:, t, :], gw1[:, t, :], ALU.mult))
                link(dve.reduce_sum(den[:, t], q1[:, t, :], AX_X))
                link(dve.reciprocal(wa[:, t], den[:, t]))
                link(dve.tensor_scalar(wag[:, t], wa[:, t], tg[:, 3:4], None, ALU.mult))
                dve.tensor_tensor(gw1[:, t, :], q1[:, t, :], per_tile(wag, h), ALU.mult).then_inc(gw1_ready, 1)

            def gate_output(n, s):
                dve.wait_ge(h_used, NC * n)
                y = GB[:, 2 * s:2 * s + 2, :].rearrange("p a b -> p (a b)")
                dve.scalar_tensor_tensor(ygated[:, :], y, b2s[s][:, 0:1], wbc[s][:, :],
                                         ALU.add, ALU.mult).then_inc(y1_gated, 1)
                dve.wait_ge(y1_gated, n)
                dve.wait_ge(y1_added, n - 1)
                dve.tensor_tensor(x_res[:, :], x_res[:, :], ygated[:, :], ALU.add).then_inc(y1_added, 1)

            def expert_pair(i, first):
                for u in range(2 * NC):
                    s, c = u // NC, u % NC
                    if c == 0:
                        dve.wait_ge(wb1_ps, 2 * i + s + 1)
                        dve.tensor_copy(wbc[s][:, :], GB[:, 2 * s:2 * s + 2, :].rearrange("p a b -> p (a b)"))\
                           .then_inc(wb1_ready, 1)
                    n = 2 * NC * i + u + 1
                    dve.wait_ge(gelu_ready, n)
                    dve.tensor_tensor(hl[u % 2][:, :], SC[:, u % 2, :, :].rearrange("p a b -> p (a b)"),
                                      hh[u % 2][:, :].bitcast(f32), ALU.subtract).then_inc(hl_ready, 1)
                    if c == 1 and not (first and s == 0):
                        gate_output(2 * i + s, 1 - s)

            expert_pair(0, True)
            with dve.Fori(1, NE // 2) as i:
                expert_pair(i, False)
            gate_output(NE, 1)

        @block.tensor
        def _(pe):
            def transposes(bank, src, h):
                for j in range(HT):
                    last = pe.transpose(bank[:, j * P:(j + 1) * P], src(h * HT + j), ident[:, :])
                return last

            pe.wait_ge(id_ready, 1)
            pe.wait_ge(ld_x, 32)
            for h in range(2):
                transposes(SC[:, h, 1, :], lambda t: x_tok[:, t, :], h).then_inc(xT_ps, 1)
            pe.wait_ge(ld_gru, 32)
            for n, w in enumerate((wih, whh)):
                for g in range(G3):
                    last = pe.transpose(GB[:, 2 + n, g * D:(g + 1) * D], w[:, g, :], ident[:, :])
                last.then_inc(wT_ps, 1)
            pe.wait_ge(ld_qkv0, 48)
            pe.matmul(GB[:, 1, 0:D], wk0[:, :], wq0[:, :], start=True, stop=True).then_inc(mq_ps, 1)
            pe.wait_ge(ld_rows, 16 * len(row_loads))
            pe.transpose(GB[:, 0, 0:NROW], rows[:, :], ident[0:NROW, 0:NROW]).then_inc(vecT, 1)
            for h in range(2):
                pe.wait_ge(ln_norm[0], h + 1)
                transposes(SC[:, h, 0, :], lambda t: xn_tok[:, t, :], h).then_inc(ln_back[0], 1)
            pe.wait_ge(vec_ready, 1)
            pe.wait_ge(wT_ready, 1)
            pe.matmul(GB[:, 0, 0:G3 * D], wv0[:, :], wihT[:, :], start=True, stop=True).then_inc(gxw_ps, 1)
            pe.wait_ge(pn_ready, 1)
            for h in range(2):
                pe.wait_ge(xres_ready, h + 1)
                transposes(SC[:, h, 1, :], lambda t: pn_tok[:, t, :], h).then_inc(pnT_ps, 1)
            pe.wait_ge(mq_ready, 1)
            for h in range(2):
                pe.wait_ge(pnT_ready, h + 1)
                pe.matmul(GB[:, 1 + h, :], mq[:, :], pnT[:, cols(h)], start=True, stop=True).then_inc(kq_ps, 1)

            def slot_ms(n, h):
                pe.wait_ge(sq_ready, n)
                for j in range(HT):
                    t = h * HT + j
                    last = pe.matmul(SC[:, h, 0, j:j + 1], sq[:, t * P:(t + 1) * P], ones[:, :], start=True, stop=True)
                last.then_inc(ms_ps, 1)

            def slot_rstd_rows(n, h):
                pe.wait_ge(rst_ready, n)
                for j in range(HT):
                    t = h * HT + j
                    last = pe.transpose(SC[:, h, 1, j * P:(j + 1) * P], rst[:, t:t + 1].to_broadcast([P, P]), ident[:, :])
                last.then_inc(rb_ps, 1)

            slot_ms(1, 0)
            pe.wait_ge(gxw_ready, 1)
            transposes(GB[:, 0, :], lambda t: c_tok[:, t, :], 0).then_inc(ctxT_ps, 1)
            pe.wait_ge(wT_ready, 2)
            transposes(GB[:, 3, :], lambda t: c_tok[:, t, :], 1).then_inc(ctxT_ps, 1)
            slot_rstd_rows(1, 0)
            pe.wait_ge(ld_a1, 64)
            pe.wait_ge(kq_ready, 1)
            pe.transpose(GB[0:DH, 1, 0:D], wv1[:, :], ident[:, :]).then_inc(wv1T_ps, 1)
            pe.wait_ge(kq_ready, 2)
            pe.wait_ge(wv1T_ready, 1)
            pe.wait_ge(wos_step, 4)
            pe.matmul(GB[:, 2, 0:D], wv1T[:, :], wo1[:, 0, :], start=True, stop=True).then_inc(wvo_ps, 1)
            pe.wait_ge(ctxT_ready, 1)
            pe.matmul(GB[0:DH, 1, :], wk1[:, :], ctxT[:, cols(0)], start=True, stop=True).then_inc(kT1_ps, 1)
            pe.wait_ge(wvo_ready, 1)
            pe.wait_ge(ctxT_ready, 2)
            pe.matmul(GB[0:DH, 2, :], wk1[:, :], ctxT[:, cols(1)], start=True, stop=True).then_inc(kT1_ps, 1)
            pe.matmul(GB[:, 3, 0:1], wo1[:, 0, :], vec[0:DH, R_BV:R_BV + 1], start=True, stop=True).then_inc(ob_ps, 1)
            for h in range(2):
                if h:
                    pe.wait_ge(ob_ready, 1)
                for j in range(HT):
                    t = h * HT + j
                    last = pe.matmul(GB[:, 3 * h, j * P:(j + 1) * P], ctxT[:, t * P:(t + 1) * P], wvo[:, :],
                                     start=True, stop=True)
                last.then_inc(vo1_ps, 1)

            def slot_scores(n, h):
                pe.wait_ge(sn_ready, n)
                for j in range(HT):
                    t = h * HT + j
                    b = t // MT
                    last = pe.matmul(SC[:, h, j // MT, (j % MT) * S:(j % MT + 1) * S], kqT[:, t * P:(t + 1) * P],
                                     sn[:, b * S:(b + 1) * S], start=True, stop=True)
                last.then_inc(score_ps, 1)

            def slot_updates(n, h):
                pe.wait_ge(pv_ready, n)
                for b in range(BH):
                    for kt in range(MT):
                        for m in range(MT):
                            t = h * HT + b * MT + m
                            last = pe.matmul(SC[:, h, b, kt * (D + 1):(kt + 1) * (D + 1)],
                                             E[:, t, kt * P:(kt + 1) * P], pv[:, t, :],
                                             start=(m == 0), stop=(m == MT - 1))
                last.then_inc(upd_ps, 1)

            def updates_to_columns(n, h):
                pe.wait_ge(upd_tok_ready, n)
                pe.wait_ge(cand_in, n - 1)
                transposes(GB[:, XN_, :], lambda t: upd_tok[:, t, :], h).then_inc(updT_ps, 1)

            def state_gates(n, h):
                c = cols(h)
                pe.wait_ge(slots_ready, n)
                pe.wait_ge(tr_ready, n - 1)
                pe.matmul(GB[:, R_, :], whhT[:, 0:D], slots[:, c], start=True, stop=False)
                pe.wait_ge(tz_ready, n - 1)
                pe.matmul(GB[:, Z_, :], whhT[:, D:2 * D], slots[:, c], start=True, stop=False)
                pe.wait_ge(cand_in, n - 1)
                pe.matmul(GB[:, HN_, :], whhT[:, 2 * D:3 * D], slots[:, c], start=True, stop=True)

            def update_gates(n, h):
                c = cols(h)
                pe.wait_ge(updT_ready, n)
                pe.matmul(GB[:, R_, :], gxw[:, 0:D], updT[:, c], start=False, stop=True).then_inc(gr_ps, 1)
                pe.matmul(GB[:, XN_, :], gxw[:, 2 * D:3 * D], updT[:, c], start=True, stop=True).then_inc(gn_ps, 1)
                pe.matmul(GB[:, Z_, :], gxw[:, D:2 * D], updT[:, c], start=False, stop=True).then_inc(gz_ps, 1)

            pe.wait_ge(vo1_ready, 2)
            pe.wait_ge(kT1_ready, 2)
            def slot_trip(it):
                slot_scores(2 * it + 1, 0)
                state_gates(2 * it + 1, 0)
                slot_ms(2 * it + 2, 1)
                slot_updates(2 * it + 1, 0)
                slot_rstd_rows(2 * it + 2, 1)
                updates_to_columns(2 * it + 1, 0)
                slot_scores(2 * it + 2, 1)
                update_gates(2 * it + 1, 0)
                slot_updates(2 * it + 2, 1)
                state_gates(2 * it + 2, 1)
                updates_to_columns(2 * it + 2, 1)
                slot_ms(2 * it + 3, 0)
                update_gates(2 * it + 2, 1)
                slot_rstd_rows(2 * it + 3, 0)

            slot_trip(0)
            with pe.Fori(1, ITERS) as it:
                slot_trip(it)

            def layer_norm(k):
                for h in range(2):
                    pe.wait_ge(res_ready, 2 * (k - 1) + h + 1)
                    transposes(qb(h, 0), lambda t: x_res[:, t * P:(t + 1) * P], h).then_inc(ln_tok[k], 1)
                for h in range(2):
                    pe.wait_ge(ln_norm[k], h + 1)
                    transposes(qb(h, 1), lambda t: xn_tok[:, t, :], h).then_inc(ln_back[k], 1)

            def logits(k, h, w, done):
                pe.wait_ge(ln_out[k], h + 1)
                for j in range(HT):
                    t = h * HT + j
                    last = pe.matmul(qb(h, 0)[:, j * NE:(j + 1) * NE], xnT[:, t * P:(t + 1) * P], w,
                                     start=True, stop=True)
                last.then_inc(done, 1)

            pe.wait_ge(sn_ready, 2 * ITERS + 1)
            layer_norm(1)
            for h in range(2):
                logits(1, h, vec[:, R_GW:R_GW + NE], lg0_ps)
            pe.wait_ge(ld_f0, 32)

            def weight_rows(e, h):
                if e == 0:
                    pe.wait_ge(gw0_ready, h + 1)
                if e >= 2:
                    pe.wait_ge(xe_ready, 2 * (e - 2) + h + 1)
                for j in range(HT):
                    t = h * HT + j
                    last = pe.transpose(qb(h, 2 + e % 2)[:, j * P:(j + 1) * P], gw0[:, t, e:e + 1].to_broadcast([P, P]),
                                        ident[:, :])
                last.then_inc(wb0_ps, 1)

            for h in range(2):
                weight_rows(0, h)
            for e in range(NE):
                for h in range(2):
                    if e + 1 < NE:
                        weight_rows(e + 1, h)
                    pe.wait_ge(xe_ready, 2 * e + h + 1)
                    pe.matmul(qb(h, 1), we0[:, e, :], xe[:, h, e % 2, :], start=(e == 0),
                              stop=(e == NE - 1)).then_inc(y0_step, 1)

            layer_norm(2)
            for h in range(2):
                pe.wait_ge(ln_out[2], h + 1)
                pe.matmul(GB[0:DH, 2 * h, :], wq1[:, :], xnT[:, cols(h)], start=True, stop=True).then_inc(q1_ps, 1)
            for h in range(2):
                pe.wait_ge(q1_ready, h + 1)
                for j in range(HT):
                    t = h * HT + j
                    b = t // MT
                    last = pe.matmul(SC[:, h, j // MT, (j % MT) * S:(j % MT + 1) * S], qT1[:, t * P:(t + 1) * P],
                                     kT1[:, b * S:(b + 1) * S], start=True, stop=True)
                last.then_inc(s1_ps, 1)
            for h in range(2):
                pe.wait_ge(p1_ready, h + 1)
                for m in range(MT):
                    for j in range(HT):
                        last = pe.transpose(SC[:, h, m, j * P:(j + 1) * P], E[:, h * HT + j, m * P:(m + 1) * P],
                                            ident[:, :])
                    last.then_inc(pT1_ps, 1)
            for h in range(2):
                pe.wait_ge(pT1_ready, MT * (h + 1))
                for b in range(BH):
                    for m in range(MT):
                        last = pe.matmul(GB[:, 2 * h, b * S:(b + 1) * S], vo1[:, h * HT + b * MT + m, :],
                                         pT1[:, h, m, b * S:(b + 1) * S], start=(m == 0), stop=(m == MT - 1))
                last.then_inc(o1_ps, 1)

            layer_norm(3)
            for h in range(2):
                logits(3, h, wr1[:, :], lg1_ps)

            def up(i, u):
                s, c = (u // NC) % 2, u % NC
                k = slice(c * P, (c + 1) * P)
                if c == 0:
                    pe.wait_ge(w_ready, 4 * i + 2 * (u // NC) + 2)
                if not (isinstance(i, int) and 2 * NC * i + u < 2):
                    pe.wait_ge(hl_ready, 2 * NC * i + u - 1)
                for w, x, start, stop in ((w1h, xh, True, False), (w1h, xl, False, False), (w1l, xh, False, True)):
                    for h in range(2):
                        last = pe.matmul(SC[:, u % 2, h, :], w[s][:, k], x[:, cols(h)], start=start, stop=stop)
                last.then_inc(w1_ps, 1)

            def down(i, u):
                s, c = u // NC, u % NC
                pe.wait_ge(hl_ready, 2 * NC * i + u + 1)
                if c == 0:
                    pe.wait_ge(wb1_ready, 2 * i + s + 1)
                for w, x, start, stop in ((w2h, hh, c == 0, False), (w2h, hl, False, False), (w2l, hh, False, c == NC - 1)):
                    for h in range(2):
                        last = pe.matmul(GB[:, 2 * s + h, :], w[s][:, c, :], x[u % 2][:, cols(h)],
                                         start=start, stop=stop)
                last.then_inc(h_used, 1)

            def gate_rows(i, s):
                pe.wait_ge(gws_ready, 2 * i + s + 1)
                if not (isinstance(i, int) and i == 0):
                    pe.wait_ge(y1_gated, 2 * i + s - 1)
                for t in range(NT):
                    last = pe.transpose(GB[:, 2 * s + t // HT, (t % HT) * P:(t % HT + 1) * P],
                                        gws[s][:, t, :].to_broadcast([P, P]), ident[:, :])
                last.then_inc(wb1_ps, 1)

            def expert_pair(i, last_pair):
                for u in range(2 * NC):
                    if u % NC == 0:
                        gate_rows(i, u // NC)
                    if u + 1 < 2 * NC or not last_pair:
                        up(i, u + 1)
                    down(i, u)

            pe.wait_ge(xhl_ready, 2)
            pe.wait_ge(sh_ready, 2)
            up(0, 0)
            expert_pair(0, False)
            with pe.Fori(1, NE // 2 - 1) as i:
                expert_pair(i, False)
            expert_pair(NE // 2 - 1, True)

            pe.wait_ge(y1_added, NE)
            for h in range(2):
                transposes(qb(h, 0), lambda t: x_res[:, t * P:(t + 1) * P], h).then_inc(oT_ps, 1)


_INS = ["x", "ctx_1024", "g_xattn", "g_ffn", "L0_xattn_Wq", "L0_xattn_Wk", "L0_xattn_Wv",
        "L0_xattn_gru_wih", "L0_xattn_gru_whh", "L0_xattn_gru_bih", "L0_xattn_gru_bhh",
        "L0_xattn_slot_norm_w", "L0_xattn_input_norm_w", "L0_ffn_gate_w", "L0_ffn_We",
        "L1_xattn_Wq", "L1_xattn_bq", "L1_xattn_Wk", "L1_xattn_bk", "L1_xattn_Wv", "L1_xattn_bv",
        "L1_xattn_Wo", "L1_xattn_bo", "L1_ffn_W1", "L1_ffn_b1", "L1_ffn_W2", "L1_ffn_b2",
        "L1_ffn_Wr", "L1_ffn_br"]


def kernel(**inputs):
    import numpy as _np
    import concourse.bacc as _bacc
    from concourse import mybir as _mybir
    from concourse.bass_utils import run_bass_kernel_spmd as _run

    nc = _bacc.Bacc("TRN2", target_bir_lowering=False, num_devices=1)
    arrays, args = {}, []
    for name in _INS:
        a = _np.ascontiguousarray(inputs[name])
        arrays[f"in_{name}"] = a
        args.append(nc.dram_tensor(f"in_{name}", a.shape, _mybir.dt.from_np(a.dtype), kind="ExternalInput").ap())
    shape = arrays["in_x"].shape
    args.append(nc.dram_tensor("out_x", shape, _mybir.dt.float32, kind="ExternalOutput").ap())
    flamingo_gated_two_layer_kernel(nc, *args)
    r = _run(nc, [arrays], core_ids=[0])
    return r.results[0]["out_x"]
```

```python
import concourse.bass as bass
from concourse import mybir
from contextlib import ExitStack


def flamingo_gated_two_layer_kernel(
    nc: bass.Bass,
    x_in: bass.AP, ctx_in: bass.AP, g_xattn: bass.AP, g_ffn: bass.AP,
    a0_Wq: bass.AP, a0_Wk: bass.AP, a0_Wv: bass.AP,
    gru_wih: bass.AP, gru_whh: bass.AP, gru_bih: bass.AP, gru_bhh: bass.AP,
    slot_norm_w: bass.AP, input_norm_w: bass.AP,
    f0_gate_w: bass.AP, f0_We: bass.AP,
    a1_Wq: bass.AP, a1_bq: bass.AP, a1_Wk: bass.AP, a1_bk: bass.AP,
    a1_Wv: bass.AP, a1_bv: bass.AP, a1_Wo: bass.AP, a1_bo: bass.AP,
    f1_W1: bass.AP, f1_b1: bass.AP, f1_W2: bass.AP, f1_b2: bass.AP,
    f1_Wr: bass.AP, f1_br: bass.AP,
    out: bass.AP,
):
    f32 = mybir.dt.float32
    f32r = mybir.dt.float32r
    u32 = mybir.dt.uint32
    ALU = mybir.AluOpType
    ACT = mybir.ActivationFunctionType
    AX_X = mybir.AxisListType.X

    B, S, D = x_in.shape
    T = B * S
    P = 128
    NT = T // P
    HT = NT // 2
    HW = HT * P
    BH = B // 2
    MT = S // P
    G3 = 3
    NE = f0_We.shape[0]
    DH = a1_Wq.shape[1]
    NHEAD = a1_Wo.shape[0] // DH
    HID = f1_W1.shape[2]
    NC = HID // P
    ITERS = 3
    SCALE = float(D) ** -0.5
    QSCALE = float(DH) ** -0.5
    RMS_EPS, LN_EPS = 1e-6, 1e-5

    R_BIH, R_BHH, R_SW, R_IW = 0, 3, 6, 7
    NROW_A = 8
    R_BQ, R_BK, R_BV, R_B1 = 0, 1, 2, 3
    R_B2 = R_B1 + NE * NC
    R_GW = R_B2 + NE
    NROW = R_GW + NE

    x_v = x_in.rearrange("b (t p) d -> p (b t) d", p=P)
    ctx_v = ctx_in.rearrange("b (t p) d -> p (b t) d", p=P)
    out_v = out.rearrange("b (t p) d -> p (b t) d", p=P)
    W1_v = f1_W1.rearrange("e d h -> d e h")
    W2_v = f1_W2.rearrange("e (c p) d -> p e c d", p=P)

    ctx = ExitStack()
    with ctx:
        def sb(name, shape, dt=f32):
            return ctx.enter_context(nc.sbuf_tensor(name, shape, dt))

        def sem(name):
            return ctx.enter_context(nc.semaphore(name))

        ident = sb("ident", [P, P])
        neg_half = sb("neg_half", [P, NT])
        ones = sb("ones", [P, 1])
        iota8 = sb("iota8", [P, NE])
        rows_a = sb("rows_a", [NROW_A, P])
        vec_a = sb("vec_a", [P, NROW_A])
        rows = sb("rows", [NROW, P])
        vec = sb("vec", [P, NROW])
        g_raw = sb("g_raw", [P, 4])
        tg = sb("tg", [P, 4])
        br_bc = sb("br_bc", [P, NE])
        b_gate = sb("b_gate", [P, 2])
        b_sum = sb("b_sum", [P, 2])
        bq_s = sb("bq_s", [DH, 1])
        bo_bc = sb("bo_bc", [P, D])
        bias_row = sb("bias_row", [P, D])
        out_bias = sb("out_bias", [P, D])

        x_tok = sb("x_tok", [P, NT, D])
        c_tok = sb("c_tok", [P, NT, D])
        pn_tok = sb("pn_tok", [P, NT, D])
        pnT = sb("pnT", [P, T])
        kqT = sb("kqT", [P, T])
        wq0 = sb("wq0", [P, D])
        wk0 = sb("wk0", [P, D])
        wv0 = sb("wv0", [P, D])
        wih = sb("wih", [P, G3, D])
        whh = sb("whh", [P, G3, D])
        mq = sb("mq", [P, D])
        wihT = sb("wihT", [P, G3 * D])
        whhT = sb("whhT", [P, G3 * D])
        gxw = sb("gxw", [P, G3 * D])
        wq1 = sb("wq1", [P, DH])
        wk1 = sb("wk1", [P, DH])
        wv1 = sb("wv1", [P, DH])
        wv1T = sb("wv1T", [DH, D])
        wo1 = sb("wo1", [DH, NHEAD, D])
        wvo = sb("wvo", [P, D])
        we0 = sb("we0", [P, NE, D])
        we0h = sb("we0h", [P, NE, D], f32r)
        we0l = sb("we0l", [P, NE, D], f32r)
        gwh = sb("gwh", [P, NE], f32r)
        gwl = sb("gwl", [P, NE], f32r)
        wrh = sb("wrh", [P, NE], f32r)
        wrl = sb("wrl", [P, NE], f32r)
        wr1 = sb("wr1", [P, NE])

        st = sb("st", [P, 4, NT, 6])
        mv = sb("mv", [P, 4, NT, 2])
        ve = sb("ve", [P, 4, NT])
        rs = sb("rs", [P, 4, NT])
        css = sb("css", [P, NT])
        cse = sb("cse", [P, NT])
        crs = sb("crs", [P, NT])

        slots = sb("slots", [P, T])
        sq = sb("sq", [P, T])
        sn = sb("sn", [P, T])
        mse = sb("mse", [P, NT])
        rst = sb("rst", [P, NT])
        neg_max = sb("neg_max", [P, NT])
        row_sum = sb("row_sum", [P, NT])
        row_inv = sb("row_inv", [P, NT])
        E = sb("E", [P, NT, S])
        pv = sb("pv", [P, NT, D + 1])
        su = sb("su", [P, NT])
        siv = sb("siv", [P, NT])
        upd_tok = sb("upd_tok", [P, NT, D])
        updT = sb("updT", [P, T])
        tr = sb("tr", [P, T])
        tz = sb("tz", [P, T])
        rg = sb("rg", [P, T])
        t1 = sb("t1", [P, T])
        t2 = sb("t2", [P, T])
        nn = sb("nn", [P, T])
        dd = sb("dd", [P, T])

        xn_tok = sb("xn_tok", [P, NT, D])
        xnT = sn
        ctxT = pnT
        kT1 = nn[0:DH, :]
        qT1 = sq[0:DH, :]
        vo1 = updT[:, :].rearrange("p (t d) -> p t d", t=NT)
        pT1 = [rg, dd]
        acc = t1
        odd_acc = sb("odd_acc", [P, NT, D])
        lg = sb("lg", [P, NT, NE])
        m8 = sb("m8", [P, NT, 8])
        ix = sb("ix", [P, NT, 8], u32)
        ixf = sb("ixf", [P, NT, 8])
        dl = sb("dl", [P, NT])
        ed = sb("ed", [P, NT])
        den = sb("den", [P, NT])
        wa = sb("wa", [P, NT])
        wag = sb("wag", [P, NT])
        wbg = sb("wbg", [P, NT])
        q1 = sb("q1", [P, NT, NE])
        q2 = sb("q2", [P, NT, NE])
        gw0 = sb("gw0", [P, NT, NE])
        gw1 = sb("gw1", [P, NT, NE])
        gT1 = sb("gT1", [NE, T])
        xh = sb("xh", [P, T], f32r)
        xl = sb("xl", [P, T], f32r)
        w1r = [sb(f"w1r{s}", [P, HID]) for s in range(2)]
        w2r = [sb(f"w2r{s}", [P, NC, D]) for s in range(2)]
        w1h = [sb(f"w1h{s}", [P, HID], f32r) for s in range(2)]
        w1l = [sb(f"w1l{s}", [P, HID], f32r) for s in range(2)]
        w2h = [sb(f"w2h{s}", [P, NC, D], f32r) for s in range(2)]
        w2l = [sb(f"w2l{s}", [P, NC, D], f32r) for s in range(2)]
        b1s = [sb(f"b1s{s}", [P, NC]) for s in range(2)]
        b2s = [sb(f"b2s{s}", [P, 1]) for s in range(2)]
        wbc = [tr, tz]
        NH = 4
        hh = [sb(f"hh{s}", [P, T], f32r) for s in range(NH)]
        hl = [sb(f"hl{s}", [P, T], f32r) for s in range(NH)]
        ygated = t2
        o_tok = upd_tok

        PS = ctx.enter_context(nc.psum_tensor("PS", [P, 8, 512], f32))
        SC = PS[:, 0:4, :].rearrange("p (h b) c -> p h b c", h=2)
        R_, Z_, XN_, HN_ = 4, 5, 6, 7
        gates_dram = nc.dram_tensor("gates_dram", [NE, T], f32, kind="Internal").ap()

        ld_wv0 = sem("ld_wv0")
        ld_x, ld_c, ld_rows, ld_gate = sem("ld_x"), sem("ld_c"), sem("ld_rows"), sem("ld_gate")
        ld_qkv0, ld_gru, ld_a1, ld_f0 = sem("ld_qkv0"), sem("ld_gru"), sem("ld_a1"), sem("ld_f0")
        ld_ffn = [sem("ld_ffn0"), sem("ld_ffn1")]
        ld_rows_a, ld_bc, ld_gates, gates_stored = sem("ld_rows_a"), sem("ld_bc"), [sem("ld_gates0"), sem("ld_gates1")], sem("gates_stored")
        rows_clear, id_clear, id_ready, consts = sem("rows_clear"), sem("id_clear"), sem("id_ready"), sem("consts")
        stored = sem("stored")
        vecA_ps, vecA_ready = sem("vecA_ps"), sem("vecA_ready")
        vecT, vec_ready, tg_ready, bias_ready = sem("vecT"), sem("vec_ready"), sem("tg_ready"), sem("bias_ready")
        we0_high, we0_ready, bias_added = sem("we0_high"), sem("we0_ready"), sem("bias_added")
        slotsT_ps, gw_split, xh_ready, xl_ready = (sem(n) for n in ("slotsT_ps", "gw_split", "xh_ready", "xl_ready"))
        mq_ps, mq_ready, wT_ps, wT_ready, gxw_ps, gxw_ready = (sem(n) for n in (
            "mq_ps", "mq_ready", "wT_ps", "wT_ready", "gxw_ps", "gxw_ready"))
        css_ready, cse_ready, crs_ready, pn_ready = sem("css_ready"), sem("cse_ready"), sem("crs_ready"), sem("pn_ready")
        pnT_ps, pnT_ready, kq_ps, kq_ready = sem("pnT_ps"), sem("pnT_ready"), sem("kq_ps"), sem("kq_ready")
        wos_step, gT1_ps, gT1_ready = sem("wos_step"), sem("gT1_ps"), sem("gT1_ready")
        wv1T_ps, wv1T_ready, wvo_ps, wvo_ready = sem("wv1T_ps"), sem("wv1T_ready"), sem("wvo_ps"), sem("wvo_ready")
        ctxT_ps, ctxT_ready, kT1_ps, kT1_ready = sem("ctxT_ps"), sem("ctxT_ready"), sem("kT1_ps"), sem("kT1_ready")
        vo1_ps, vo1_ready, ob_ps, ob_ready = sem("vo1_ps"), sem("vo1_ready"), sem("ob_ps"), sem("ob_ready")
        ln_var = [sem(f"ln_var{k}") for k in range(4)]
        ln_rstd = [sem(f"ln_rstd{k}") for k in range(4)]
        ln_norm = [sem(f"ln_norm{k}") for k in range(4)]
        ln_back = [sem(f"ln_back{k}") for k in range(4)]
        ln_out = [sem(f"ln_out{k}") for k in range(4)]
        slots_ready, sq_ready, ms_ps, mse_ready, rst_ready, rb_ps, sn_ready = (sem(n) for n in (
            "slots_ready", "sq_ready", "ms_ps", "mse_ready", "rst_ready", "rb_ps", "sn_ready"))
        score_ps, max_ready, exp_ready, pv_ready, upd_ps, upd_tok_ready, updT_ps, updT_ready = (sem(n) for n in (
            "score_ps", "max_ready", "exp_ready", "pv_ready", "upd_ps", "upd_tok_ready", "updT_ps", "updT_ready"))
        gr_ps, gn_ps, gz_ps, tr_ready, tz_ready, cand_in, cand_ready = (sem(n) for n in (
            "gr_ps", "gn_ps", "gz_ps", "tr_ready", "tz_ready", "cand_in", "cand_ready"))
        dve_step, dve_loop, res_ready = sem("dve_step"), sem("dve_loop"), sem("res_ready")
        lg0_ps, dl_ready, ed_ready, gw0_ready, y0_ps, y0_read, y0_sum = (sem(n) for n in (
            "lg0_ps", "dl_ready", "ed_ready", "gw0_ready", "y0_ps", "y0_read", "y0_sum"))
        q1_ps, q1_ready, s1_ps, max1_ready, exp1_ready, p1_ready, pT1_ps, pT1_ready, o1_ps = (sem(n) for n in (
            "q1_ps", "q1_ready", "s1_ps", "max1_ready", "exp1_ready", "p1_ready", "pT1_ps", "pT1_ready", "o1_ps"))
        gate_sum, lg1_ps, sh_ready, ex_ready, gw1_ready = (sem(n) for n in (
            "gate_sum", "lg1_ps", "sh_ready", "ex_ready", "gw1_ready"))
        w_high, w_ready, w1_ps, hh_ready, gelu_ready, hl_ready, h_used, w1_ready, w2_high, y1_gated, y1_added = (sem(n) for n in (
            "w_high", "w_ready", "w1_ps", "hh_ready", "gelu_ready", "hl_ready", "h_used", "w1_ready", "w2_high", "y1_gated", "y1_added"))
        oT_ps, o_ready = sem("oT_ps"), sem("o_ready")

        block = ctx.enter_context(nc.Block())

        def cols(h):
            return slice(h * HW, (h + 1) * HW)

        def tiles(h):
            return slice(h * HT, (h + 1) * HT)

        def tiled(ap, n=HT):
            return ap.rearrange("p (t d) -> p t d", t=n)

        def row(v):
            return v.rearrange("(a d) -> a d", a=1)

        row_loads_a = [
            (R_BIH, G3, gru_bih.rearrange("(g d) -> g d", d=P)),
            (R_BHH, G3, gru_bhh.rearrange("(g d) -> g d", d=P)),
            (R_SW, 1, row(slot_norm_w)),
            (R_IW, 1, row(input_norm_w)),
        ]
        row_loads = [
            (R_BQ, 1, row(a1_bq), DH),
            (R_BK, 1, row(a1_bk), DH),
            (R_BV, 1, row(a1_bv), DH),
            (R_B1, NE * NC, f1_b1.rearrange("e (c d) -> (e c) d", d=P), P),
            (R_B2, NE, f1_b2, P),
            (R_GW, NE, f0_gate_w, P),
        ]

        @block.sync
        def _(sp):
            sp.dma_start(x_tok[:, :, :], x_v).then_inc(ld_x, 16)
            sp.dma_start(c_tok[:, :, :], ctx_v).then_inc(ld_c, 16)
            sp.dma_start(wk0[:, :], a0_Wk).then_inc(ld_qkv0, 16)
            sp.dma_start(wq0[:, :], a0_Wq).then_inc(ld_qkv0, 16)
            for r, n, src in row_loads_a:
                sp.dma_start(rows_a[r:r + n, :], src).then_inc(ld_rows_a, 16)
            sp.dma_start(whh[:, :, :], gru_whh.rearrange("(g p) d -> p g d", p=P)).then_inc(ld_gru, 16)
            sp.dma_start(wih[:, :, :], gru_wih.rearrange("(g p) d -> p g d", p=P)).then_inc(ld_gru, 16)
            sp.dma_start(wv0[:, :], a0_Wv).then_inc(ld_wv0, 16)
            sp.dma_start(we0[:, :, :], f0_We.rearrange("e d m -> d e m")).then_inc(ld_f0, 16)
            sp.dma_start(wr1[:, :], f1_Wr).then_inc(ld_f0, 16)
            sp.wait_ge(rows_clear, 1)
            for r, n, src, w in row_loads:
                sp.dma_start(rows[r:r + n, 0:w], src).then_inc(ld_rows, 16)
            sp.dma_start(g_raw[:, 0:2], g_xattn.partition_broadcast(P)).then_inc(ld_gate, 16)
            sp.dma_start(g_raw[:, 2:4], g_ffn.partition_broadcast(P)).then_inc(ld_gate, 16)
            sp.dma_start(br_bc[:, :], f1_br.partition_broadcast(P)).then_inc(ld_bc, 16)
            sp.dma_start(bo_bc[:, :], a1_bo.partition_broadcast(P)).then_inc(ld_bc, 16)
            sp.dma_start(wo1[:, :, :], a1_Wo.rearrange("(n p) d -> p n d", p=DH)).then_inc(ld_a1, 16)
            for dst, src in ((wq1, a1_Wq), (wk1, a1_Wk), (wv1, a1_Wv)):
                sp.dma_start(dst[:, :], src).then_inc(ld_a1, 16)
            for s in range(2):
                sp.dma_start(w1r[s][:, :], W1_v[:, s, :]).then_inc(ld_ffn[s], 16)
                sp.dma_start(w2r[s][:, :, :], W2_v[:, s, :, :]).then_inc(ld_ffn[s], 16)
            sp.wait_ge(gT1_ready, 1)
            sp.dma_start(gates_dram, gT1[:, :]).then_inc(gates_stored, 16)
            sp.wait_ge(gates_stored, 16)
            for s in range(2):
                sp.dma_start(wbc[s][:, :], gates_dram[s, :].partition_broadcast(P)).then_inc(ld_gates[s], 16)
            with sp.Fori(1, NE // 2) as i:
                for s in range(2):
                    sp.wait_ge(w_ready, 4 * i + 2 * s - 2)
                    sp.dma_start(w1r[s][:, :], W1_v[:, bass.ds(2 * i + s, 1), :]).then_inc(ld_ffn[s], 16)
                    sp.dma_start(w2r[s][:, :, :], W2_v[:, bass.ds(2 * i + s, 1), :, :]).then_inc(ld_ffn[s], 16)
                    sp.wait_ge(y1_gated, 4 * i + 2 * s - 2)
                    sp.dma_start(wbc[s][:, :], gates_dram[bass.ds(2 * i + s, 1), :].rearrange("a t -> (a t)")
                                 .partition_broadcast(P)).then_inc(ld_gates[s], 16)
            for h in range(2):
                sp.wait_ge(o_ready, h + 1)
                sp.dma_start(out_v[:, tiles(h), :], o_tok[:, tiles(h), :]).then_inc(stored, 16)
            sp.wait_ge(stored, 32)

        @block.gpsimd
        def _(pool):
            pool.memset(rows[:, :], 0.0).then_inc(rows_clear, 1)
            pool.memset(ident[:, :], 0.0).then_inc(id_clear, 1)
            pool.memset(ones[:, :], 1.0)
            pool.memset(neg_half[:, :], -0.5).then_inc(consts, 1)
            pool.wait_ge(id_clear, 1)
            pool.affine_select(out=ident[:, :], in_=ident[:, :], compare_op=ALU.not_equal, fill=1.0,
                               base=0, pattern=[[-1, P]], channel_multiplier=1).then_inc(id_ready, 1)
            pool.iota(iota8[:, :], pattern=[[1, NE]], base=0, channel_multiplier=0,
                      allow_small_or_imprecise_dtypes=True).then_inc(consts, 1)
            pool.wait_ge(consts, 2)
            for h in range(2):
                pool.wait_ge(ln_var[0], h + 1)
                pool.tensor_tensor(rs[:, 0, tiles(h)], ve[:, 0, tiles(h)], neg_half[:, 0:HT],
                                   ALU.pow).then_inc(ln_rstd[0], 1)
            pool.wait_ge(cse_ready, 1)
            pool.tensor_tensor(crs[:, :], cse[:, :], neg_half[:, :], ALU.pow).then_inc(crs_ready, 1)

            def slot_rstd(n, h):
                pool.wait_ge(mse_ready, n)
                pool.tensor_tensor(rst[:, tiles(h)], mse[:, tiles(h)], neg_half[:, 0:HT],
                                   ALU.pow).then_inc(rst_ready, 1)

            slot_rstd(1, 0)
            pool.wait_ge(ld_f0, 32)
            pool.tensor_copy(we0h[:, :, :], we0[:, :, :]).then_inc(we0_high, 1)
            pool.tensor_copy(wrh[:, :], wr1[:, :]).then_inc(we0_high, 1)
            pool.wait_ge(we0_high, 2)
            pool.tensor_tensor(we0l[:, :, :], we0[:, :, :], we0h[:, :, :].bitcast(f32), ALU.subtract).then_inc(we0_ready, 1)
            pool.tensor_tensor(wrl[:, :], wr1[:, :], wrh[:, :].bitcast(f32), ALU.subtract).then_inc(we0_ready, 1)

            def slot_trip(it):
                slot_rstd(2 * it + 2, 1)
                slot_rstd(2 * it + 3, 0)

            slot_trip(0)
            pool.wait_ge(ld_a1, 64)
            n, k = NHEAD, 0
            while n > 1:
                n //= 2
                k += 1
                pool.tensor_tensor(wo1[:, 0:n, :], wo1[:, 0:n, :], wo1[:, n:2 * n, :], ALU.add).then_inc(wos_step, 1)
                pool.wait_ge(wos_step, k)
            with pool.Fori(1, ITERS) as it:
                slot_trip(it)

            def token_rstd(k):
                for h in range(2):
                    pool.wait_ge(ln_var[k], h + 1)
                    pool.tensor_tensor(rs[:, k, tiles(h)], ve[:, k, tiles(h)], neg_half[:, 0:HT],
                                       ALU.pow).then_inc(ln_rstd[k], 1)

            def split_weights(i, s, first):
                pool.wait_ge(ld_ffn[s], 32 * i + 32)
                if not first:
                    pool.wait_ge(w1_ps, NC * (2 * i + s - 1))
                    pool.wait_ge(gelu_ready, NC * (2 * i + s - 1))
                pool.tensor_tensor(w1h[s][:, :], w1r[s][:, :], ones[:, :].to_broadcast([P, HID]), ALU.mult).then_inc(w_high, 1)
                pool.tensor_copy(b1s[s][:, :], vec[:, bass.ds(R_B1 + NC * (2 * i + s), NC)]).then_inc(w_high, 1)
                pool.wait_ge(w_high, 2 * (2 * i + s) + 2)
                pool.tensor_tensor(w1l[s][:, :], w1r[s][:, :], w1h[s][:, :].bitcast(f32), ALU.subtract).then_inc(w1_ready, 1)
                if not first:
                    pool.wait_ge(h_used, NC * (2 * i + s - 1))
                    pool.wait_ge(y1_gated, 2 * (2 * i + s - 1))
                pool.tensor_tensor(w2h[s][:, :, :], w2r[s][:, :, :],
                                   ones[:, :].rearrange("p (a b) -> p a b", a=1).to_broadcast([P, NC, D]), ALU.mult).then_inc(w2_high, 1)
                pool.tensor_copy(b2s[s][:, :], vec[:, bass.ds(R_B2 + 2 * i + s, 1)]).then_inc(w2_high, 1)
                pool.wait_ge(w2_high, 2 * (2 * i + s) + 2)
                pool.tensor_tensor(w2l[s][:, :, :], w2r[s][:, :, :], w2h[s][:, :, :].bitcast(f32), ALU.subtract).then_inc(w_ready, 2)

            token_rstd(1)
            pool.wait_ge(vec_ready, 1)
            split_weights(0, 0, True)
            split_weights(0, 1, True)
            token_rstd(2)
            pool.wait_ge(ln_norm[2], 2)
            pool.wait_ge(ob_ready, 1)
            pool.tensor_tensor(x_tok[:, :, :], x_tok[:, :, :],
                               out_bias[:, :].rearrange("p (a d) -> p a d", a=1).to_broadcast([P, NT, D]),
                               ALU.add).then_inc(bias_added, 1)
            token_rstd(3)
            with pool.Fori(1, NE // 2) as i:
                for s in range(2):
                    split_weights(i, s, False)

        @block.scalar
        def _(act):
            act.wait_ge(ld_c, 16)
            for t in range(NT):
                last = act.activation(updT[:, t * P:(t + 1) * P], c_tok[:, t, :], ACT.Square,
                                      accum_out=css[:, t:t + 1])
            last.then_inc(css_ready, 1)
            act.wait_ge(ln_back[0], 1)
            act.activation(slots[:, cols(0)], PS[:, 0, :], ACT.Copy).then_inc(slots_ready, 1)
            act.wait_ge(slots_ready, 1)
            act.activation(sq[:, cols(0)], slots[:, cols(0)], ACT.Square).then_inc(sq_ready, 1)
            act.wait_ge(pnT_ps, 1)
            act.activation(pnT[:, cols(0)], PS[:, 1, :], ACT.Copy).then_inc(pnT_ready, 1)
            act.wait_ge(ln_back[0], 2)
            act.activation(slots[:, cols(1)], PS[:, 2, :], ACT.Copy).then_inc(slots_ready, 1)
            act.wait_ge(pnT_ps, 2)
            act.activation(pnT[:, cols(1)], PS[:, 3, :], ACT.Copy).then_inc(pnT_ready, 1)
            act.wait_ge(vecA_ready, 1)
            for h, bank in ((0, HN_), (1, R_)):
                act.wait_ge(kq_ps, h + 1)
                act.activation(kqT[:, cols(h)], PS[:, bank, :], ACT.Copy,
                               scale=vec_a[:, R_SW:R_SW + 1]).then_inc(kq_ready, 1)
            for n, (bank, dst) in enumerate(((XN_, whhT), (Z_, wihT))):
                act.wait_ge(wT_ps, n + 1)
                act.activation(dst[:, :], PS[:, bank, 0:G3 * D], ACT.Copy).then_inc(wT_ready, 1)

            def square_slots(n, h):
                act.wait_ge(slots_ready, n)
                act.activation(sq[:, cols(h)], slots[:, cols(h)], ACT.Square).then_inc(sq_ready, 1)

            def slot_exp(n, h):
                act.wait_ge(max_ready, n)
                for j in range(HT):
                    t = h * HT + j
                    last = act.activation(E[:, t, :], SC[:, h, j // MT, (j % MT) * S:(j % MT + 1) * S],
                                          ACT.Exp, bias=neg_max[:, t:t + 1], accum_out=row_sum[:, t:t + 1])
                last.then_inc(exp_ready, 1)

            def copy_updates(n, h):
                act.wait_ge(updT_ps, n)
                act.activation(updT[:, cols(h)], PS[:, XN_, :], ACT.Copy).then_inc(updT_ready, 1)

            def gates(n, h):
                act.wait_ge(gr_ps, n)
                act.activation(tr[:, cols(h)], PS[:, R_, :], ACT.Tanh, scale=0.5,
                               bias=b_gate[:, 0:1]).then_inc(tr_ready, 1)
                act.wait_ge(gz_ps, n)
                act.activation(tz[:, cols(h)], PS[:, Z_, :], ACT.Tanh, scale=0.5,
                               bias=b_gate[:, 1:2]).then_inc(tz_ready, 1)
                act.wait_ge(cand_in, n)
                act.activation(nn[:, cols(h)], t2[:, cols(h)], ACT.Tanh,
                               bias=vec_a[:, R_BIH + 2:R_BIH + 3]).then_inc(cand_ready, 1)

            act.wait_ge(bias_ready, 1)
            def slot_trip(it):
                square_slots(2 * it + 2, 1)
                slot_exp(2 * it + 1, 0)
                copy_updates(2 * it + 1, 0)
                slot_exp(2 * it + 2, 1)
                gates(2 * it + 1, 0)
                copy_updates(2 * it + 2, 1)
                square_slots(2 * it + 3, 0)
                gates(2 * it + 2, 1)

            slot_trip(0)
            with act.Fori(1, ITERS) as it:
                slot_trip(it)

            act.wait_ge(ld_gate, 32)
            act.activation(tg[:, :], g_raw[:, :], ACT.Tanh).then_inc(tg_ready, 1)
            for h in range(2):
                act.wait_ge(ctxT_ps, h + 1)
                act.activation(ctxT[:, cols(h)], PS[:, 4 + h, :], ACT.Copy).then_inc(ctxT_ready, 1)
            act.wait_ge(wv1T_ps, 1)
            act.activation(wv1T[:, :], PS[0:DH, 6, 0:D], ACT.Copy).then_inc(wv1T_ready, 1)
            act.wait_ge(wvo_ps, 1)
            act.activation(wvo[:, :], PS[:, 7, 0:D], ACT.Copy).then_inc(wvo_ready, 1)

            def norm_high(k, h):
                act.wait_ge(ln_back[k], h + 1)
                act.activation(xh[:, cols(h)], PS[:, 2 * h + 1, :], ACT.Copy).then_inc(xh_ready, 1)

            def keys1(h):
                act.wait_ge(kT1_ps, h + 1)
                act.activation(kT1[:, cols(h)], PS[0:DH, 6 + h, :], ACT.Identity,
                               bias=vec[0:DH, R_BK:R_BK + 1]).then_inc(kT1_ready, 1)

            def values1(n, h):
                act.wait_ge(vo1_ps, n)
                act.activation(vo1[:, tiles(h), :], tiled(PS[:, 4 + h, :]), ACT.Copy,
                               scale=tg[:, 1:2]).then_inc(vo1_ready, 1)

            act.wait_ge(vec_ready, 1)
            act.wait_ge(tg_ready, 1)
            keys1(0)
            norm_high(1, 0)
            keys1(1)
            norm_high(1, 1)
            values1(1, 1)
            values1(2, 0)
            for h in range(2):
                act.wait_ge(dl_ready, h + 1)
                act.activation(ed[:, tiles(h)], dl[:, tiles(h)], ACT.Exp).then_inc(ed_ready, 1)
            for h in range(2):
                act.wait_ge(ln_back[2], h + 1)
                act.activation(xnT[:, cols(h)], PS[:, 2 * h + 1, :], ACT.Copy).then_inc(ln_out[2], 1)
            for h in range(2):
                act.wait_ge(q1_ps, h + 1)
                act.activation(qT1[:, cols(h)], PS[0:DH, 4 + h, :], ACT.Identity, scale=QSCALE,
                               bias=bq_s[:, 0:1]).then_inc(q1_ready, 1)
            for h in range(2):
                act.wait_ge(max1_ready, h + 1)
                for j in range(HT):
                    t = h * HT + j
                    last = act.activation(E[:, t, :], SC[:, h, j // MT, (j % MT) * S:(j % MT + 1) * S],
                                          ACT.Exp, bias=neg_max[:, t:t + 1], accum_out=row_sum[:, t:t + 1])
                last.then_inc(exp1_ready, 1)
            for h in range(2):
                for m in range(MT):
                    act.wait_ge(pT1_ps, MT * h + m + 1)
                    act.activation(pT1[m][:, cols(h)], SC[:, h, m, :], ACT.Copy).then_inc(pT1_ready, 1)
            norm_high(3, 0)
            norm_high(3, 1)
            act.wait_ge(sh_ready, 1)
            act.activation(q1[:, :, :], q2[:, :, :], ACT.Exp).then_inc(ex_ready, 1)

            def expert_pair(i, first):
                for u in range(2 * NC):
                    s, c = u // NC, u % NC
                    n = 2 * NC * i + u + 1
                    if first and u == 2:
                        act.wait_ge(gT1_ps, 1)
                        act.activation(gT1[:, :], PS[0:NE, 6:8, :].rearrange("p a b -> p (a b)"),
                                       ACT.Copy).then_inc(gT1_ready, 1)
                    act.wait_ge(w1_ps, n)
                    if not (first and u < NH):
                        act.wait_ge(h_used, n - NH)
                    hid = PS[:, 2 * (u % 2):2 * (u % 2) + 2, :].rearrange("p a b -> p (a b)")
                    act.activation(hh[u % NH][:, :], hid, ACT.Gelu, bias=b1s[s][:, c:c + 1]).then_inc(hh_ready, 1)
                    act.activation(hid, hid, ACT.Gelu, bias=b1s[s][:, c:c + 1]).then_inc(gelu_ready, 1)

            expert_pair(0, True)
            with act.Fori(1, NE // 2) as i:
                expert_pair(i, False)

        @block.vector
        def _(dve):
            steps = [0]

            def link(ins):
                steps[0] += 1
                ins.then_inc(dve_step, 1)
                dve.wait_ge(dve_step, steps[0])

            def ln_stats(k, h):
                for j in range(HT):
                    last = dve.bn_stats(st[:, k, h * HT + j, :], x_tok[:, h * HT + j, :])
                link(last)
                for j in range(HT):
                    last = dve.bn_aggr(mv[:, k, h * HT + j, :], st[:, k, h * HT + j, :])
                link(last)
                dve.tensor_scalar_add(ve[:, k, tiles(h)], mv[:, k, tiles(h), 1], LN_EPS).then_inc(ln_var[k], 1)

            def ln_normalise(k, h):
                dve.wait_ge(ln_rstd[k], h + 1)
                for j in range(HT):
                    t = h * HT + j
                    last = dve.tensor_scalar(xn_tok[:, t, :], x_tok[:, t, :], mv[:, k, t, 0:1], rs[:, k, t:t + 1],
                                             ALU.subtract, ALU.mult)
                last.then_inc(ln_norm[k], 1)

            def norm_low(k, h, n):
                dve.wait_ge(xh_ready, n)
                dve.tensor_tensor(xl[:, cols(h)], PS[:, 2 * h + 1, :], xh[:, cols(h)].bitcast(f32),
                                  ALU.subtract).then_inc(xl_ready, 1)

            dve.wait_ge(ld_x, 16)
            ln_stats(0, 0)
            ln_stats(0, 1)
            ln_normalise(0, 0)
            dve.wait_ge(css_ready, 1)
            dve.tensor_scalar(cse[:, :], css[:, :], 1.0 / D, RMS_EPS, ALU.mult, ALU.add).then_inc(cse_ready, 1)
            ln_normalise(0, 1)
            dve.wait_ge(vecA_ps, 1)
            dve.tensor_copy(vec_a[:, :], PS[:, HN_, 0:NROW_A]).then_inc(vecA_ready, 1)
            dve.wait_ge(vecA_ready, 1)
            dve.wait_ge(mq_ps, 1)
            dve.tensor_scalar(mq[:, :], PS[:, R_, 0:D], vec_a[:, R_IW:R_IW + 1], SCALE,
                              ALU.mult, ALU.mult).then_inc(mq_ready, 1)
            dve.wait_ge(crs_ready, 1)
            for h in range(2):
                dve.tensor_tensor(pn_tok[:, tiles(h), :], c_tok[:, tiles(h), :],
                                  crs[:, tiles(h)].rearrange("p (t a) -> p t a", a=1).to_broadcast([P, HT, D]),
                                  ALU.mult).then_inc(pn_ready, 1)
            link(dve.tensor_tensor(b_sum[:, :], vec_a[:, R_BIH:R_BIH + 2], vec_a[:, R_BHH:R_BHH + 2], ALU.add))
            dve.tensor_scalar_mul(b_gate[:, :], b_sum[:, :], 0.5).then_inc(bias_ready, 1)

            def slot_ms(n, h):
                dve.wait_ge(ms_ps, n)
                dve.tensor_scalar(mse[:, tiles(h)], SC[:, h, 0, 0:HT], 1.0 / D, RMS_EPS,
                                  ALU.mult, ALU.add).then_inc(mse_ready, 1)

            def slot_norm(n, h):
                dve.wait_ge(rb_ps, n)
                dve.tensor_tensor(sn[:, cols(h)], SC[:, h, 1, :], slots[:, cols(h)], ALU.mult).then_inc(sn_ready, 1)

            slot_ms(1, 0)
            slot_norm(1, 0)
            dve.wait_ge(gxw_ps, 1)
            dve.tensor_scalar(gxw[:, :], PS[:, R_, 0:G3 * D], vec_a[:, R_IW:R_IW + 1], None,
                              ALU.mult).then_inc(gxw_ready, 1)

            LOOP_STEPS = 2 * 7
            def slot_trip(it):
                k = [0]

                def loop_link(ins):
                    k[0] += 1
                    ins.then_inc(dve_loop, 1)
                    dve.wait_ge(dve_loop, LOOP_STEPS * it + k[0])

                def slot_max(n, h):
                    dve.wait_ge(score_ps, n)
                    dve.tensor_reduce(neg_max[:, tiles(h)], SC[:, h, :, :].rearrange("p b (m k) -> p (b m) k", m=MT),
                                      AX_X, ALU.max, negate=True).then_inc(max_ready, 1)

                def slot_values(n, h):
                    dve.wait_ge(exp_ready, n)
                    loop_link(dve.reciprocal(row_inv[:, tiles(h)], row_sum[:, tiles(h)]))
                    inv = row_inv[:, tiles(h)].rearrange("p (t a) -> p t a", a=1)
                    dve.tensor_copy(pv[:, tiles(h), D:D + 1], inv)
                    dve.tensor_tensor(pv[:, tiles(h), 0:D], pn_tok[:, tiles(h), :],
                                      inv.to_broadcast([P, HT, D]), ALU.mult).then_inc(pv_ready, 1)

                def scale_updates(n, h):
                    dve.wait_ge(upd_ps, n)
                    u = SC[:, h, :, 0:MT * (D + 1)].rearrange("p b (t c) -> p b t c", c=D + 1)
                    s_u = su[:, tiles(h)].rearrange("p (b t a) -> p b t a", b=BH, a=1)
                    loop_link(dve.tensor_scalar_add(s_u, u[:, :, :, D:D + 1], RMS_EPS))
                    loop_link(dve.reciprocal(siv[:, tiles(h)], su[:, tiles(h)]))
                    dve.tensor_tensor(upd_tok[:, tiles(h), :].rearrange("p (b t) d -> p b t d", b=BH),
                                      u[:, :, :, 0:D],
                                      siv[:, tiles(h)].rearrange("p (b t a) -> p b t a", b=BH, a=1)
                                      .to_broadcast([P, BH, MT, D]), ALU.mult).then_inc(upd_tok_ready, 1)

                def candidate(n, h):
                    c = cols(h)
                    dve.wait_ge(tr_ready, n)
                    loop_link(dve.tensor_scalar(rg[:, c], tr[:, c], 0.5, 0.5, ALU.mult, ALU.add))
                    dve.wait_ge(gn_ps, n)
                    loop_link(dve.scalar_tensor_tensor(t1[:, c], PS[:, HN_, :], vec_a[:, R_BHH + 2:R_BHH + 3],
                                                       rg[:, c], ALU.add, ALU.mult))
                    dve.tensor_tensor(t2[:, c], PS[:, XN_, :], t1[:, c], ALU.add).then_inc(cand_in, 1)

                def new_slots(n, h):
                    c = cols(h)
                    dve.wait_ge(cand_ready, n)
                    loop_link(dve.tensor_tensor(dd[:, c], slots[:, c], nn[:, c], ALU.subtract))
                    loop_link(dve.scalar_tensor_tensor(t1[:, c], tz[:, c], 1.0, dd[:, c], ALU.add, ALU.mult))
                    dve.scalar_tensor_tensor(slots[:, c], t1[:, c], 0.5, nn[:, c],
                                             ALU.mult, ALU.add).then_inc(slots_ready, 1)

                slot_max(2 * it + 1, 0)
                slot_values(2 * it + 1, 0)
                slot_ms(2 * it + 2, 1)
                scale_updates(2 * it + 1, 0)
                slot_norm(2 * it + 2, 1)
                slot_max(2 * it + 2, 1)
                slot_values(2 * it + 2, 1)
                candidate(2 * it + 1, 0)
                new_slots(2 * it + 1, 0)
                scale_updates(2 * it + 2, 1)
                slot_ms(2 * it + 3, 0)
                slot_norm(2 * it + 3, 0)
                candidate(2 * it + 2, 1)
                new_slots(2 * it + 2, 1)
                assert k[0] == LOOP_STEPS

            slot_trip(0)
            with dve.Fori(1, ITERS) as it:
                slot_trip(it)

            dve.wait_ge(tg_ready, 1)
            for h in range(2):
                dve.wait_ge(slotsT_ps, h + 1)
                link(dve.scalar_tensor_tensor(x_tok[:, tiles(h), :], tiled(PS[:, 2 * h, :]), tg[:, 0:1],
                                              x_tok[:, tiles(h), :], ALU.mult, ALU.add))
                ln_stats(1, h)
            dve.wait_ge(vecT, 1)
            dve.tensor_copy(vec[:, :], PS[:, 7, 0:NROW]).then_inc(vec_ready, 1)
            ln_normalise(1, 0)
            ln_normalise(1, 1)
            dve.wait_ge(vec_ready, 1)
            link(dve.tensor_copy(gwh[:, :], vec[:, R_GW:R_GW + NE]))
            dve.tensor_scalar_mul(bq_s[:, :], vec[0:DH, R_BQ:R_BQ + 1], QSCALE)
            dve.tensor_tensor(gwl[:, :], vec[:, R_GW:R_GW + NE], gwh[:, :].bitcast(f32), ALU.subtract).then_inc(gw_split, 1)
            norm_low(1, 0, 1)
            norm_low(1, 1, 2)
            dve.wait_ge(ob_ps, 1)
            dve.wait_ge(ld_bc, 32)
            link(dve.tensor_tensor(bias_row[:, :], PS[:, 4, 0:D], bo_bc[:, :], ALU.add))
            dve.tensor_scalar(out_bias[:, :], bias_row[:, :], tg[:, 1:2], None, ALU.mult).then_inc(ob_ready, 1)

            def per_tile(ap, h):
                return ap[:, tiles(h)].rearrange("p (t a) -> p t a", a=1).to_broadcast([P, HT, NE])

            iota_t = iota8[:, :].rearrange("p (a e) -> p a e", a=1).to_broadcast([P, HT, NE])
            for h in range(2):
                t = tiles(h)
                dve.wait_ge(lg0_ps, h + 1)
                link(dve.tensor_copy(lg[:, t, :], PS[:, 2 * h, 0:HT * NE].rearrange("p (t e) -> p t e", t=HT)))
                for j in range(HT):
                    last = dve.max(m8[:, h * HT + j, :], lg[:, h * HT + j, :])
                link(last)
                dve.tensor_tensor(dl[:, t], m8[:, t, 1], m8[:, t, 0], ALU.subtract).then_inc(dl_ready, 1)
                for j in range(HT):
                    last = dve.max_index(ix[:, h * HT + j, :], m8[:, h * HT + j, :], lg[:, h * HT + j, :])
                link(last)
                link(dve.tensor_copy(ixf[:, t, :], ix[:, t, :]))
                dve.tensor_tensor(q1[:, t, :], iota_t, ixf[:, t, 0:1].to_broadcast([P, HT, NE]), ALU.is_equal)
                dve.tensor_tensor(q2[:, t, :], iota_t, ixf[:, t, 1:2].to_broadcast([P, HT, NE]), ALU.is_equal)
                dve.wait_ge(ed_ready, h + 1)
                link(dve.tensor_scalar_add(den[:, t], ed[:, t], 1.0))
                link(dve.reciprocal(wa[:, t], den[:, t]))
                link(dve.tensor_scalar(wag[:, t], wa[:, t], tg[:, 2:3], None, ALU.mult))
                link(dve.tensor_tensor(wbg[:, t], ed[:, t], wag[:, t], ALU.mult))
                dve.tensor_tensor(q1[:, t, :], q1[:, t, :], per_tile(wag, h), ALU.mult)
                link(dve.tensor_tensor(q2[:, t, :], q2[:, t, :], per_tile(wbg, h), ALU.mult))
                dve.tensor_tensor(gw0[:, t, :], q1[:, t, :], q2[:, t, :], ALU.add).then_inc(gw0_ready, 1)
            k = 0
            for t in range(NT):
                dve.wait_ge(y0_ps, t + 1)
                bank = 4 + 2 * (t % 2)
                for e in range(NE):
                    y = PS[:, bank + e // HT, (e % HT) * D:(e % HT + 1) * D]
                    w = gw0[:, t, e:e + 1]
                    if e == 1:
                        last = dve.tensor_scalar(odd_acc[:, t, :], y, w, None, ALU.mult)
                    else:
                        if e > 1:
                            dve.wait_ge(y0_sum, k - 1)
                        a = odd_acc if e % 2 else x_tok
                        last = dve.scalar_tensor_tensor(a[:, t, :], y, w, a[:, t, :], ALU.mult, ALU.add)
                    last.then_inc(y0_sum, 1)
                    k += 1
                dve.wait_ge(y0_sum, k)
                dve.tensor_tensor(x_tok[:, t, :], x_tok[:, t, :], odd_acc[:, t, :], ALU.add).then_inc(y0_read, 1)

            for h in range(2):
                dve.wait_ge(y0_read, HT * (h + 1))
                ln_stats(2, h)
            for h in range(2):
                ln_normalise(2, h)
            for h in range(2):
                dve.wait_ge(s1_ps, h + 1)
                dve.tensor_reduce(neg_max[:, tiles(h)], SC[:, h, :, :].rearrange("p b (m k) -> p (b m) k", m=MT),
                                  AX_X, ALU.max, negate=True).then_inc(max1_ready, 1)
            for h in range(2):
                dve.wait_ge(exp1_ready, h + 1)
                link(dve.reciprocal(row_inv[:, tiles(h)], row_sum[:, tiles(h)]))
                for j in range(HT):
                    t = h * HT + j
                    last = dve.tensor_scalar(E[:, t, :], E[:, t, :], row_inv[:, t:t + 1], None, ALU.mult)
                last.then_inc(p1_ready, 1)
            dve.wait_ge(bias_added, 1)
            for h in range(2):
                dve.wait_ge(o1_ps, h + 1)
                link(dve.tensor_tensor(x_tok[:, tiles(h), :], tiled(PS[:, 6 + h, :]), x_tok[:, tiles(h), :], ALU.add))
                ln_stats(3, h)

            for h in range(2):
                ln_normalise(3, h)
            norm_low(3, 0, 3)
            norm_low(3, 1, 4)
            dve.wait_ge(lg1_ps, 1)
            dve.wait_ge(ld_bc, 32)
            link(dve.tensor_tensor(lg[:, :, :], PS[:, 4, 0:NT * NE].rearrange("p (t e) -> p t e", t=NT),
                                   br_bc[:, :].rearrange("p (a e) -> p a e", a=1).to_broadcast([P, NT, NE]), ALU.add))
            for t in range(NT):
                last = dve.max(m8[:, t, :], lg[:, t, :])
            link(last)
            dve.tensor_tensor(q2[:, :, :], lg[:, :, :], m8[:, :, 0:1].to_broadcast([P, NT, NE]),
                              ALU.subtract).then_inc(sh_ready, 1)
            link(dve.tensor_tensor(gw1[:, :, :], lg[:, :, :], m8[:, :, 1:2].to_broadcast([P, NT, NE]), ALU.is_ge))
            dve.wait_ge(ex_ready, 1)
            link(dve.tensor_tensor(q1[:, :, :], q1[:, :, :], gw1[:, :, :], ALU.mult))
            link(dve.reduce_sum(den[:, :], q1[:, :, :], AX_X))
            link(dve.reciprocal(wa[:, :], den[:, :]))
            link(dve.tensor_scalar(wag[:, :], wa[:, :], tg[:, 3:4], None, ALU.mult))
            dve.tensor_tensor(gw1[:, :, :], q1[:, :, :],
                              wag[:, :].rearrange("p (t a) -> p t a", a=1).to_broadcast([P, NT, NE]),
                              ALU.mult).then_inc(gw1_ready, 1)

            def gate_output(n, s, h, first=False):
                y = PS[:, 4 + 2 * s + h, :]
                dst = acc if first else ygated
                dve.scalar_tensor_tensor(dst[:, cols(h)], y, b2s[s][:, 0:1], wbc[s][:, cols(h)],
                                         ALU.add, ALU.mult).then_inc(y1_gated, 1)
                if not first:
                    dve.wait_ge(y1_gated, 2 * n - 1 + h)
                    dve.tensor_tensor(acc[:, cols(h)], acc[:, cols(h)], ygated[:, cols(h)],
                                      ALU.add).then_inc(y1_added, 1)

            def expert_pair(i, first):
                for u in range(2 * NC):
                    s, c = u // NC, u % NC
                    n = 2 * NC * i + u + 1
                    dve.wait_ge(gelu_ready, n)
                    dve.tensor_tensor(hl[u % NH][:, :], PS[:, 2 * (u % 2):2 * (u % 2) + 2, :].rearrange("p a b -> p (a b)"),
                                      hh[u % NH][:, :].bitcast(f32), ALU.subtract).then_inc(hl_ready, 1)
                    if c in (1, 2) and not (first and s == 0):
                        if c == 1:
                            dve.wait_ge(h_used, NC * (2 * i + s))
                            dve.wait_ge(ld_gates[1 - s], 16 * i + 16 * s)
                        gate_output(2 * i + s, 1 - s, c - 1, first)

            expert_pair(0, True)
            with dve.Fori(1, NE // 2) as i:
                expert_pair(i, False)
            dve.wait_ge(h_used, NC * NE)
            dve.wait_ge(ld_gates[1], 16 * (NE // 2))
            gate_output(NE, 1, 0)
            gate_output(NE, 1, 1)
            for h in range(2):
                dve.wait_ge(oT_ps, h + 1)
                dve.tensor_tensor(o_tok[:, tiles(h), :], tiled(PS[:, h, :]), x_tok[:, tiles(h), :],
                                  ALU.add).then_inc(o_ready, 1)

        @block.tensor
        def _(pe):
            def transposes(bank, src, h):
                for j in range(HT):
                    last = pe.transpose(bank[:, j * P:(j + 1) * P], src(h * HT + j), ident[:, :])
                return last

            pe.wait_ge(id_ready, 1)
            pe.wait_ge(ld_qkv0, 32)
            pe.matmul(PS[:, R_, 0:D], wk0[:, :], wq0[:, :], start=True, stop=True).then_inc(mq_ps, 1)
            pe.wait_ge(ld_rows_a, 16 * len(row_loads_a))
            pe.transpose(PS[:, HN_, 0:NROW_A], rows_a[:, :], ident[0:NROW_A, 0:NROW_A]).then_inc(vecA_ps, 1)
            for h in range(2):
                pe.wait_ge(ln_norm[0], h + 1)
                transposes(PS[:, 2 * h, :], lambda t: xn_tok[:, t, :], h).then_inc(ln_back[0], 1)
            for h in range(2):
                pe.wait_ge(pn_ready, h + 1)
                transposes(PS[:, 2 * h + 1, :], lambda t: pn_tok[:, t, :], h).then_inc(pnT_ps, 1)

            def slot_ms(n, h):
                pe.wait_ge(sq_ready, n)
                for j in range(HT):
                    t = h * HT + j
                    last = pe.matmul(SC[:, h, 0, j:j + 1], sq[:, t * P:(t + 1) * P], ones[:, :], start=True, stop=True)
                last.then_inc(ms_ps, 1)

            def slot_rstd_rows(n, h):
                pe.wait_ge(rst_ready, n)
                for j in range(HT):
                    t = h * HT + j
                    last = pe.transpose(SC[:, h, 1, j * P:(j + 1) * P], rst[:, t:t + 1].to_broadcast([P, P]), ident[:, :])
                last.then_inc(rb_ps, 1)

            slot_ms(1, 0)
            pe.wait_ge(ld_gru, 32)
            for n, (bank, w) in enumerate(((XN_, whh), (Z_, wih))):
                for g in range(G3):
                    last = pe.transpose(PS[:, bank, g * D:(g + 1) * D], w[:, g, :], ident[:, :])
                last.then_inc(wT_ps, 1)
            pe.wait_ge(pnT_ready, 1)
            slot_rstd_rows(1, 0)
            pe.wait_ge(mq_ready, 1)
            pe.wait_ge(vecA_ready, 1)
            for h, bank in ((0, HN_), (1, R_)):
                pe.wait_ge(pnT_ready, h + 1)
                pe.matmul(PS[:, bank, :], mq[:, :], pnT[:, cols(h)], start=True, stop=True).then_inc(kq_ps, 1)
            pe.wait_ge(kq_ready, 2)
            pe.wait_ge(wT_ready, 2)
            pe.wait_ge(ld_wv0, 16)
            pe.matmul(PS[:, R_, 0:G3 * D], wv0[:, :], wihT[:, :], start=True, stop=True).then_inc(gxw_ps, 1)

            def slot_scores(n, h):
                pe.wait_ge(sn_ready, n)
                for j in range(HT):
                    t = h * HT + j
                    b = t // MT
                    last = pe.matmul(SC[:, h, j // MT, (j % MT) * S:(j % MT + 1) * S], kqT[:, t * P:(t + 1) * P],
                                     sn[:, b * S:(b + 1) * S], start=True, stop=True)
                last.then_inc(score_ps, 1)

            def slot_updates(n, h):
                pe.wait_ge(pv_ready, n)
                for b in range(BH):
                    for kt in range(MT):
                        for m in range(MT):
                            t = h * HT + b * MT + m
                            last = pe.matmul(SC[:, h, b, kt * (D + 1):(kt + 1) * (D + 1)],
                                             E[:, t, kt * P:(kt + 1) * P], pv[:, t, :],
                                             start=(m == 0), stop=(m == MT - 1))
                last.then_inc(upd_ps, 1)

            def updates_to_columns(n, h):
                pe.wait_ge(upd_tok_ready, n)
                pe.wait_ge(cand_in, n - 1)
                transposes(PS[:, XN_, :], lambda t: upd_tok[:, t, :], h).then_inc(updT_ps, 1)

            def state_gates(n, h, gates):
                c = cols(h)
                if R_ in gates:
                    pe.wait_ge(slots_ready, n)
                    pe.wait_ge(tr_ready, n - 1)
                    pe.matmul(PS[:, R_, :], whhT[:, 0:D], slots[:, c], start=True, stop=False)
                if Z_ in gates:
                    pe.wait_ge(tz_ready, n - 1)
                    pe.matmul(PS[:, Z_, :], whhT[:, D:2 * D], slots[:, c], start=True, stop=False)
                if HN_ in gates:
                    pe.wait_ge(cand_in, n - 1)
                    pe.matmul(PS[:, HN_, :], whhT[:, 2 * D:3 * D], slots[:, c], start=True, stop=True)

            def update_reset(n, h):
                pe.wait_ge(updT_ready, n)
                pe.matmul(PS[:, R_, :], gxw[:, 0:D], updT[:, cols(h)], start=False, stop=True).then_inc(gr_ps, 1)

            def update_rest(n, h):
                c = cols(h)
                pe.matmul(PS[:, XN_, :], gxw[:, 2 * D:3 * D], updT[:, c], start=True, stop=True).then_inc(gn_ps, 1)
                pe.matmul(PS[:, Z_, :], gxw[:, D:2 * D], updT[:, c], start=False, stop=True).then_inc(gz_ps, 1)

            def slot_trip(it):
                slot_scores(2 * it + 1, 0)
                if isinstance(it, int):
                    pe.wait_ge(gxw_ready, 1)
                state_gates(2 * it + 1, 0, (R_, Z_, HN_))
                slot_ms(2 * it + 2, 1)
                slot_updates(2 * it + 1, 0)
                slot_rstd_rows(2 * it + 2, 1)
                updates_to_columns(2 * it + 1, 0)
                slot_scores(2 * it + 2, 1)
                update_reset(2 * it + 1, 0)
                update_rest(2 * it + 1, 0)
                slot_updates(2 * it + 2, 1)
                state_gates(2 * it + 2, 1, (R_, Z_))
                updates_to_columns(2 * it + 2, 1)
                state_gates(2 * it + 2, 1, (HN_,))
                slot_ms(2 * it + 3, 0)
                update_reset(2 * it + 2, 1)
                slot_rstd_rows(2 * it + 3, 0)
                update_rest(2 * it + 2, 1)

            slot_trip(0)
            with pe.Fori(1, ITERS) as it:
                slot_trip(it)

            for h in range(2):
                pe.wait_ge(slots_ready, 2 * ITERS + h + 1)
                transposes(PS[:, 2 * h, :], lambda t: slots[:, t * P:(t + 1) * P], h).then_inc(slotsT_ps, 1)

            pe.wait_ge(ld_rows, 16 * len(row_loads))
            pe.transpose(PS[:, 7, 0:NROW], rows[:, :], ident[0:NROW, 0:NROW]).then_inc(vecT, 1)
            transposes(PS[:, 4, :], lambda t: c_tok[:, t, :], 0).then_inc(ctxT_ps, 1)
            transposes(PS[:, 5, :], lambda t: c_tok[:, t, :], 1).then_inc(ctxT_ps, 1)
            pe.wait_ge(ld_a1, 64)
            pe.transpose(PS[0:DH, 6, 0:D], wv1[:, :], ident[:, :]).then_inc(wv1T_ps, 1)
            pe.wait_ge(vec_ready, 1)
            pe.wait_ge(wv1T_ready, 1)
            pe.wait_ge(wos_step, 4)
            pe.matmul(PS[:, 7, 0:D], wv1T[:, :], wo1[:, 0, :], start=True, stop=True).then_inc(wvo_ps, 1)
            pe.matmul(PS[0:DH, 6, :], wk1[:, :], ctxT[:, cols(0)], start=True, stop=True).then_inc(kT1_ps, 1)
            pe.matmul(PS[:, 4, 0:D], vec[0:DH, R_BV:R_BV + 1].to_broadcast([DH, P]), wo1[:, 0, :],
                      start=True, stop=True).then_inc(ob_ps, 1)

            def tokens_to_columns(k, h):
                pe.wait_ge(ln_norm[k], h + 1)
                transposes(PS[:, 2 * h + 1, :], lambda t: xn_tok[:, t, :], h).then_inc(ln_back[k], 1)

            def exact_product(bank, x_parts, w_parts):
                (xhi, xlo), (whi, wlo) = x_parts, w_parts
                pe.matmul(bank, xhi, whi, start=True, stop=False)
                pe.matmul(bank, xhi, wlo, start=False, stop=False)
                return pe.matmul(bank, xlo, whi, start=False, stop=True)

            tokens_to_columns(1, 0)
            pe.wait_ge(wvo_ready, 1)
            pe.matmul(PS[0:DH, 7, :], wk1[:, :], ctxT[:, cols(1)], start=True, stop=True).then_inc(kT1_ps, 1)
            tokens_to_columns(1, 1)
            for h in (1, 0):
                if h == 0:
                    pe.wait_ge(ob_ready, 1)
                for j in range(HT):
                    t = h * HT + j
                    last = pe.matmul(PS[:, 4 + h, j * P:(j + 1) * P], ctxT[:, t * P:(t + 1) * P], wvo[:, :],
                                     start=True, stop=True)
                last.then_inc(vo1_ps, 1)

            pe.wait_ge(gw_split, 1)
            for h in range(2):
                pe.wait_ge(xl_ready, h + 1)
                for j in range(HT):
                    c = slice((h * HT + j) * P, (h * HT + j + 1) * P)
                    last = exact_product(PS[:, 2 * h, j * NE:(j + 1) * NE], (xh[:, c], xl[:, c]), (gwh[:, :], gwl[:, :]))
                last.then_inc(lg0_ps, 1)
            pe.wait_ge(we0_ready, 2)
            pe.wait_ge(vo1_ready, 2)
            pe.wait_ge(kT1_ready, 2)
            for t in range(NT):
                c = slice(t * P, (t + 1) * P)
                bank = 4 + 2 * (t % 2)
                if t >= 2:
                    pe.wait_ge(y0_read, t - 1)
                for x, w, start, stop in ((xh, we0h, True, False), (xh, we0l, False, False), (xl, we0h, False, True)):
                    for g in range(2):
                        last = pe.matmul(PS[:, bank + g, :], x[:, c], w[:, g * HT:(g + 1) * HT, :].rearrange("p e m -> p (e m)"),
                                         start=start, stop=stop)
                last.then_inc(y0_ps, 1)

            for h in range(2):
                tokens_to_columns(2, h)
            for h in range(2):
                pe.wait_ge(ln_out[2], h + 1)
                pe.matmul(PS[0:DH, 4 + h, :], wq1[:, :], xnT[:, cols(h)], start=True, stop=True).then_inc(q1_ps, 1)
            for h in range(2):
                pe.wait_ge(q1_ready, h + 1)
                for j in range(HT):
                    t = h * HT + j
                    b = t // MT
                    last = pe.matmul(SC[:, h, j // MT, (j % MT) * S:(j % MT + 1) * S], qT1[:, t * P:(t + 1) * P],
                                     kT1[:, b * S:(b + 1) * S], start=True, stop=True)
                last.then_inc(s1_ps, 1)
            for h in range(2):
                pe.wait_ge(p1_ready, h + 1)
                for m in range(MT):
                    for j in range(HT):
                        last = pe.transpose(SC[:, h, m, j * P:(j + 1) * P], E[:, h * HT + j, m * P:(m + 1) * P],
                                            ident[:, :])
                    last.then_inc(pT1_ps, 1)
            for h in range(2):
                pe.wait_ge(pT1_ready, MT * (h + 1))
                for j in range(HT):
                    t = h * HT + j
                    b = t // MT
                    for m in range(MT):
                        last = pe.matmul(PS[:, 6 + h, j * P:(j + 1) * P], pT1[m][:, t * P:(t + 1) * P],
                                         vo1[:, b * MT + m, :], start=(m == 0), stop=(m == MT - 1))
                last.then_inc(o1_ps, 1)

            for h in range(2):
                tokens_to_columns(3, h)

            def router_logits():
                pe.wait_ge(xl_ready, 4)
                for t in range(NT):
                    c = slice(t * P, (t + 1) * P)
                    last = exact_product(PS[:, 4, t * NE:(t + 1) * NE], (xh[:, c], xl[:, c]), (wrh[:, :], wrl[:, :]))
                last.then_inc(lg1_ps, 1)

            def gate_columns():
                pe.wait_ge(gw1_ready, 1)
                for t in range(NT):
                    last = pe.transpose(PS[0:NE, 6 + t // HT, (t % HT) * P:(t % HT + 1) * P], gw1[:, t, :], ident[:, :])
                last.then_inc(gT1_ps, 1)

            def up(i, u):
                s, c = (u // NC) % 2, u % NC
                k = slice(c * P, (c + 1) * P)
                if c == 0:
                    pe.wait_ge(w1_ready, 2 * i + u // NC + 1)
                if not (isinstance(i, int) and 2 * NC * i + u < 2):
                    pe.wait_ge(hl_ready, 2 * NC * i + u - 1)
                for w, x, start, stop in ((w1h, xh, True, False), (w1h, xl, False, False), (w1l, xh, False, True)):
                    for h in range(2):
                        last = pe.matmul(PS[:, 2 * (u % 2) + h, :], w[s][:, k], x[:, cols(h)], start=start, stop=stop)
                last.then_inc(w1_ps, 1)

            def down(i, u):
                s, c = u // NC, u % NC
                pe.wait_ge(hl_ready, 2 * NC * i + u + 1)
                if c == 0:
                    pe.wait_ge(w_ready, 4 * i + 2 * s + 2)
                    if isinstance(i, int) and i == 0:
                        if s == 1:
                            pe.wait_ge(gT1_ready, 1)
                    else:
                        pe.wait_ge(y1_gated, 4 * i + 2 * s - 2)
                for w, x, start, stop in ((w2h, hh, c == 0, False), (w2h, hl, False, False), (w2l, hh, False, c == NC - 1)):
                    for h in range(2):
                        last = pe.matmul(PS[:, 4 + 2 * s + h, :], w[s][:, c, :], x[u % NH][:, cols(h)],
                                         start=start, stop=stop)
                last.then_inc(h_used, 1)

            LAG = 2

            def expert_pair(i, last_pair):
                for u in range(2 * NC):
                    if u + LAG < 2 * NC or not last_pair:
                        up(i, u + LAG)
                    down(i, u)

            pe.wait_ge(xl_ready, 4)
            up(0, 0)
            router_logits()
            up(0, 1)
            gate_columns()
            pe.wait_ge(sh_ready, 1)
            expert_pair(0, False)
            with pe.Fori(1, NE // 2 - 1) as i:
                expert_pair(i, False)
            expert_pair(NE // 2 - 1, True)

            for h in range(2):
                pe.wait_ge(y1_added, 2 * (NE - 1) - 1 + h)
                transposes(PS[:, h, :], lambda t: acc[:, t * P:(t + 1) * P], h).then_inc(oT_ps, 1)


_INS = ["x", "ctx_1024", "g_xattn", "g_ffn", "L0_xattn_Wq", "L0_xattn_Wk", "L0_xattn_Wv",
        "L0_xattn_gru_wih", "L0_xattn_gru_whh", "L0_xattn_gru_bih", "L0_xattn_gru_bhh",
        "L0_xattn_slot_norm_w", "L0_xattn_input_norm_w", "L0_ffn_gate_w", "L0_ffn_We",
        "L1_xattn_Wq", "L1_xattn_bq", "L1_xattn_Wk", "L1_xattn_bk", "L1_xattn_Wv", "L1_xattn_bv",
        "L1_xattn_Wo", "L1_xattn_bo", "L1_ffn_W1", "L1_ffn_b1", "L1_ffn_W2", "L1_ffn_b2",
        "L1_ffn_Wr", "L1_ffn_br"]


def kernel(**inputs):
    import numpy as _np
    import concourse.bacc as _bacc
    from concourse import mybir as _mybir
    from concourse.bass_utils import run_bass_kernel_spmd as _run

    nc = _bacc.Bacc("TRN2", target_bir_lowering=False, num_devices=1)
    arrays, args = {}, []
    for name in _INS:
        a = _np.ascontiguousarray(inputs[name])
        arrays[f"in_{name}"] = a
        args.append(nc.dram_tensor(f"in_{name}", a.shape, _mybir.dt.from_np(a.dtype), kind="ExternalInput").ap())
    shape = arrays["in_x"].shape
    args.append(nc.dram_tensor("out_x", shape, _mybir.dt.float32, kind="ExternalOutput").ap())
    flamingo_gated_two_layer_kernel(nc, *args)
    r = _run(nc, [arrays], core_ids=[0])
    return r.results[0]["out_x"]
```

```python
import concourse.bass as bass
from concourse import mybir
from contextlib import ExitStack


def flamingo_gated_two_layer_kernel(
    nc: bass.Bass,
    x_in: bass.AP, ctx_in: bass.AP, g_xattn: bass.AP, g_ffn: bass.AP,
    a0_Wq: bass.AP, a0_Wk: bass.AP, a0_Wv: bass.AP,
    gru_wih: bass.AP, gru_whh: bass.AP, gru_bih: bass.AP, gru_bhh: bass.AP,
    slot_norm_w: bass.AP, input_norm_w: bass.AP,
    f0_gate_w: bass.AP, f0_We: bass.AP,
    a1_Wq: bass.AP, a1_bq: bass.AP, a1_Wk: bass.AP, a1_bk: bass.AP,
    a1_Wv: bass.AP, a1_bv: bass.AP, a1_Wo: bass.AP, a1_bo: bass.AP,
    f1_W1: bass.AP, f1_b1: bass.AP, f1_W2: bass.AP, f1_b2: bass.AP,
    f1_Wr: bass.AP, f1_br: bass.AP,
    out: bass.AP,
):
    f32 = mybir.dt.float32
    f32r = mybir.dt.float32r
    u32 = mybir.dt.uint32
    ALU = mybir.AluOpType
    ACT = mybir.ActivationFunctionType
    AX_X = mybir.AxisListType.X

    B, S, D = x_in.shape
    T = B * S
    P = 128
    NT = T // P
    HT = NT // 2
    HW = HT * P
    BH = B // 2
    MT = S // P
    G3 = 3
    NE = f0_We.shape[0]
    DH = a1_Wq.shape[1]
    NHEAD = a1_Wo.shape[0] // DH
    HID = f1_W1.shape[2]
    NC = HID // P
    ITERS = 3
    SCALE = float(D) ** -0.5
    QSCALE = float(DH) ** -0.5
    RMS_EPS, LN_EPS = 1e-6, 1e-5

    R_BIH, R_BHH, R_SW, R_IW = 0, 3, 6, 7
    NROW_A = 8
    R_BQ, R_BK, R_BV, R_B1 = 0, 1, 2, 3
    R_B2 = R_B1 + NE * NC
    R_GW = R_B2 + NE
    NROW = R_GW + NE

    x_v = x_in.rearrange("b (t p) d -> p (b t) d", p=P)
    ctx_v = ctx_in.rearrange("b (t p) d -> p (b t) d", p=P)
    out_v = out.rearrange("b (t p) d -> p (b t) d", p=P)
    W1_v = f1_W1.rearrange("e d h -> d e h")
    W2_v = f1_W2.rearrange("e (c p) d -> p e c d", p=P)

    ctx = ExitStack()
    with ctx:
        def sb(name, shape, dt=f32):
            return ctx.enter_context(nc.sbuf_tensor(name, shape, dt))

        def sem(name):
            return ctx.enter_context(nc.semaphore(name))

        ident = sb("ident", [P, P])
        neg_half = sb("neg_half", [P, NT])
        ones = sb("ones", [P, 1])
        inv_d = sb("inv_d", [P, 1])
        iota8 = sb("iota8", [P, NE])
        rows_a = sb("rows_a", [NROW_A, P])
        vec_a = sb("vec_a", [P, NROW_A])
        rows = sb("rows", [NROW, P])
        vec = sb("vec", [P, NROW])
        g_raw = sb("g_raw", [P, 4])
        tg = sb("tg", [P, 4])
        br_col = sb("br_col", [NE, 1])
        b_gate = sb("b_gate", [P, 2])
        b_sum = sb("b_sum", [P, 2])
        b_hn = sb("b_hn", [P, 1])
        bq_s = sb("bq_s", [DH, 1])
        bo_bc = sb("bo_bc", [P, D])
        bias_row = sb("bias_row", [P, D])
        out_bias = sb("out_bias", [P, D])

        x_tok = sb("x_tok", [P, NT, D])
        c_tok = sb("c_tok", [P, NT, D])
        pn_tok = sb("pn_tok", [P, NT, D])
        pnT = sb("pnT", [P, T])
        kqT = sb("kqT", [P, T])
        wq0 = sb("wq0", [P, D])
        wk0 = sb("wk0", [P, D])
        wv0 = sb("wv0", [P, D])
        wih = sb("wih", [P, G3, D])
        whh = sb("whh", [P, G3, D])
        mq = sb("mq", [P, D])
        wihT = sb("wihT", [P, G3 * D])
        whhT = sb("whhT", [P, G3 * D])
        gxw = sb("gxw", [P, G3 * D])
        wq1 = sb("wq1", [P, DH])
        wk1 = sb("wk1", [P, DH])
        wv1 = sb("wv1", [P, DH])
        wT1 = sb("wT1", [DH, 2, D])
        wo1 = sb("wo1", [DH, NHEAD, D])
        wvo = sb("wvo", [P, D])
        we0 = sb("we0", [P, NE, D])
        we0h = sb("we0h", [P, NE, D], f32r)
        we0l = sb("we0l", [P, NE, D], f32r)
        gwh = sb("gwh", [P, NE], f32r)
        gwl = sb("gwl", [P, NE], f32r)
        wrh = sb("wrh", [P, NE], f32r)
        wrl = sb("wrl", [P, NE], f32r)
        wr1 = sb("wr1", [P, NE])

        st = sb("st", [P, 4, NT, 6])
        mv = sb("mv", [P, 4, NT, 2])
        ve = sb("ve", [P, 4, NT])
        rs = sb("rs", [P, 4, NT])
        nmr = sb("nmr", [P, HT])
        css = sb("css", [P, NT])
        cse = sb("cse", [P, NT])
        crs = sb("crs", [P, NT])

        slots = sb("slots", [P, T])
        sq = sb("sq", [P, T])
        sn = sb("sn", [P, T])
        mse = sb("mse", [P, NT])
        rst = sb("rst", [P, NT])
        neg_max = sb("neg_max", [P, NT])
        row_sum = sb("row_sum", [P, NT])
        row_inv = sb("row_inv", [P, NT])
        E = sb("E", [P, NT, S])
        pv = sb("pv", [P, NT, D + 1])
        su = sb("su", [P, NT])
        siv = sb("siv", [P, NT])
        upd_tok = sb("upd_tok", [P, NT, D])
        updT = sb("updT", [P, T])
        tr = sb("tr", [P, T])
        tz = sb("tz", [P, T])
        hn_zg = sb("hn_zg", [P, 2, T])
        hn = hn_zg[:, 0, :]
        zg = hn_zg[:, 1, :]
        zs = sb("zs", [P, T])
        t1 = sb("t1", [P, T])
        t2 = sb("t2", [P, T])
        nn = sb("nn", [P, T])

        xn_tok = sb("xn_tok", [P, NT, D])
        xnT = sn
        ctxT = pnT
        kT1 = nn[0:DH, :]
        kq1 = tr
        vo1 = updT[:, :].rearrange("p (t d) -> p t d", t=NT)
        pT1 = hn_zg
        ys = kqT[:, :].rearrange("p (r e d) -> p r e d", r=2, e=HT)
        ypair = t2[:, 0:HW].rearrange("p (r e d) -> p r e d", r=2, e=2)
        ysum = zs[:, :].rearrange("p (t d) -> p t d", t=NT)
        acc = t1
        odd_acc = sb("odd_acc", [P, NT, D])
        lg = sb("lg", [P, NT, NE])
        m8 = sb("m8", [P, NT, 8])
        ix = sb("ix", [P, NT, 8], u32)
        ixf = sb("ixf", [P, NT, 8])
        dl = sb("dl", [P, NT])
        ed = sb("ed", [P, NT])
        den = sb("den", [P, NT])
        wa = sb("wa", [P, NT])
        wag = sb("wag", [P, NT])
        wbg = sb("wbg", [P, NT])
        q1 = sb("q1", [P, NT, NE])
        q2 = sb("q2", [P, NT, NE])
        gw0 = sb("gw0", [P, NT, NE])
        gw1 = sb("gw1", [P, NT, NE])
        gT1 = sb("gT1", [NE, T])
        xh = sb("xh", [P, T], f32r)
        xl = sb("xl", [P, T], f32r)
        w1r = [sb(f"w1r{s}", [P, HID]) for s in range(2)]
        w2r = [sb(f"w2r{s}", [P, NC, D]) for s in range(2)]
        w1h = [sb(f"w1h{s}", [P, HID], f32r) for s in range(2)]
        w1l = [sb(f"w1l{s}", [P, HID], f32r) for s in range(2)]
        w2h = [sb(f"w2h{s}", [P, NC, D], f32r) for s in range(2)]
        w2l = [sb(f"w2l{s}", [P, NC, D], f32r) for s in range(2)]
        b1s = [sb(f"b1s{s}", [P, NC]) for s in range(2)]
        b2s = [sb(f"b2s{s}", [P, 1]) for s in range(2)]
        wbc = [tr, tz]
        NH = 4
        hh = [sb(f"hh{s}", [P, T], f32r) for s in range(NH)]
        hl = [sb(f"hl{s}", [P, T], f32r) for s in range(NH)]
        ygated = t2
        o_tok = upd_tok

        PS = ctx.enter_context(nc.psum_tensor("PS", [P, 8, 512], f32))
        SC = PS[:, 0:4, :].rearrange("p (h b) c -> p h b c", h=2)
        R_, Z_, XN_, HN_ = 4, 5, 6, 7
        gates_dram = nc.dram_tensor("gates_dram", [NE, T], f32, kind="Internal").ap()

        ld_wv0 = sem("ld_wv0")
        ld_x, ld_c, ld_rows, ld_gate = [sem("ld_x0"), sem("ld_x1")], sem("ld_c"), sem("ld_rows"), sem("ld_gate")
        ld_qkv0, ld_gru, ld_a1, ld_f0 = sem("ld_qkv0"), sem("ld_gru"), sem("ld_a1"), sem("ld_f0")
        ld_ffn = [sem("ld_ffn0"), sem("ld_ffn1")]
        ld_rows_a, ld_bc, ld_gates, gates_stored = sem("ld_rows_a"), sem("ld_bc"), [sem("ld_gates0"), sem("ld_gates1")], sem("gates_stored")
        rows_clear, id_clear, id_ready, consts = sem("rows_clear"), sem("id_clear"), sem("id_ready"), sem("consts")
        stored = sem("stored")
        vecA_ps, vecA_ready = sem("vecA_ps"), sem("vecA_ready")
        vecT, vec_ready, tg_ready, bias_ready = sem("vecT"), sem("vec_ready"), sem("tg_ready"), sem("bias_ready")
        we0_high, we0_ready = sem("we0_high"), sem("we0_ready")
        gw_high = sem("gw_high")
        slotsT_ps, gw_split, xh_ready, xl_ready = (sem(n) for n in ("slotsT_ps", "gw_split", "xh_ready", "xl_ready"))
        mq_ps, mq_ready, wT_ps, wT_ready, gxw_ps, gxw_ready = (sem(n) for n in (
            "mq_ps", "mq_ready", "wT_ps", "wT_ready", "gxw_ps", "gxw_ready"))
        css_ready, cse_ready, crs_ready, pn_ready = sem("css_ready"), sem("cse_ready"), sem("crs_ready"), sem("pn_ready")
        pnT_ps, pnT_ready, kq_ps, kq_ready = sem("pnT_ps"), sem("pnT_ready"), sem("kq_ps"), sem("kq_ready")
        wos_step, gT1_ps, gT1_ready = sem("wos_step"), sem("gT1_ps"), sem("gT1_ready")
        wv1T_ps, wv1T_ready, wvo_ps, wvo_ready = sem("wv1T_ps"), sem("wv1T_ready"), sem("wvo_ps"), sem("wvo_ready")
        ctxT_ps, ctxT_ready, kT1_ps, kT1_ready = sem("ctxT_ps"), sem("ctxT_ready"), sem("kT1_ps"), sem("kT1_ready")
        vo1_ps, vo1_ready, ob_ps, ob_ready = sem("vo1_ps"), sem("vo1_ready"), sem("ob_ps"), sem("ob_ready")
        ln_var = [sem(f"ln_var{k}") for k in range(4)]
        ln_rstd = [sem(f"ln_rstd{k}") for k in range(4)]
        ln_norm = [sem(f"ln_norm{k}") for k in range(4)]
        ln_back = [sem(f"ln_back{k}") for k in range(4)]
        columns_ready = sem("columns_ready")
        slots_ready, sq_ready, ms_ps, mse_ready, rst_ready, rb_ps, sn_ready = (sem(n) for n in (
            "slots_ready", "sq_ready", "ms_ps", "mse_ready", "rst_ready", "rb_ps", "sn_ready"))
        score_ps, max_ready, exp_ready, pv_ready, upd_ps, upd_tok_ready, updT_ps, updT_ready = (sem(n) for n in (
            "score_ps", "max_ready", "exp_ready", "pv_ready", "upd_ps", "upd_tok_ready", "updT_ps", "updT_ready"))
        gr_ps, gn_ps, gz_ps, tr_ready, tz_ready, cand_in, cand_ready = (sem(n) for n in (
            "gr_ps", "gn_ps", "gz_ps", "tr_ready", "tz_ready", "cand_in", "cand_ready"))
        ghn_ps, cand_state = sem("ghn_ps"), sem("cand_state")
        hn_ready, zg_ready = sem("hn_ready"), sem("zg_ready")
        dve_step, dve_loop = sem("dve_step"), sem("dve_loop")
        lg0_ps, dl_ready, ed_ready, gw0_ready, y0_ps, y0_sum = (sem(n) for n in (
            "lg0_ps", "dl_ready", "ed_ready", "gw0_ready", "y0_ps", "y0_sum"))
        ys_ready, y0_pair, y0_four, y0_odd = (sem(n) for n in ("ys_ready", "y0_pair", "y0_four", "y0_odd"))
        kq1_ps, kq1_ready, s1_ps, max1_ready, exp1_ready, pT1_ps, pT1_ready, o1_ps = (sem(n) for n in (
            "kq1_ps", "kq1_ready", "s1_ps", "max1_ready", "exp1_ready", "pT1_ps", "pT1_ready", "o1_ps"))
        lgT_ps, lgT_ready = sem("lgT_ps"), sem("lgT_ready")
        mask_ready, lg1_ps, sh_ready, tanh_ready, gw1_ready = (sem(n) for n in (
            "mask_ready", "lg1_ps", "sh_ready", "tanh_ready", "gw1_ready"))
        w_high, w_ready, w1_ps, hh_ready, gelu_ready, hl_ready, h_used, w1_ready, w2_high, y1_gated, y1_added = (sem(n) for n in (
            "w_high", "w_ready", "w1_ps", "hh_ready", "gelu_ready", "hl_ready", "h_used", "w1_ready", "w2_high", "y1_gated", "y1_added"))
        b2_ready = sem("b2_ready")
        nmr_ready, norm_first, x_added = sem("nmr_ready"), sem("norm_first"), sem("x_added")
        oT_ps, o_ready = sem("oT_ps"), sem("o_ready")

        block = ctx.enter_context(nc.Block())

        RING = 3
        LAG = 2

        def y0_bank(t):
            return (4, 6, 2)[t % RING]

        def cols(h):
            return slice(h * HW, (h + 1) * HW)

        def tiles(h):
            return slice(h * HT, (h + 1) * HT)

        def tiled(ap, n=HT):
            return ap.rearrange("p (t d) -> p t d", t=n)

        def row(v):
            return v.rearrange("(a d) -> a d", a=1)

        row_loads_a = [
            (R_BIH, G3, gru_bih.rearrange("(g d) -> g d", d=P)),
            (R_BHH, G3, gru_bhh.rearrange("(g d) -> g d", d=P)),
            (R_SW, 1, row(slot_norm_w)),
            (R_IW, 1, row(input_norm_w)),
        ]
        row_loads = [
            (R_BQ, 1, row(a1_bq), DH),
            (R_BK, 1, row(a1_bk), DH),
            (R_BV, 1, row(a1_bv), DH),
            (R_B1, NE * NC, f1_b1.rearrange("e (c d) -> (e c) d", d=P), P),
            (R_B2, NE, f1_b2, P),
            (R_GW, NE, f0_gate_w, P),
        ]

        @block.sync
        def _(sp):
            for h in range(2):
                sp.dma_start(x_tok[:, tiles(h), :], x_v[:, tiles(h), :]).then_inc(ld_x[h], 16)
            sp.dma_start(c_tok[:, :, :], ctx_v).then_inc(ld_c, 16)
            sp.dma_start(wk0[:, :], a0_Wk).then_inc(ld_qkv0, 16)
            sp.dma_start(wq0[:, :], a0_Wq).then_inc(ld_qkv0, 16)
            for r, n, src in row_loads_a:
                sp.dma_start(rows_a[r:r + n, :], src).then_inc(ld_rows_a, 16)
            sp.dma_start(whh[:, :, :], gru_whh.rearrange("(g p) d -> p g d", p=P)).then_inc(ld_gru, 16)
            sp.dma_start(wih[:, :, :], gru_wih.rearrange("(g p) d -> p g d", p=P)).then_inc(ld_gru, 16)
            sp.dma_start(wv0[:, :], a0_Wv).then_inc(ld_wv0, 16)
            sp.dma_start(we0[:, :, :], f0_We.rearrange("e d m -> d e m")).then_inc(ld_f0, 16)
            sp.dma_start(wr1[:, :], f1_Wr).then_inc(ld_f0, 16)
            sp.wait_ge(rows_clear, 1)
            for r, n, src, w in row_loads:
                sp.dma_start(rows[r:r + n, 0:w], src).then_inc(ld_rows, 16)
            sp.dma_start(g_raw[:, 0:2], g_xattn.partition_broadcast(P)).then_inc(ld_gate, 16)
            sp.dma_start(g_raw[:, 2:4], g_ffn.partition_broadcast(P)).then_inc(ld_gate, 16)
            sp.dma_start(br_col[:, :], f1_br.rearrange("(e a) -> e a", a=1)).then_inc(ld_bc, 16)
            sp.dma_start(bo_bc[:, :], a1_bo.partition_broadcast(P)).then_inc(ld_bc, 16)
            sp.dma_start(wo1[:, :, :], a1_Wo.rearrange("(n p) d -> p n d", p=DH)).then_inc(ld_a1, 16)
            for dst, src in ((wq1, a1_Wq), (wk1, a1_Wk), (wv1, a1_Wv)):
                sp.dma_start(dst[:, :], src).then_inc(ld_a1, 16)
            def expert_matrices(i, s):
                e = slice(s, s + 1) if isinstance(i, int) and i == 0 else bass.ds(2 * i + s, 1)
                if not (isinstance(i, int) and i == 0):
                    sp.wait_ge(w_ready, 4 * i + 2 * s - 2)
                sp.dma_start(w1r[s][:, :], W1_v[:, e, :]).then_inc(ld_ffn[s], 16)
                sp.dma_start(w2r[s][:, :, :], W2_v[:, e, :, :]).then_inc(ld_ffn[s], 16)

            def expert_gates(i, s):
                if not (isinstance(i, int) and i == 0):
                    sp.wait_ge(y1_gated, 4 * i + 2 * s - 2)
                sp.dma_start(wbc[s][:, :], gates_dram[bass.ds(2 * i + s, 1), :].rearrange("a t -> (a t)")
                             .partition_broadcast(P)).then_inc(ld_gates[s], 16)

            for i in range(2):
                for s in range(2):
                    expert_matrices(i, s)
            sp.wait_ge(gT1_ready, 1)
            sp.dma_start(gates_dram, gT1[:, :]).then_inc(gates_stored, 16)
            sp.wait_ge(gates_stored, 16)
            for s in range(2):
                expert_gates(0, s)
            with sp.Fori(1, NE // 2 - 1) as i:
                for s in range(2):
                    expert_gates(i, s)
                    expert_matrices(i + 1, s)
            for s in range(2):
                expert_gates(NE // 2 - 1, s)
            for h in range(2):
                sp.wait_ge(o_ready, h + 1)
                sp.dma_start(out_v[:, tiles(h), :], o_tok[:, tiles(h), :]).then_inc(stored, 16)
            sp.wait_ge(stored, 32)

        @block.gpsimd
        def _(pool):
            pool.memset(rows[:, :], 0.0).then_inc(rows_clear, 1)
            pool.memset(ident[:, :], 0.0).then_inc(id_clear, 1)
            pool.memset(ones[:, :], 1.0)
            pool.memset(inv_d[:, :], 1.0 / D)
            pool.memset(neg_half[:, :], -0.5).then_inc(consts, 1)
            pool.wait_ge(id_clear, 1)
            pool.affine_select(out=ident[:, :], in_=ident[:, :], compare_op=ALU.not_equal, fill=1.0,
                               base=0, pattern=[[-1, P]], channel_multiplier=1).then_inc(id_ready, 1)
            pool.iota(iota8[:, :], pattern=[[1, NE]], base=0, channel_multiplier=0,
                      allow_small_or_imprecise_dtypes=True).then_inc(consts, 1)
            pool.wait_ge(consts, 2)
            for h in range(2):
                pool.wait_ge(ln_var[0], h + 1)
                pool.tensor_tensor(rs[:, 0, tiles(h)], ve[:, 0, tiles(h)], neg_half[:, 0:HT],
                                   ALU.pow).then_inc(ln_rstd[0], 1)
            for h in range(2):
                pool.wait_ge(cse_ready, h + 1)
                pool.tensor_tensor(crs[:, tiles(h)], cse[:, tiles(h)], neg_half[:, 0:HT], ALU.pow).then_inc(crs_ready, 1)

            def slot_rstd(n, h):
                pool.wait_ge(mse_ready, n)
                pool.tensor_tensor(rst[:, tiles(h)], mse[:, tiles(h)], neg_half[:, 0:HT],
                                   ALU.pow).then_inc(rst_ready, 1)

            slot_rstd(1, 0)
            pool.wait_ge(ld_f0, 32)
            pool.tensor_copy(we0h[:, :, :], we0[:, :, :]).then_inc(we0_high, 1)
            pool.tensor_copy(wrh[:, :], wr1[:, :]).then_inc(we0_high, 1)
            pool.wait_ge(we0_high, 2)
            pool.tensor_tensor(we0l[:, :, :], we0[:, :, :], we0h[:, :, :].bitcast(f32), ALU.subtract).then_inc(we0_ready, 1)
            pool.tensor_tensor(wrl[:, :], wr1[:, :], wrh[:, :].bitcast(f32), ALU.subtract).then_inc(we0_ready, 1)

            def slot_trip(it):
                slot_rstd(2 * it + 2, 1)
                slot_rstd(2 * it + 3, 0)

            slot_rstd(2, 1)
            pool.wait_ge(ld_a1, 64)
            n, k = NHEAD, 0
            while n > 1:
                n //= 2
                k += 1
                pool.tensor_tensor(wo1[:, 0:n, :], wo1[:, 0:n, :], wo1[:, n:2 * n, :], ALU.add).then_inc(wos_step, 1)
                pool.wait_ge(wos_step, k)
            slot_rstd(3, 0)
            with pool.Fori(1, ITERS) as it:
                slot_trip(it)

            def token_rstd(k, h):
                pool.wait_ge(ln_var[k], h + 1)
                pool.tensor_tensor(rs[:, k, tiles(h)], ve[:, k, tiles(h)], neg_half[:, 0:HT],
                                   ALU.pow).then_inc(ln_rstd[k], 1)

            def split_weights(i, s, first):
                pool.wait_ge(ld_ffn[s], 32 * i + 32)
                if not first:
                    pool.wait_ge(w1_ps, NC * (2 * i + s - 1))
                    pool.wait_ge(gelu_ready, NC * (2 * i + s - 1))
                pool.tensor_tensor(w1h[s][:, :], w1r[s][:, :], ones[:, :].to_broadcast([P, HID]), ALU.mult).then_inc(w_high, 1)
                pool.tensor_copy(b1s[s][:, :], vec[:, bass.ds(R_B1 + NC * (2 * i + s), NC)]).then_inc(w_high, 1)
                pool.wait_ge(w_high, 2 * (2 * i + s) + 2)
                pool.tensor_tensor(w1l[s][:, :], w1r[s][:, :], w1h[s][:, :].bitcast(f32), ALU.subtract).then_inc(w1_ready, 1)
                if not first:
                    pool.wait_ge(h_used, NC * (2 * i + s - 1))
                pool.tensor_tensor(w2h[s][:, :, :], w2r[s][:, :, :],
                                   ones[:, :].rearrange("p (a b) -> p a b", a=1).to_broadcast([P, NC, D]), ALU.mult).then_inc(w2_high, 1)
                pool.wait_ge(w2_high, 2 * i + s + 1)
                pool.tensor_tensor(w2l[s][:, :, :], w2r[s][:, :, :], w2h[s][:, :, :].bitcast(f32), ALU.subtract).then_inc(w_ready, 2)

            def add_experts(t):
                k = t % 2
                pool.wait_ge(ys_ready, t + 1)
                pool.tensor_tensor(ypair[:, k, :, :], ys[:, k, 0:2, :], ys[:, k, 2:4, :], ALU.add).then_inc(y0_pair, 1)
                pool.wait_ge(y0_pair, t + 1)
                pool.tensor_tensor(ysum[:, t, :], ypair[:, k, 0, :], ypair[:, k, 1, :], ALU.add).then_inc(y0_four, 1)

            token_rstd(1, 0)
            token_rstd(1, 1)
            pool.wait_ge(vec_ready, 1)
            for s in range(2):
                pool.tensor_copy(b2s[s][:, :], vec[:, R_B2 + s:R_B2 + s + 1]).then_inc(b2_ready, 1)
            split_weights(0, 0, True)
            for t in range(NT):
                add_experts(t)
                if t == HT + 1:
                    token_rstd(2, 0)
            token_rstd(2, 1)
            split_weights(0, 1, True)
            token_rstd(3, 0)
            token_rstd(3, 1)
            with pool.Fori(1, NE // 2) as i:
                for s in range(2):
                    split_weights(i, s, False)

        @block.scalar
        def _(act):
            act.wait_ge(ld_c, 16)
            for t in range(NT):
                last = act.activation(updT[:, t * P:(t + 1) * P], c_tok[:, t, :], ACT.Square,
                                      accum_out=css[:, t:t + 1])
                if t % HT == HT - 1:
                    last.then_inc(css_ready, 1)
            act.wait_ge(ln_back[0], 1)
            act.activation(slots[:, cols(0)], PS[:, 0, :], ACT.Copy).then_inc(slots_ready, 1)
            act.wait_ge(slots_ready, 1)
            act.activation(sq[:, cols(0)], slots[:, cols(0)], ACT.Square).then_inc(sq_ready, 1)
            act.wait_ge(pnT_ps, 1)
            act.activation(pnT[:, cols(0)], PS[:, 1, :], ACT.Copy).then_inc(pnT_ready, 1)
            act.wait_ge(ln_back[0], 2)
            act.activation(slots[:, cols(1)], PS[:, 2, :], ACT.Copy).then_inc(slots_ready, 1)
            act.wait_ge(pnT_ps, 2)
            act.activation(pnT[:, cols(1)], PS[:, 3, :], ACT.Copy).then_inc(pnT_ready, 1)
            act.wait_ge(vecA_ready, 1)
            for h, bank in ((0, HN_), (1, R_)):
                act.wait_ge(kq_ps, h + 1)
                act.activation(kqT[:, cols(h)], PS[:, bank, :], ACT.Copy,
                               scale=vec_a[:, R_SW:R_SW + 1]).then_inc(kq_ready, 1)
            for n, (bank, dst) in enumerate(((Z_, wihT), (XN_, whhT))):
                act.wait_ge(wT_ps, n + 1)
                act.activation(dst[:, :], PS[:, bank, 0:G3 * D], ACT.Copy).then_inc(wT_ready, 1)

            def square_slots(n, h):
                act.wait_ge(slots_ready, n)
                act.activation(sq[:, cols(h)], slots[:, cols(h)], ACT.Square).then_inc(sq_ready, 1)

            def slot_exp(n, h, b):
                act.wait_ge(max_ready, 2 * n - 1 + b)
                for m in range(MT):
                    t = h * HT + b * MT + m
                    last = act.activation(E[:, t, :], SC[:, h, b, m * S:(m + 1) * S],
                                          ACT.Exp, bias=neg_max[:, t:t + 1], accum_out=row_sum[:, t:t + 1])
                last.then_inc(exp_ready, 1)

            def state_candidate(n, h):
                act.wait_ge(ghn_ps, n)
                act.activation(hn[:, cols(h)], PS[:, HN_, :], ACT.Identity, scale=0.5,
                               bias=b_hn[:, 0:1]).then_inc(hn_ready, 1)

            def copy_updates(n, h, b):
                c = slice(h * HW + b * S, h * HW + (b + 1) * S)
                act.wait_ge(updT_ps, 2 * n - 1 + b)
                act.activation(updT[:, c], SC[:, h, b, 0:S], ACT.Copy).then_inc(updT_ready, 1)

            def reset_gate(n, h):
                act.wait_ge(gr_ps, n)
                act.activation(tr[:, cols(h)], PS[:, R_, :], ACT.Tanh, scale=0.5,
                               bias=b_gate[:, 0:1]).then_inc(tr_ready, 1)

            def update_gate(n, h):
                act.wait_ge(gz_ps, n)
                act.activation(tz[:, cols(h)], PS[:, Z_, :], ACT.Tanh, scale=0.5,
                               bias=b_gate[:, 1:2]).then_inc(tz_ready, 1)
                act.wait_ge(tz_ready, n)
                act.activation(zg[:, cols(h)], tz[:, cols(h)], ACT.Copy, scale=0.5, bias=0.5).then_inc(zg_ready, 1)

            def candidate_tanh(n, h):
                act.wait_ge(cand_in, n)
                act.activation(nn[:, cols(h)], t2[:, cols(h)], ACT.Tanh,
                               bias=vec_a[:, R_BIH + 2:R_BIH + 3]).then_inc(cand_ready, 1)

            act.wait_ge(ld_gate, 32)
            act.activation(tg[:, :], g_raw[:, :], ACT.Tanh).then_inc(tg_ready, 1)
            act.wait_ge(bias_ready, 1)

            def slot_trip(it, first=False):
                a, b = 2 * it + 1, 2 * it + 2
                if not first:
                    state_candidate(a, 0)
                square_slots(b, 1)
                slot_exp(a, 0, 0)
                slot_exp(a, 0, 1)
                if first:
                    act.wait_ge(gxw_ps, 1)
                    act.activation(gxw[:, :], PS[:, XN_, 0:G3 * D], ACT.Copy,
                                   scale=vec_a[:, R_IW:R_IW + 1]).then_inc(gxw_ready, 1)
                    state_candidate(a, 0)
                state_candidate(b, 1)
                copy_updates(a, 0, 0)
                slot_exp(b, 1, 0)
                copy_updates(a, 0, 1)
                slot_exp(b, 1, 1)
                reset_gate(a, 0)
                update_gate(a, 0)
                copy_updates(b, 1, 0)
                candidate_tanh(a, 0)
                copy_updates(b, 1, 1)
                reset_gate(b, 1)
                square_slots(a + 2, 0)
                update_gate(b, 1)
                candidate_tanh(b, 1)

            slot_trip(0, True)
            with act.Fori(1, ITERS) as it:
                slot_trip(it)

            for h in range(2):
                act.wait_ge(ctxT_ps, h + 1)
                act.activation(ctxT[:, cols(h)], PS[:, 4 + h, :], ACT.Copy).then_inc(ctxT_ready, 1)
            act.wait_ge(vecT, 1)
            act.activation(vec[:, :], PS[:, 7, 0:NROW], ACT.Copy).then_inc(vec_ready, 1)
            act.wait_ge(wv1T_ps, 1)
            act.activation(wT1[:, :, :], PS[0:DH, 6, 0:2 * D].rearrange("p (w d) -> p w d", w=2),
                           ACT.Copy).then_inc(wv1T_ready, 1)
            act.wait_ge(vec_ready, 1)
            act.activation(gwh[:, :], vec[:, R_GW:R_GW + NE], ACT.Copy).then_inc(gw_high, 1)
            act.wait_ge(wvo_ps, 1)
            act.activation(wvo[:, :], PS[:, 7, 0:D], ACT.Copy).then_inc(wvo_ready, 1)
            for h in range(2):
                act.wait_ge(kT1_ps, h + 1)
                act.activation(kT1[:, cols(h)], PS[0:DH, 4 + h, :], ACT.Identity,
                               bias=vec[0:DH, R_BK:R_BK + 1]).then_inc(kT1_ready, 1)
            for h in range(2):
                act.wait_ge(kq1_ps, h + 1)
                act.activation(kq1[:, cols(h)], PS[:, 4 + h, :], ACT.Copy, scale=QSCALE).then_inc(kq1_ready, 1)

            def norm_high(k, h):
                act.wait_ge(ln_back[k], h + 1)
                act.activation(xh[:, cols(h)], PS[:, 2 * h + 1, :], ACT.Copy).then_inc(xh_ready, 1)

            norm_high(1, 0)
            norm_high(1, 1)
            act.wait_ge(dl_ready, 1)
            act.activation(ed[:, :], dl[:, :], ACT.Exp).then_inc(ed_ready, 1)
            act.wait_ge(gw0_ready, 1)
            for t in range(NT):
                act.wait_ge(y0_ps, 2 * t + 2)
                if t >= 2:
                    act.wait_ge(y0_pair, t - 1)
                for e in range(HT):
                    last = act.activation(ys[:, t % 2, e, :], PS[:, y0_bank(t) + 1, e * D:(e + 1) * D], ACT.Copy,
                                          scale=gw0[:, t, HT + e:HT + e + 1])
                last.then_inc(ys_ready, 1)

            def normalise_first(k, n):
                act.wait_ge(nmr_ready, n)
                for j in range(HT):
                    last = act.activation(xn_tok[:, j, :], x_tok[:, j, :], ACT.Identity, scale=rs[:, k, j:j + 1],
                                          bias=nmr[:, j:j + 1])
                last.then_inc(norm_first, 1)

            normalise_first(2, 1)

            def norm_columns(h):
                act.wait_ge(ln_back[2], h + 1)
                act.activation(xnT[:, cols(h)], PS[:, 4 + h, :], ACT.Copy).then_inc(columns_ready, 1)

            def exp1(h, b):
                act.wait_ge(max1_ready, BH * h + b + 1)
                for m in range(MT):
                    t = h * HT + b * MT + m
                    last = act.activation(E[:, t, :], SC[:, h, b, m * S:(m + 1) * S],
                                          ACT.Exp, bias=neg_max[:, t:t + 1], accum_out=row_sum[:, t:t + 1])
                last.then_inc(exp1_ready, 1)

            def weights_to_keys(h, b):
                act.wait_ge(pT1_ps, BH * h + b + 1)
                act.activation(pT1[:, :, h * HW + b * S:h * HW + (b + 1) * S],
                               SC[:, h, b, :].rearrange("p (m q) -> p m q", m=MT), ACT.Copy).then_inc(pT1_ready, 1)

            norm_columns(0)
            exp1(0, 0)
            norm_columns(1)
            exp1(0, 1)
            weights_to_keys(0, 0)
            exp1(1, 0)
            weights_to_keys(0, 1)
            exp1(1, 1)
            weights_to_keys(1, 0)
            weights_to_keys(1, 1)
            normalise_first(3, 2)
            norm_high(3, 0)
            norm_high(3, 1)

            def expert_pair(i, first):
                for u in range(2 * NC):
                    s, c = u // NC, u % NC
                    n = 2 * NC * i + u + 1
                    if first and u == 3:
                        act.wait_ge(sh_ready, 1)
                        act.activation(q1[:, :, :], q2[:, :, :], ACT.Tanh, scale=0.5).then_inc(tanh_ready, 1)
                    act.wait_ge(w1_ps, n)
                    if not (first and u < NH):
                        act.wait_ge(h_used, n - NH)
                    hid = PS[:, 2 * (u % 2):2 * (u % 2) + 2, :].rearrange("p a b -> p (a b)")
                    act.activation(hh[u % NH][:, :], hid, ACT.Gelu, bias=b1s[s][:, c:c + 1]).then_inc(hh_ready, 1)
                    act.activation(hid, hid, ACT.Gelu, bias=b1s[s][:, c:c + 1]).then_inc(gelu_ready, 1)

            expert_pair(0, True)
            with act.Fori(1, NE // 2) as i:
                expert_pair(i, False)

        @block.vector
        def _(dve):
            steps = [0]

            def link(ins):
                steps[0] += 1
                ins.then_inc(dve_step, 1)
                dve.wait_ge(dve_step, steps[0])

            def ln_parts(k, h):
                for j in range(HT):
                    last = dve.bn_stats(st[:, k, h * HT + j, :], x_tok[:, h * HT + j, :])
                link(last)

            def ln_mean_var(k, h):
                for j in range(HT):
                    last = dve.bn_aggr(mv[:, k, h * HT + j, :], st[:, k, h * HT + j, :])
                link(last)
                dve.tensor_scalar_add(ve[:, k, tiles(h)], mv[:, k, tiles(h), 1], LN_EPS).then_inc(ln_var[k], 1)

            def ln_stats(k, h):
                ln_parts(k, h)
                ln_mean_var(k, h)

            def ln_offset(k, n):
                dve.wait_ge(ln_rstd[k], 1)
                if n > 1:
                    dve.wait_ge(norm_first, n - 1)
                dve.scalar_tensor_tensor(nmr[:, :], mv[:, k, tiles(0), 0], -1.0, rs[:, k, tiles(0)],
                                         ALU.mult, ALU.mult).then_inc(nmr_ready, 1)

            def ln_normalise(k, h):
                dve.wait_ge(ln_rstd[k], h + 1)
                for j in range(HT):
                    t = h * HT + j
                    last = dve.tensor_scalar(xn_tok[:, t, :], x_tok[:, t, :], mv[:, k, t, 0:1], rs[:, k, t:t + 1],
                                             ALU.subtract, ALU.mult)
                last.then_inc(ln_norm[k], 1)

            def norm_low(k, h, n):
                dve.wait_ge(xh_ready, n)
                dve.tensor_tensor(xl[:, cols(h)], PS[:, 2 * h + 1, :], xh[:, cols(h)].bitcast(f32),
                                  ALU.subtract).then_inc(xl_ready, 1)

            dve.wait_ge(ld_x[0], 16)
            ln_stats(0, 0)
            dve.wait_ge(ld_x[1], 16)
            ln_stats(0, 1)

            def context_ms(h):
                dve.wait_ge(css_ready, h + 1)
                dve.tensor_scalar(cse[:, tiles(h)], css[:, tiles(h)], 1.0 / D, RMS_EPS,
                                  ALU.mult, ALU.add).then_inc(cse_ready, 1)

            context_ms(0)
            ln_normalise(0, 0)
            context_ms(1)
            ln_normalise(0, 1)
            dve.wait_ge(vecA_ps, 1)
            dve.tensor_copy(vec_a[:, :], PS[:, HN_, 0:NROW_A]).then_inc(vecA_ready, 1)
            dve.wait_ge(vecA_ready, 1)
            dve.wait_ge(mq_ps, 1)
            dve.tensor_scalar(mq[:, :], PS[:, R_, 0:D], vec_a[:, R_IW:R_IW + 1], SCALE,
                              ALU.mult, ALU.mult).then_inc(mq_ready, 1)
            for h in range(2):
                dve.wait_ge(crs_ready, h + 1)
                dve.tensor_tensor(pn_tok[:, tiles(h), :], c_tok[:, tiles(h), :],
                                  crs[:, tiles(h)].rearrange("p (t a) -> p t a", a=1).to_broadcast([P, HT, D]),
                                  ALU.mult).then_inc(pn_ready, 1)
            link(dve.tensor_tensor(b_sum[:, :], vec_a[:, R_BIH:R_BIH + 2], vec_a[:, R_BHH:R_BHH + 2], ALU.add))
            dve.tensor_scalar_mul(b_hn[:, :], vec_a[:, R_BHH + 2:R_BHH + 3], 0.5)
            dve.tensor_scalar_mul(b_gate[:, :], b_sum[:, :], 0.5).then_inc(bias_ready, 1)

            def slot_ms(n, h):
                dve.wait_ge(ms_ps, n)
                dve.tensor_scalar_add(mse[:, tiles(h)], SC[:, h, 0, 0:HT], RMS_EPS).then_inc(mse_ready, 1)

            def slot_norm(n, h):
                dve.wait_ge(rb_ps, n)
                dve.tensor_tensor(sn[:, cols(h)], SC[:, h, 1, :], slots[:, cols(h)], ALU.mult).then_inc(sn_ready, 1)

            slot_ms(1, 0)
            slot_norm(1, 0)

            LOOP_STEPS = 2 * 8

            def slot_trip(it, first=False):
                k = [0]

                def loop_link(ins):
                    k[0] += 1
                    ins.then_inc(dve_loop, 1)
                    dve.wait_ge(dve_loop, LOOP_STEPS * it + k[0])

                def batch(h, b):
                    return slice(h * HT + b * MT, h * HT + (b + 1) * MT)

                def slot_max(n, h, b):
                    dve.wait_ge(score_ps, 2 * n - 1 + b)
                    dve.tensor_reduce(neg_max[:, batch(h, b)], SC[:, h, b, :].rearrange("p (m k) -> p m k", m=MT),
                                      AX_X, ALU.max, negate=True).then_inc(max_ready, 1)

                def slot_values(n, h, b):
                    t = batch(h, b)
                    dve.wait_ge(exp_ready, 2 * n - 1 + b)
                    loop_link(dve.reciprocal(row_inv[:, t], row_sum[:, t]))
                    inv = row_inv[:, t].rearrange("p (t a) -> p t a", a=1)
                    dve.tensor_copy(pv[:, t, D:D + 1], inv)
                    dve.tensor_tensor(pv[:, t, 0:D], pn_tok[:, t, :], inv.to_broadcast([P, MT, D]),
                                      ALU.mult).then_inc(pv_ready, 1)

                def scale_updates(n, h, b):
                    t = batch(h, b)
                    dve.wait_ge(upd_ps, 2 * n - 1 + b)
                    u = SC[:, h, b, 0:MT * (D + 1)].rearrange("p (t c) -> p t c", c=D + 1)
                    loop_link(dve.tensor_scalar_add(su[:, t].rearrange("p (t a) -> p t a", a=1), u[:, :, D:D + 1], RMS_EPS))
                    loop_link(dve.reciprocal(siv[:, t], su[:, t]))
                    dve.tensor_tensor(upd_tok[:, t, :], u[:, :, 0:D],
                                      siv[:, t].rearrange("p (t a) -> p t a", a=1).to_broadcast([P, MT, D]),
                                      ALU.mult).then_inc(upd_tok_ready, 1)

                def candidate_state(n, h):
                    c = cols(h)
                    dve.wait_ge(tr_ready, n)
                    dve.wait_ge(hn_ready, n)
                    ins = dve.scalar_tensor_tensor(t1[:, c], tr[:, c], 1.0, hn[:, c], ALU.add, ALU.mult)
                    ins.then_inc(cand_state, 1)

                def candidate(n, h):
                    c = cols(h)
                    dve.wait_ge(gn_ps, n)
                    dve.wait_ge(cand_state, n)
                    dve.tensor_tensor(t2[:, c], PS[:, XN_, :], t1[:, c], ALU.add).then_inc(cand_in, 1)

                def keep_slots(n, h):
                    c = cols(h)
                    dve.wait_ge(zg_ready, n)
                    loop_link(dve.tensor_tensor(zs[:, c], zg[:, c], slots[:, c], ALU.mult))

                def new_slots(n, h):
                    c = cols(h)
                    dve.wait_ge(cand_ready, n)
                    loop_link(dve.scalar_tensor_tensor(t1[:, c], zg[:, c], 1.0, nn[:, c], ALU.subtract, ALU.mult))
                    dve.tensor_tensor(slots[:, c], zs[:, c], t1[:, c], ALU.subtract).then_inc(slots_ready, 1)

                a, b = 2 * it + 1, 2 * it + 2
                if not first:
                    slot_norm(a, 0)
                slot_max(a, 0, 0)
                slot_max(a, 0, 1)
                slot_values(a, 0, 0)
                slot_ms(b, 1)
                slot_values(a, 0, 1)
                slot_norm(b, 1)
                scale_updates(a, 0, 0)
                scale_updates(a, 0, 1)
                slot_max(b, 1, 0)
                slot_max(b, 1, 1)
                slot_values(b, 1, 0)
                slot_values(b, 1, 1)
                candidate_state(a, 0)
                scale_updates(b, 1, 0)
                scale_updates(b, 1, 1)
                candidate(a, 0)
                keep_slots(a, 0)
                new_slots(a, 0)
                candidate_state(b, 1)
                candidate(b, 1)
                slot_ms(a + 2, 0)
                keep_slots(b, 1)
                new_slots(b, 1)
                assert k[0] == LOOP_STEPS

            slot_trip(0, True)
            with dve.Fori(1, ITERS) as it:
                slot_trip(it)

            dve.wait_ge(tg_ready, 1)
            for h in range(2):
                dve.wait_ge(slotsT_ps, h + 1)
                link(dve.scalar_tensor_tensor(x_tok[:, tiles(h), :], tiled(PS[:, 2 * h, :]), tg[:, 0:1],
                                              x_tok[:, tiles(h), :], ALU.mult, ALU.add))
                ln_stats(1, h)
            ln_normalise(1, 0)
            ln_normalise(1, 1)
            dve.wait_ge(gw_high, 1)
            dve.tensor_scalar_mul(bq_s[:, :], vec[0:DH, R_BQ:R_BQ + 1], QSCALE)
            dve.tensor_tensor(gwl[:, :], vec[:, R_GW:R_GW + NE], gwh[:, :].bitcast(f32), ALU.subtract).then_inc(gw_split, 1)
            dve.wait_ge(ob_ps, 1)
            dve.wait_ge(ld_bc, 32)
            link(dve.tensor_tensor(bias_row[:, :], PS[:, 6, 0:D], bo_bc[:, :], ALU.add))
            dve.tensor_scalar(out_bias[:, :], bias_row[:, :], tg[:, 1:2], None, ALU.mult).then_inc(ob_ready, 1)
            norm_low(1, 0, 1)
            norm_low(1, 1, 2)
            for h in range(2):
                dve.wait_ge(vo1_ps, h + 1)
                dve.wait_ge(ob_ready, 1)
                dve.scalar_tensor_tensor(vo1[:, tiles(h), :], tiled(PS[:, 7 - h, :]), tg[:, 1:2],
                                         out_bias[:, :].rearrange("p (a d) -> p a d", a=1).to_broadcast([P, HT, D]),
                                         ALU.mult, ALU.add).then_inc(vo1_ready, 1)

            def over_experts(ap):
                return ap.rearrange("p (t a) -> p t a", a=1).to_broadcast([P, NT, NE])

            iota_t = iota8[:, :].rearrange("p (a e) -> p a e", a=1).to_broadcast([P, NT, NE])
            dve.wait_ge(lg0_ps, 1)
            link(dve.tensor_copy(lg[:, :, :], PS[:, 0, 0:NT * NE].rearrange("p (t e) -> p t e", t=NT)))
            for t in range(NT):
                last = dve.max(m8[:, t, :], lg[:, t, :])
            link(last)
            dve.tensor_tensor(dl[:, :], m8[:, :, 1], m8[:, :, 0], ALU.subtract).then_inc(dl_ready, 1)
            for t in range(NT):
                last = dve.max_index(ix[:, t, :], m8[:, t, :], lg[:, t, :])
            link(last)
            link(dve.tensor_copy(ixf[:, :, :], ix[:, :, :]))
            dve.tensor_tensor(q1[:, :, :], iota_t, ixf[:, :, 0:1].to_broadcast([P, NT, NE]), ALU.is_equal)
            dve.tensor_tensor(q2[:, :, :], iota_t, ixf[:, :, 1:2].to_broadcast([P, NT, NE]), ALU.is_equal)
            dve.wait_ge(ed_ready, 1)
            link(dve.tensor_scalar_add(den[:, :], ed[:, :], 1.0))
            link(dve.reciprocal(wa[:, :], den[:, :]))
            link(dve.tensor_scalar(wag[:, :], wa[:, :], tg[:, 2:3], None, ALU.mult))
            link(dve.tensor_tensor(wbg[:, :], ed[:, :], wag[:, :], ALU.mult))
            dve.tensor_tensor(q1[:, :, :], q1[:, :, :], over_experts(wag[:, :]), ALU.mult)
            link(dve.tensor_tensor(q2[:, :, :], q2[:, :, :], over_experts(wbg[:, :]), ALU.mult))
            dve.tensor_tensor(gw0[:, :, :], q1[:, :, :], q2[:, :, :], ALU.add).then_inc(gw0_ready, 1)
            dve.wait_ge(gw0_ready, 1)

            def first_experts(t):
                dve.wait_ge(y0_ps, 2 * t + 1)
                y = [PS[:, y0_bank(t), e * D:(e + 1) * D] for e in range(HT)]
                w = [gw0[:, t, e:e + 1] for e in range(HT)]
                dve.scalar_tensor_tensor(x_tok[:, t, :], y[0], w[0], x_tok[:, t, :], ALU.mult, ALU.add).then_inc(y0_sum, 1)
                dve.tensor_scalar(odd_acc[:, t, :], y[1], w[1], None, ALU.mult).then_inc(y0_sum, 1)
                dve.wait_ge(y0_sum, 3 * t + 1)
                dve.scalar_tensor_tensor(x_tok[:, t, :], y[2], w[2], x_tok[:, t, :], ALU.mult, ALU.add).then_inc(y0_sum, 1)
                dve.wait_ge(y0_sum, 3 * t + 2)
                dve.scalar_tensor_tensor(odd_acc[:, t, :], y[3], w[3], odd_acc[:, t, :], ALU.mult, ALU.add).then_inc(y0_odd, 1)

            def other_experts(t):
                two = slice(t, t + 2)
                dve.wait_ge(y0_odd, t + 2)
                dve.wait_ge(y0_sum, 3 * t + 6)
                link(dve.tensor_tensor(x_tok[:, two, :], x_tok[:, two, :], odd_acc[:, two, :], ALU.add))
                dve.wait_ge(y0_four, t + 2)
                return dve.tensor_tensor(x_tok[:, two, :], x_tok[:, two, :], ysum[:, two, :], ALU.add)

            first_experts(0)
            first_experts(1)
            first_experts(2)
            other_experts(0)
            first_experts(3)
            first_experts(4)
            link(other_experts(2))
            ln_stats(2, 0)
            first_experts(5)
            first_experts(6)
            ln_offset(2, 1)
            first_experts(7)
            other_experts(4)
            link(other_experts(6))
            ln_stats(2, 1)

            def max1(h, b):
                dve.wait_ge(s1_ps, BH * h + b + 1)
                t = h * HT + b * MT
                dve.tensor_reduce(neg_max[:, t:t + MT], SC[:, h, b, :].rearrange("p (m k) -> p m k", m=MT),
                                  AX_X, ALU.max, negate=True).then_inc(max1_ready, 1)

            def attention_sums(h):
                dve.wait_ge(exp1_ready, BH * (h + 1))
                link(dve.reciprocal(row_inv[:, tiles(h)], row_sum[:, tiles(h)]))

            def add_attention(h, b):
                dve.wait_ge(o1_ps, BH * h + b + 1)
                for j in range(MT):
                    t = h * HT + b * MT + j
                    last = dve.scalar_tensor_tensor(x_tok[:, t, :], PS[:, 4 + 2 * h + b, j * P:(j + 1) * P],
                                                    row_inv[:, t:t + 1], x_tok[:, t, :], ALU.mult, ALU.add)
                return last

            max1(0, 0)
            ln_normalise(2, 1)
            max1(0, 1)
            max1(1, 0)
            max1(1, 1)
            attention_sums(0)
            add_attention(0, 0)
            link(add_attention(0, 1))
            attention_sums(1)
            ln_parts(3, 0)
            ln_mean_var(3, 0)
            add_attention(1, 0)
            link(add_attention(1, 1))
            ln_offset(3, 2)
            ln_parts(3, 1)
            ln_mean_var(3, 1)
            ln_normalise(3, 1)
            norm_low(3, 0, 3)
            norm_low(3, 1, 4)

            def logits_out():
                dve.wait_ge(lgT_ps, 1)
                dve.wait_ge(ld_bc, 32)
                dve.tensor_scalar(gT1[:, :], PS[0:NE, 4:6, :].rearrange("p a b -> p (a b)"), br_col[:, 0:1], None,
                                  ALU.add).then_inc(lgT_ready, 1)

            def routing():
                dve.wait_ge(lg1_ps, 1)
                logits = PS[:, 6, 0:NT * NE].rearrange("p (t e) -> p t e", t=NT)
                for t in range(NT):
                    last = dve.max(m8[:, t, :], PS[:, 6, t * NE:(t + 1) * NE])
                link(last)
                dve.tensor_tensor(q2[:, :, :], logits, m8[:, :, 0:1].to_broadcast([P, NT, NE]),
                                  ALU.subtract).then_inc(sh_ready, 1)
                dve.tensor_tensor(gw1[:, :, :], logits, m8[:, :, 1:2].to_broadcast([P, NT, NE]),
                                  ALU.is_ge).then_inc(mask_ready, 1)

            def gates1():
                dve.wait_ge(tanh_ready, 1)
                dve.wait_ge(mask_ready, 1)
                link(dve.tensor_scalar(q2[:, :, :], q1[:, :, :], -1.0, 1.0, ALU.mult, ALU.add))
                dve.scalar_tensor_tensor(gw1[:, :, :], q1[:, :, :], 1.0, gw1[:, :, :], ALU.add, ALU.mult)
                link(dve.reciprocal(lg[:, :, :], q2[:, :, :]))
                link(dve.tensor_tensor(q1[:, :, :], gw1[:, :, :], lg[:, :, :], ALU.mult))
                link(dve.reduce_sum(den[:, :], q1[:, :, :], AX_X))
                link(dve.reciprocal(wa[:, :], den[:, :]))
                link(dve.tensor_scalar(wag[:, :], wa[:, :], tg[:, 3:4], None, ALU.mult))
                dve.tensor_tensor(gw1[:, :, :], q1[:, :, :], over_experts(wag[:, :]), ALU.mult).then_inc(gw1_ready, 1)

            def gate_output(n, s, h, dst=None):
                y = PS[:, 4 + 2 * s + h, :]
                out_cols = (ygated if dst is None else dst)[:, cols(h)]
                dve.scalar_tensor_tensor(out_cols, y, b2s[s][:, 0:1], wbc[s][:, cols(h)],
                                         ALU.add, ALU.mult).then_inc(y1_gated, 1)
                if dst is None:
                    dve.wait_ge(y1_gated, 2 * n - 1 + h)
                    dve.tensor_tensor(acc[:, cols(h)], acc[:, cols(h)], ygated[:, cols(h)],
                                      ALU.add).then_inc(y1_added, 1)

            def expert_pair(i, first):
                for u in range(2 * NC):
                    s, c = u // NC, u % NC
                    n = 2 * NC * i + u + 1
                    if first and u == 1:
                        logits_out()
                    if first and u == 2:
                        routing()
                    if first and u == 3:
                        gates1()
                    if first and u == 4:
                        dve.wait_ge(gT1_ps, 1)
                        dve.tensor_copy(gT1[:, :], PS[0:NE, 6:8, :].rearrange("p a b -> p (a b)")).then_inc(gT1_ready, 1)
                    dve.wait_ge(gelu_ready, n)
                    dve.tensor_tensor(hl[u % NH][:, :], PS[:, 2 * (u % 2):2 * (u % 2) + 2, :].rearrange("p a b -> p (a b)"),
                                      hh[u % NH][:, :].bitcast(f32), ALU.subtract).then_inc(hl_ready, 1)
                    c0 = 2 if first else 1
                    if c in (c0, c0 + 1) and not (first and s == 0):
                        if c == c0:
                            dve.wait_ge(h_used, NC * (2 * i + s))
                            dve.wait_ge(ld_gates[1 - s], 16 * i + 16 * s)
                            dve.wait_ge(b2_ready, 2 * i + s + 1)
                        gate_output(2 * i + s, 1 - s, c - c0, acc if first else None)
                        if c == c0 + 1:
                            dve.wait_ge(y1_gated, 4 * i + 2 * s)
                            dve.tensor_copy(b2s[1 - s][:, :], vec[:, bass.ds(R_B2 + 2 * i + s + 1, 1)]).then_inc(b2_ready, 1)

            expert_pair(0, True)
            with dve.Fori(1, NE // 2) as i:
                expert_pair(i, False)
            for h in range(2):
                dve.wait_ge(oT_ps, h + 1)
                dve.tensor_tensor(x_tok[:, tiles(h), :], tiled(PS[:, h, :]), x_tok[:, tiles(h), :],
                                  ALU.add).then_inc(x_added, 1)
            dve.wait_ge(h_used, NC * NE)
            dve.wait_ge(ld_gates[1], 16 * (NE // 2))
            dve.wait_ge(b2_ready, NE)
            gate_output(NE, 1, 0, ygated)
            gate_output(NE, 1, 1, ygated)
            for h in range(2):
                dve.wait_ge(oT_ps, 3 + h)
                dve.wait_ge(x_added, h + 1)
                dve.tensor_tensor(o_tok[:, tiles(h), :], tiled(PS[:, 2 + h, :]), x_tok[:, tiles(h), :],
                                  ALU.add).then_inc(o_ready, 1)

        @block.tensor
        def _(pe):
            def transposes(bank, src, h):
                for j in range(HT):
                    last = pe.transpose(bank[:, j * P:(j + 1) * P], src(h * HT + j), ident[:, :])
                return last

            pe.wait_ge(id_ready, 1)
            pe.wait_ge(ld_qkv0, 32)
            pe.matmul(PS[:, R_, 0:D], wk0[:, :], wq0[:, :], start=True, stop=True).then_inc(mq_ps, 1)
            pe.wait_ge(ld_rows_a, 16 * len(row_loads_a))
            pe.transpose(PS[:, HN_, 0:NROW_A], rows_a[:, :], ident[0:NROW_A, 0:NROW_A]).then_inc(vecA_ps, 1)

            def slots_to_columns(h):
                pe.wait_ge(ln_norm[0], h + 1)
                transposes(PS[:, 2 * h, :], lambda t: xn_tok[:, t, :], h).then_inc(ln_back[0], 1)

            def context_to_columns(h):
                pe.wait_ge(pn_ready, h + 1)
                transposes(PS[:, 2 * h + 1, :], lambda t: pn_tok[:, t, :], h).then_inc(pnT_ps, 1)

            def slot_keys(h, bank):
                pe.wait_ge(mq_ready, 1)
                pe.wait_ge(pnT_ready, h + 1)
                pe.matmul(PS[:, bank, :], mq[:, :], pnT[:, cols(h)], start=True, stop=True).then_inc(kq_ps, 1)

            def gru_transposes(bank, w):
                for g in range(G3):
                    last = pe.transpose(PS[:, bank, g * D:(g + 1) * D], w[:, g, :], ident[:, :])
                last.then_inc(wT_ps, 1)

            def slot_ms(n, h):
                pe.wait_ge(sq_ready, n)
                for j in range(HT):
                    t = h * HT + j
                    last = pe.matmul(SC[:, h, 0, j:j + 1], sq[:, t * P:(t + 1) * P], inv_d[:, :], start=True, stop=True)
                last.then_inc(ms_ps, 1)

            def slot_rstd_rows(n, h):
                pe.wait_ge(rst_ready, n)
                for j in range(HT):
                    t = h * HT + j
                    last = pe.transpose(SC[:, h, 1, j * P:(j + 1) * P], rst[:, t:t + 1].to_broadcast([P, P]), ident[:, :])
                last.then_inc(rb_ps, 1)

            slots_to_columns(0)
            slots_to_columns(1)
            context_to_columns(0)
            slot_ms(1, 0)
            context_to_columns(1)
            slot_keys(0, HN_)
            pe.wait_ge(pnT_ready, 1)
            slot_rstd_rows(1, 0)
            slot_keys(1, R_)
            pe.wait_ge(ld_gru, 32)
            gru_transposes(Z_, wih)
            gru_transposes(XN_, whh)

            def slot_scores(n, h, b):
                pe.wait_ge(sn_ready, n)
                for m in range(MT):
                    t = h * HT + b * MT + m
                    last = pe.matmul(SC[:, h, b, m * S:(m + 1) * S], kqT[:, t * P:(t + 1) * P],
                                     sn[:, h * HW + b * S:h * HW + (b + 1) * S], start=True, stop=True)
                last.then_inc(score_ps, 1)

            def slot_updates(n, h, b):
                pe.wait_ge(pv_ready, 2 * n - 1 + b)
                for kt in range(MT):
                    for m in range(MT):
                        t = h * HT + b * MT + m
                        last = pe.matmul(SC[:, h, b, kt * (D + 1):(kt + 1) * (D + 1)],
                                         E[:, t, kt * P:(kt + 1) * P], pv[:, t, :],
                                         start=(m == 0), stop=(m == MT - 1))
                last.then_inc(upd_ps, 1)

            def updates_to_columns(n, h, b):
                pe.wait_ge(upd_tok_ready, 2 * n - 1 + b)
                for m in range(MT):
                    last = pe.transpose(SC[:, h, b, m * P:(m + 1) * P], upd_tok[:, h * HT + b * MT + m, :], ident[:, :])
                last.then_inc(updT_ps, 1)

            def state_reset(n, h):
                pe.wait_ge(slots_ready, n)
                if not (isinstance(n, int) and n == 1):
                    pe.wait_ge(tr_ready, n - 1)
                pe.matmul(PS[:, R_, :], whhT[:, 0:D], slots[:, cols(h)], start=True, stop=False)

            def state_update(n, h):
                pe.wait_ge(slots_ready, n)
                if not (isinstance(n, int) and n == 1):
                    pe.wait_ge(tz_ready, n - 1)
                pe.matmul(PS[:, Z_, :], whhT[:, D:2 * D], slots[:, cols(h)], start=True, stop=False)

            def state_candidate(n, h):
                pe.wait_ge(slots_ready, n)
                if not (isinstance(n, int) and n == 1):
                    pe.wait_ge(hn_ready, n - 1)
                pe.matmul(PS[:, HN_, :], whhT[:, 2 * D:3 * D], slots[:, cols(h)], start=True, stop=True).then_inc(ghn_ps, 1)

            def update_reset(n, h):
                pe.wait_ge(updT_ready, 2 * n)
                pe.matmul(PS[:, R_, :], gxw[:, 0:D], updT[:, cols(h)], start=False, stop=True).then_inc(gr_ps, 1)

            def update_update(n, h):
                pe.matmul(PS[:, Z_, :], gxw[:, D:2 * D], updT[:, cols(h)], start=False, stop=True).then_inc(gz_ps, 1)

            def update_candidate(n, h):
                if not (isinstance(n, int) and n == 1):
                    pe.wait_ge(cand_in, n - 1)
                pe.matmul(PS[:, XN_, :], gxw[:, 2 * D:3 * D], updT[:, cols(h)], start=True, stop=True).then_inc(gn_ps, 1)

            def slot_trip(it, first=False):
                a, b = 2 * it + 1, 2 * it + 2
                if not first:
                    state_candidate(a, 0)
                    state_update(a, 0)
                    slot_rstd_rows(a, 0)
                    state_reset(a, 0)
                else:
                    pe.wait_ge(kq_ready, 1)
                slot_scores(a, 0, 0)
                slot_scores(a, 0, 1)
                slot_ms(b, 1)
                if first:
                    pe.wait_ge(kq_ready, 2)
                    pe.wait_ge(wT_ready, 2)
                    pe.wait_ge(ld_wv0, 16)
                    pe.matmul(PS[:, XN_, 0:G3 * D], wv0[:, :], wihT[:, :], start=True, stop=True).then_inc(gxw_ps, 1)
                    state_candidate(a, 0)
                    state_update(a, 0)
                    state_reset(a, 0)
                state_candidate(b, 1)
                slot_updates(a, 0, 0)
                slot_rstd_rows(b, 1)
                slot_updates(a, 0, 1)
                slot_scores(b, 1, 0)
                updates_to_columns(a, 0, 0)
                slot_scores(b, 1, 1)
                updates_to_columns(a, 0, 1)
                if first:
                    pe.wait_ge(gxw_ready, 1)
                update_reset(a, 0)
                slot_updates(b, 1, 0)
                update_update(a, 0)
                slot_updates(b, 1, 1)
                update_candidate(a, 0)
                updates_to_columns(b, 1, 0)
                state_reset(b, 1)
                updates_to_columns(b, 1, 1)
                state_update(b, 1)
                update_reset(b, 1)
                update_update(b, 1)
                update_candidate(b, 1)
                slot_ms(a + 2, 0)

            slot_trip(0, True)
            with pe.Fori(1, ITERS) as it:
                slot_trip(it)

            pe.wait_ge(ld_c, 16)
            pe.wait_ge(tr_ready, 2 * ITERS)
            transposes(PS[:, 4, :], lambda t: c_tok[:, t, :], 0).then_inc(ctxT_ps, 1)
            pe.wait_ge(tz_ready, 2 * ITERS)
            transposes(PS[:, 5, :], lambda t: c_tok[:, t, :], 1).then_inc(ctxT_ps, 1)
            pe.wait_ge(hn_ready, 2 * ITERS)
            pe.wait_ge(ld_rows, 16 * len(row_loads))
            pe.transpose(PS[:, 7, 0:NROW], rows[:, :], ident[0:NROW, 0:NROW]).then_inc(vecT, 1)
            pe.wait_ge(cand_in, 2 * ITERS)
            pe.wait_ge(ld_a1, 64)
            pe.transpose(PS[0:DH, 6, 0:D], wv1[:, :], ident[:, :])
            pe.transpose(PS[0:DH, 6, D:2 * D], wq1[:, :], ident[:, :]).then_inc(wv1T_ps, 1)

            def slots_to_tokens(h):
                pe.wait_ge(slots_ready, 2 * ITERS + h + 1)
                transposes(PS[:, 2 * h, :], lambda t: slots[:, t * P:(t + 1) * P], h).then_inc(slotsT_ps, 1)

            def keys1(h):
                pe.wait_ge(ctxT_ready, h + 1)
                pe.matmul(PS[0:DH, 4 + h, :], wk1[:, :], ctxT[:, cols(h)], start=True, stop=True).then_inc(kT1_ps, 1)

            def query_keys1(h):
                pe.wait_ge(kT1_ready, h + 1)
                pe.matmul(PS[:, 4 + h, :], wT1[:, 1, :], kT1[:, cols(h)], start=True, stop=True).then_inc(kq1_ps, 1)

            def values1(h):
                for j in range(HT):
                    t = h * HT + j
                    last = pe.matmul(PS[:, 7 - h, j * P:(j + 1) * P], ctxT[:, t * P:(t + 1) * P], wvo[:, :],
                                     start=True, stop=True)
                last.then_inc(vo1_ps, 1)

            def tokens_to_columns(k, h):
                if k >= 2:
                    pe.wait_ge(ln_norm[k] if h else norm_first, 1 if h else k - 1)
                else:
                    pe.wait_ge(ln_norm[k], h + 1)
                transposes(PS[:, 4 + h if k == 2 else 2 * h + 1, :], lambda t: xn_tok[:, t, :], h).then_inc(ln_back[k], 1)

            def exact_product(bank, x_parts, w_parts):
                (xhi, xlo), (whi, wlo) = x_parts, w_parts
                pe.matmul(bank, xhi, whi, start=True, stop=False)
                pe.matmul(bank, xhi, wlo, start=False, stop=False)
                return pe.matmul(bank, xlo, whi, start=False, stop=True)

            pe.wait_ge(mse_ready, 2 * ITERS + 1)
            slots_to_tokens(0)
            pe.wait_ge(vec_ready, 1)
            pe.wait_ge(wv1T_ready, 1)
            pe.wait_ge(wos_step, 4)
            pe.matmul(PS[:, 7, 0:D], wT1[:, 0, :], wo1[:, 0, :], start=True, stop=True).then_inc(wvo_ps, 1)
            pe.matmul(PS[:, 6, 0:D], vec[0:DH, R_BV:R_BV + 1].to_broadcast([DH, P]), wo1[:, 0, :],
                      start=True, stop=True).then_inc(ob_ps, 1)
            keys1(0)
            slots_to_tokens(1)
            keys1(1)
            pe.wait_ge(wvo_ready, 1)
            query_keys1(0)
            values1(0)
            query_keys1(1)
            tokens_to_columns(1, 0)
            tokens_to_columns(1, 1)
            pe.wait_ge(ob_ready, 1)
            values1(1)

            pe.wait_ge(gw_split, 1)
            for h in range(2):
                pe.wait_ge(xl_ready, h + 1)
                for j in range(HT):
                    t = h * HT + j
                    c = slice(t * P, (t + 1) * P)
                    last = exact_product(PS[:, 0, t * NE:(t + 1) * NE], (xh[:, c], xl[:, c]), (gwh[:, :], gwl[:, :]))
            last.then_inc(lg0_ps, 1)

            def experts0(t):
                c = slice(t * P, (t + 1) * P)
                for g in range(2):
                    if t >= RING:
                        pe.wait_ge(ys_ready if g else y0_odd, t - RING + 1)
                    for x, w, start, stop in ((xh, we0h, True, False), (xh, we0l, False, False), (xl, we0h, False, True)):
                        last = pe.matmul(PS[:, y0_bank(t) + g, :], x[:, c],
                                         w[:, g * HT:(g + 1) * HT, :].rearrange("p e m -> p (e m)"), start=start, stop=stop)
                    last.then_inc(y0_ps, 1)

            pe.wait_ge(we0_ready, 2)
            pe.wait_ge(kq1_ready, 2)
            experts0(0)
            pe.wait_ge(vo1_ready, 2)
            for t in range(1, NT):
                experts0(t)

            def query_bias1(h, b):
                keys = kT1[:, h * HW + b * S:h * HW + (b + 1) * S].rearrange("p (a k) -> p a k", a=1)
                pe.matmul(SC[:, h, b, :].rearrange("p (m k) -> p m k", m=MT), bq_s[:, :].to_broadcast([DH, P]),
                          keys.to_broadcast([DH, MT, S]), start=True, stop=False)

            def scores1(h, b):
                pe.wait_ge(columns_ready, h + 1)
                for m in range(MT):
                    t = h * HT + b * MT + m
                    last = pe.matmul(SC[:, h, b, m * S:(m + 1) * S], xnT[:, t * P:(t + 1) * P],
                                     kq1[:, h * HW + b * S:h * HW + (b + 1) * S], start=False, stop=(m == MT - 1))
                last.then_inc(s1_ps, 1)

            def weights_to_keys(h, b):
                pe.wait_ge(exp1_ready, BH * h + b + 1)
                for m in range(MT):
                    for j in range(MT):
                        last = pe.transpose(SC[:, h, b, (m * MT + j) * P:(m * MT + j + 1) * P],
                                            E[:, h * HT + b * MT + j, m * P:(m + 1) * P], ident[:, :])
                last.then_inc(pT1_ps, 1)

            def attend(h, b):
                pe.wait_ge(pT1_ready, BH * h + b + 1)
                for j in range(MT):
                    t = h * HT + b * MT + j
                    for m in range(MT):
                        last = pe.matmul(PS[:, 4 + 2 * h + b, j * P:(j + 1) * P],
                                         pT1[:, m, t * P:(t + 1) * P], vo1[:, h * HT + b * MT + m, :],
                                         start=(m == 0), stop=(m == MT - 1))
                last.then_inc(o1_ps, 1)

            query_bias1(0, 0)
            query_bias1(0, 1)
            pe.wait_ge(y0_odd, NT - 2)
            pe.wait_ge(ys_ready, NT - 2)
            query_bias1(1, 0)
            query_bias1(1, 1)
            pe.wait_ge(y0_odd, NT - 1)
            pe.wait_ge(ys_ready, NT - 1)
            tokens_to_columns(2, 0)
            scores1(0, 0)
            scores1(0, 1)
            tokens_to_columns(2, 1)
            weights_to_keys(0, 0)
            scores1(1, 0)
            scores1(1, 1)
            weights_to_keys(0, 1)
            attend(0, 0)
            weights_to_keys(1, 0)
            attend(0, 1)
            weights_to_keys(1, 1)
            attend(1, 0)
            attend(1, 1)
            tokens_to_columns(3, 0)

            def first_unit(u, h):
                pe.wait_ge(xl_ready, 3 + h)
                k = slice(u * P, (u + 1) * P)
                last = exact_product(PS[:, 2 * u + h, :], (w1h[0][:, k], w1l[0][:, k]), (xh[:, cols(h)], xl[:, cols(h)]))
                if h == 1:
                    last.then_inc(w1_ps, 1)

            def router_logits():
                for h in range(2):
                    last = exact_product(PS[0:NE, 4 + h, :], (wrh[:, :], wrl[:, :]), (xh[:, cols(h)], xl[:, cols(h)]))
                last.then_inc(lgT_ps, 1)

            def logits_to_tokens():
                pe.wait_ge(lgT_ready, 1)
                for t in range(NT):
                    last = pe.transpose(PS[:, 6, t * NE:(t + 1) * NE], gT1[:, t * P:(t + 1) * P], ident[0:NE, 0:NE])
                last.then_inc(lg1_ps, 1)

            def gate_columns():
                pe.wait_ge(gw1_ready, 1)
                for t in range(NT):
                    last = pe.transpose(PS[0:NE, 6 + t // HT, (t % HT) * P:(t % HT + 1) * P], gw1[:, t, :], ident[:, :])
                last.then_inc(gT1_ps, 1)

            def up(i, u):
                s, c = (u // NC) % 2, u % NC
                k = slice(c * P, (c + 1) * P)
                if c == 0:
                    pe.wait_ge(w1_ready, 2 * i + u // NC + 1)
                pe.wait_ge(hl_ready, 2 * NC * i + u - 1)
                for w, x, start, stop in ((w1h, xh, True, False), (w1h, xl, False, False), (w1l, xh, False, True)):
                    for h in range(2):
                        last = pe.matmul(PS[:, 2 * (u % 2) + h, :], w[s][:, k], x[:, cols(h)], start=start, stop=stop)
                last.then_inc(w1_ps, 1)

            def down(i, u):
                s, c = u // NC, u % NC
                pe.wait_ge(hl_ready, 2 * NC * i + u + 1)
                if c == 0:
                    pe.wait_ge(w_ready, 4 * i + 2 * s + 2)
                    if isinstance(i, int) and i == 0:
                        if s == 1:
                            pe.wait_ge(gT1_ready, 1)
                    else:
                        pe.wait_ge(y1_gated, 4 * i + 2 * s - 2)
                for w, x, start, stop in ((w2h, hh, c == 0, False), (w2h, hl, False, False), (w2l, hh, False, c == NC - 1)):
                    for h in range(2):
                        last = pe.matmul(PS[:, 4 + 2 * s + h, :], w[s][:, c, :], x[u % NH][:, cols(h)],
                                         start=start, stop=stop)
                last.then_inc(h_used, 1)

            def expert_pair(i, last_pair):
                for u in range(2 * NC):
                    if u + LAG < 2 * NC or not last_pair:
                        up(i, u + LAG)
                    if last_pair and u == 2 * NC - 1:
                        pe.wait_ge(hl_ready, 2 * NC * i + u)
                        pe.wait_ge(y1_added, 2 * (NE - 2))
                        for h in range(2):
                            transposes(PS[:, h, :], lambda t: acc[:, t * P:(t + 1) * P], h).then_inc(oT_ps, 1)
                    if isinstance(i, int) and i == 0 and u == 0:
                        logits_to_tokens()
                    down(i, u)
                    if isinstance(i, int) and i == 0 and u == 2:
                        gate_columns()

            pe.wait_ge(w1_ready, 1)
            tokens_to_columns(3, 1)
            first_unit(0, 0)
            first_unit(0, 1)
            first_unit(1, 0)
            first_unit(1, 1)
            router_logits()
            expert_pair(0, False)
            with pe.Fori(1, NE // 2 - 1) as i:
                expert_pair(i, False)
            expert_pair(NE // 2 - 1, True)

            for h in range(2):
                pe.wait_ge(y1_gated, 2 * (NE - 1) + h + 1)
                transposes(PS[:, 2 + h, :], lambda t: ygated[:, t * P:(t + 1) * P], h).then_inc(oT_ps, 1)


_INS = ["x", "ctx_1024", "g_xattn", "g_ffn", "L0_xattn_Wq", "L0_xattn_Wk", "L0_xattn_Wv",
        "L0_xattn_gru_wih", "L0_xattn_gru_whh", "L0_xattn_gru_bih", "L0_xattn_gru_bhh",
        "L0_xattn_slot_norm_w", "L0_xattn_input_norm_w", "L0_ffn_gate_w", "L0_ffn_We",
        "L1_xattn_Wq", "L1_xattn_bq", "L1_xattn_Wk", "L1_xattn_bk", "L1_xattn_Wv", "L1_xattn_bv",
        "L1_xattn_Wo", "L1_xattn_bo", "L1_ffn_W1", "L1_ffn_b1", "L1_ffn_W2", "L1_ffn_b2",
        "L1_ffn_Wr", "L1_ffn_br"]


def kernel(**inputs):
    import numpy as _np
    import concourse.bacc as _bacc
    from concourse import mybir as _mybir
    from concourse.bass_utils import run_bass_kernel_spmd as _run

    nc = _bacc.Bacc("TRN2", target_bir_lowering=False, num_devices=1)
    arrays, args = {}, []
    for name in _INS:
        a = _np.ascontiguousarray(inputs[name])
        arrays[f"in_{name}"] = a
        args.append(nc.dram_tensor(f"in_{name}", a.shape, _mybir.dt.from_np(a.dtype), kind="ExternalInput").ap())
    shape = arrays["in_x"].shape
    args.append(nc.dram_tensor("out_x", shape, _mybir.dt.float32, kind="ExternalOutput").ap())
    flamingo_gated_two_layer_kernel(nc, *args)
    r = _run(nc, [arrays], core_ids=[0])
    return r.results[0]["out_x"]
```
